# Optimizing a Trainium2 kernel written in Bass

```python
import numpy as np
import jax
import jax.numpy as jnp

def _softmax(x, axis=-1):
    return jax.nn.softmax(x, axis=axis)

def _gelu(x):
    return jax.nn.gelu(x, approximate=True)

def _silu(x):
    return jax.nn.silu(x)

def _sigmoid(x):
    return jax.nn.sigmoid(x)

def _layernorm(x, axis=-1, eps=1e-05):
    m = jnp.mean(x, axis=axis, keepdims=True)
    v = jnp.var(x, axis=axis, keepdims=True)
    return (x - m) / jnp.sqrt(v + eps)

def _scatter_add(tgt, idx, src, axis=0):
    return tgt.at[idx].add(src)

def _segment_sum(src, seg, n):
    return jax.ops.segment_sum(src, seg, n)
kernel_name = 'mk_adj_ffn_d4_adj_r2_48a1cf'

def setup_inputs(seed: int=0):
    np.random.seed(seed)
    _w = jnp.asarray

    def _rec_inputs():
        import jax
        import jax.numpy as jnp
        _gk = jax.random.key(seed)
        x = -0.0002928 + 1 * jax.random.normal(jax.random.fold_in(_gk, 1), (64, 128, 128), jnp.float32)
        _a = jax.random.bernoulli(jax.random.fold_in(_gk, 2), 0.125, (64, 128, 128))
        _a = jnp.logical_or(_a, jnp.swapaxes(_a, -1, -2))
        _a = jnp.logical_or(_a, jnp.eye(128, dtype=bool))
        adj = _a.astype(jnp.int32)
        return (x, adj)
    x, adj = _rec_inputs()

    def _L0_gnn_setup():
        import jax, jax.numpy as jnp
        import numpy as np
        B, N, F_IN, F_OUT = (8, 1024, 128, 128)
        key = jax.random.key(seed)
        k1, k2, k3, k4 = jax.random.split(key, 4)
        inp = jax.random.normal(k1, (B, N, F_IN), dtype=jnp.float32)
        adj = jax.random.randint(k2, (B, N, N), 0, 2, dtype=jnp.int32)
        W = jax.random.normal(k3, (F_IN, F_OUT), dtype=jnp.float32) * (1.414 * (6.0 / (F_IN + F_OUT)) ** 0.5)
        a = jax.random.normal(k4, (2 * F_OUT, 1), dtype=jnp.float32) * (1.414 * (6.0 / (2 * F_OUT + 1)) ** 0.5)
        return {'inp': inp, 'adj': adj, 'W': W, 'a': a}
    _L0_gnn_all = _L0_gnn_setup()
    _L0_gnn_in = {k: v for k, v in _L0_gnn_all.items() if k in ('W', 'a')}
    del _L0_gnn_all

    def _L0_ffn_setup():
        import jax, jax.numpy as jnp
        import numpy as np
        E = 8
        K = 2
        D = 128
        H = 256
        DOUT = 128
        EPS = 1e-05
        key = jax.random.key(seed)
        ks = jax.random.split(key, 9)
        s = 0.02
        return {'x': jax.random.normal(ks[0], (4, 4096, D), jnp.float32), 'gamma': 1.0 + 0.05 * jax.random.normal(ks[1], (D,), jnp.float32), 'beta': 0.05 * jax.random.normal(ks[2], (D,), jnp.float32), 'Wr': 0.01 * jax.random.normal(ks[3], (D, E), jnp.float32), 'br': jnp.zeros((E,), jnp.float32), 'W1': s * jax.random.normal(ks[4], (E, D, H), jnp.float32), 'b1': s * jax.random.normal(ks[5], (E, H), jnp.float32), 'W2': s * jax.random.normal(ks[6], (E, H, DOUT), jnp.float32), 'b2': s * jax.random.normal(ks[7], (E, DOUT), jnp.float32)}
    _L0_ffn_all = _L0_ffn_setup()
    _L0_ffn_in = {k: v for k, v in _L0_ffn_all.items() if k in ('gamma', 'beta', 'Wr', 'br', 'W1', 'b1', 'W2', 'b2')}
    del _L0_ffn_all

    def _L1_gnn_setup():
        import jax, jax.numpy as jnp
        import numpy as np
        import math
        B, N, IN_DIM, OUT_DIM, H = (8, 512, 128, 128, 8)
        D_K = OUT_DIM // H
        key = jax.random.key(seed)
        ks = jax.random.split(key, 12)
        s_in = 1.0 / math.sqrt(IN_DIM)
        s_out = 1.0 / math.sqrt(OUT_DIM)
        return {'X': jax.random.normal(ks[0], (B, N, IN_DIM), jnp.float32), 'A': jax.random.randint(ks[1], (B, N, N), 0, 2, jnp.int32), 'D': jax.random.uniform(ks[2], (B, N, N), jnp.float32), 'W_q': jax.random.uniform(ks[3], (IN_DIM, OUT_DIM), jnp.float32, -s_in, s_in), 'b_q': jax.random.uniform(ks[4], (OUT_DIM,), jnp.float32, -s_in, s_in), 'W_k': jax.random.uniform(ks[5], (IN_DIM, OUT_DIM), jnp.float32, -s_in, s_in), 'b_k': jax.random.uniform(ks[6], (OUT_DIM,), jnp.float32, -s_in, s_in), 'W_v': jax.random.uniform(ks[7], (IN_DIM, OUT_DIM), jnp.float32, -s_in, s_in), 'b_v': jax.random.uniform(ks[8], (OUT_DIM,), jnp.float32, -s_in, s_in), 'W_o': jax.random.uniform(ks[9], (OUT_DIM, OUT_DIM), jnp.float32, -s_out, s_out), 'b_o': jax.random.uniform(ks[10], (OUT_DIM,), jnp.float32, -s_out, s_out), 'dist_scale': jnp.array(1.0, jnp.float32)}
    _L1_gnn_all = _L1_gnn_setup()
    _L1_gnn_in = {k: v for k, v in _L1_gnn_all.items() if k in ('W_q', 'b_q', 'W_k', 'b_k', 'W_v', 'b_v', 'W_o', 'b_o', 'dist_scale')}
    del _L1_gnn_all

    def _L1_ffn_setup():
        import jax, jax.numpy as jnp
        import numpy as np
        TOP_K = 2
        LN_EPS = 1e-05
        key = jax.random.key(seed)
        ks = jax.random.split(key, 8)
        B, S, D, E, H = (16, 512, 128, 8, 512)
        x = jax.random.normal(ks[0], (B, S, D), dtype=jnp.float32)
        Wr = jax.random.normal(ks[1], (D, E), dtype=jnp.float32) * 0.1
        br = jnp.zeros((E,), dtype=jnp.float32)
        ln_g = jnp.ones((E, D), dtype=jnp.float32)
        ln_b = jnp.zeros((E, D), dtype=jnp.float32)
        W1 = jax.random.normal(ks[2], (E, D, H), dtype=jnp.float32) * (1.0 / np.sqrt(D))
        b1 = jnp.zeros((E, H), dtype=jnp.float32)
        W2 = jax.random.normal(ks[3], (E, H, D), dtype=jnp.float32) * (1.0 / np.sqrt(H))
        b2 = jnp.zeros((E, D), dtype=jnp.float32)
        return {'x': x, 'Wr': Wr, 'br': br, 'ln_g': ln_g, 'ln_b': ln_b, 'W1': W1, 'b1': b1, 'W2': W2, 'b2': b2}
    _L1_ffn_all = _L1_ffn_setup()
    _L1_ffn_in = {k: v for k, v in _L1_ffn_all.items() if k in ('Wr', 'br', 'ln_g', 'ln_b', 'W1', 'b1', 'W2', 'b2')}
    del _L1_ffn_all

    def _L2_gnn_setup():
        import jax, jax.numpy as jnp
        import numpy as np
        key = jax.random.key(seed)
        k1, k2, k3, k4 = jax.random.split(key, 4)
        B, N, F, U = (8, 1024, 128, 128)
        x = jax.random.normal(k1, (B, N, F), dtype=jnp.float32)
        adj = jax.random.randint(k2, (B, N, N), 0, 2, dtype=jnp.int32)
        W_msg = jax.random.normal(k3, (F, U), dtype=jnp.float32) / np.sqrt(F)
        W_upd = jax.random.normal(k4, (F, U), dtype=jnp.float32) / np.sqrt(F)
        bias = jnp.zeros((U,), dtype=jnp.float32)
        return {'x': x, 'adj': adj, 'W_msg': W_msg, 'W_upd': W_upd, 'bias': bias}
    _L2_gnn_all = _L2_gnn_setup()
    _L2_gnn_in = {k: v for k, v in _L2_gnn_all.items() if k in ('W_msg', 'W_upd', 'bias')}
    del _L2_gnn_all

    def _L2_ffn_setup():
        import jax, jax.numpy as jnp
        import numpy as np
        H, P, G, NS, K = (8, 64, 64, 64, 3)
        D_INNER = H * P
        CONV_DIM = D_INNER + 2 * NS
        D_IN_PROJ = 2 * D_INNER + 2 * NS + 2 * H

        def _hydra(u, in_w, conv_w, conv_b, dt_bias, A_log, Dp, fcD_w, norm_w, out_w):
            Bt, L, _ = u.shape
            zxbcdt = u @ in_w.T
            z = zxbcdt[..., :D_INNER]
            xBC = zxbcdt[..., D_INNER:D_INNER + CONV_DIM]
            dt = zxbcdt[..., -2 * H:]
            dt = jnp.concatenate([dt[..., :H], jnp.flip(dt[..., H:], axis=1)], axis=0)
            dt = jax.nn.softplus(dt + dt_bias)
            xp = jnp.pad(xBC, ((0, 0), (K - 1, 0), (0, 0)))
            xBC = sum((xp[:, k:k + L, :] * conv_w[:, k] for k in range(K))) + conv_b
            xBC = jax.nn.silu(xBC)
            x = xBC[..., :D_INNER]
            Bm = xBC[..., D_INNER:D_INNER + NS]
            Cm = xBC[..., D_INNER + NS:]
            x_og = x
            x2 = jnp.concatenate([x, jnp.flip(x, 1)], 0).reshape(2 * Bt, L, H, P)
            B2 = jnp.concatenate([Bm, jnp.flip(Bm, 1)], 0)
            C2 = jnp.concatenate([Cm, jnp.flip(Cm, 1)], 0)
            dA = jnp.exp(dt * -jnp.exp(A_log))
            dBx = jnp.einsum('blh,bln,blhp->blhpn', dt, B2, x2)

            def step(h, inp):
                dA_t, dBx_t, C_t = inp
                h = h * dA_t[:, :, None, None] + dBx_t
                return (h, jnp.einsum('bhpn,bn->bhp', h, C_t))
            h0 = jnp.zeros((2 * Bt, H, P, NS), u.dtype)
            _, ys = jax.lax.scan(step, h0, (dA.transpose(1, 0, 2), dBx.transpose(1, 0, 2, 3, 4), C2.transpose(1, 0, 2)))
            y = ys.transpose(1, 0, 2, 3).reshape(2 * Bt, L, D_INNER)
            y_fw, y_bw = (y[:Bt], jnp.flip(y[Bt:], 1))
            y = jnp.pad(y_fw[:, :-1], ((0, 0), (1, 0), (0, 0))) + jnp.pad(y_bw[:, 1:], ((0, 0), (0, 1), (0, 0)))
            y = y + x_og * jnp.repeat(x_og @ fcD_w.T + Dp, P, axis=-1)
            yg = y * jax.nn.silu(z)
            yg = yg * jax.lax.rsqrt(jnp.mean(jnp.square(yg), -1, keepdims=True) + 1e-05) * norm_w
            return yg @ out_w.T
        key = jax.random.key(seed)
        ks = jax.random.split(key, 10)
        dim, Bsz, N = (128, 4, 4096)
        s = 0.02
        return {'x': jax.random.normal(ks[0], (Bsz, N, dim), jnp.float32), 'W_fx': jax.random.normal(ks[1], (D_INNER, dim), jnp.float32) * s, 'b_fx': jnp.zeros((D_INNER,), jnp.float32), 'W_x': jax.random.normal(ks[2], (D_INNER, dim), jnp.float32) * s, 'b_x': jnp.zeros((D_INNER,), jnp.float32), 'W_slice': jax.random.normal(ks[3], (G, P), jnp.float32) * s, 'b_slice': jnp.zeros((G,), jnp.float32), 'temperature': jnp.full((1, H, 1, 1), 0.5, jnp.float32), 'hy_in_w': jax.random.normal(ks[4], (D_IN_PROJ, D_INNER), jnp.float32) * s, 'hy_conv_w': jax.random.normal(ks[5], (CONV_DIM, K), jnp.float32) * s, 'hy_conv_b': jnp.zeros((CONV_DIM,), jnp.float32), 'hy_dt_bias': jnp.log(jnp.expm1(jnp.full((H,), 0.01, jnp.float32))), 'hy_A_log': jnp.log(jnp.linspace(1.0, 16.0, H)).astype(jnp.float32), 'hy_D': jnp.ones((H,), jnp.float32), 'hy_fcD_w': jax.random.normal(ks[6], (H, D_INNER), jnp.float32) * s, 'hy_norm_w': jnp.ones((D_INNER,), jnp.float32), 'hy_out_w': jax.random.normal(ks[7], (D_INNER, D_INNER), jnp.float32) * s, 'out_w': jax.random.normal(ks[8], (dim, D_INNER), jnp.float32) * s, 'out_b': jnp.zeros((dim,), jnp.float32)}
    _L2_ffn_all = _L2_ffn_setup()
    _L2_ffn_in = {k: v for k, v in _L2_ffn_all.items() if k in ('W_fx', 'b_fx', 'W_x', 'b_x', 'W_slice', 'b_slice', 'temperature', 'hy_in_w', 'hy_conv_w', 'hy_conv_b', 'hy_dt_bias', 'hy_A_log', 'hy_D', 'hy_fcD_w', 'hy_norm_w', 'hy_out_w', 'out_w', 'out_b')}
    del _L2_ffn_all

    def _L3_gnn_setup():
        import jax, jax.numpy as jnp
        import numpy as np
        B, S, D = (64, 256, 128)

        def _leaky(x):
            return jnp.where(x >= 0, x, 0.2 * x)
        key = jax.random.key(seed)
        k = jax.random.split(key, 6)
        stdv = 1.0 / np.sqrt(D)
        return {'hidden': jax.random.normal(k[0], (B, S, D), dtype=jnp.float32), 'adj': jax.random.randint(k[1], (B, S, S), 0, 5, dtype=jnp.int32), 'a0': jax.random.uniform(k[2], (D, 1), jnp.float32, -stdv, stdv), 'a1': jax.random.uniform(k[3], (D, 1), jnp.float32, -stdv, stdv), 'a2': jax.random.uniform(k[4], (D, 1), jnp.float32, -stdv, stdv), 'a3': jax.random.uniform(k[5], (D, 1), jnp.float32, -stdv, stdv), 'bias': jnp.zeros((D,), dtype=jnp.float32)}
    _L3_gnn_all = _L3_gnn_setup()
    _L3_gnn_in = {k: v for k, v in _L3_gnn_all.items() if k in ('a0', 'a1', 'a2', 'a3', 'bias')}
    del _L3_gnn_all

    def _L3_ffn_setup():
        import jax, jax.numpy as jnp
        import numpy as np
        B, S, D, F, E, K = (8, 1024, 128, 512, 8, 2)
        key = jax.random.key(seed)
        ks = jax.random.split(key, 10)
        s = 0.02
        return {'x': jax.random.normal(ks[0], (B, S, D), dtype=jnp.float32), 'Wr': jax.random.normal(ks[1], (D, E), dtype=jnp.float32) * s, 'W1s': jax.random.normal(ks[2], (D, F), dtype=jnp.float32) * s, 'b1s': jnp.zeros((F,), dtype=jnp.float32), 'W2s': jax.random.normal(ks[3], (F, D), dtype=jnp.float32) * s, 'b2s': jnp.zeros((D,), dtype=jnp.float32), 'W1p': jax.random.normal(ks[4], (E, D, F), dtype=jnp.float32) * s, 'b1p': jnp.zeros((E, F), dtype=jnp.float32), 'W2p': jax.random.normal(ks[5], (E, F, D), dtype=jnp.float32) * s, 'b2p': jnp.zeros((E, D), dtype=jnp.float32)}
    _L3_ffn_all = _L3_ffn_setup()
    _L3_ffn_in = {k: v for k, v in _L3_ffn_all.items() if k in ('Wr', 'W1s', 'b1s', 'W2s', 'b2s', 'W1p', 'b1p', 'W2p', 'b2p')}
    del _L3_ffn_all
    return {'x': x, 'adj': adj, 'L0_gnn_W': _L0_gnn_in['W'], 'L0_gnn_a': _L0_gnn_in['a'], 'L0_ffn_gamma': _L0_ffn_in['gamma'], 'L0_ffn_beta': _L0_ffn_in['beta'], 'L0_ffn_Wr': _L0_ffn_in['Wr'], 'L0_ffn_br': _L0_ffn_in['br'], 'L0_ffn_W1': _L0_ffn_in['W1'], 'L0_ffn_b1': _L0_ffn_in['b1'], 'L0_ffn_W2': _L0_ffn_in['W2'], 'L0_ffn_b2': _L0_ffn_in['b2'], 'L1_gnn_W_q': _L1_gnn_in['W_q'], 'L1_gnn_b_q': _L1_gnn_in['b_q'], 'L1_gnn_W_k': _L1_gnn_in['W_k'], 'L1_gnn_b_k': _L1_gnn_in['b_k'], 'L1_gnn_W_v': _L1_gnn_in['W_v'], 'L1_gnn_b_v': _L1_gnn_in['b_v'], 'L1_gnn_W_o': _L1_gnn_in['W_o'], 'L1_gnn_b_o': _L1_gnn_in['b_o'], 'L1_gnn_dist_scale': _L1_gnn_in['dist_scale'], 'L1_ffn_Wr': _L1_ffn_in['Wr'], 'L1_ffn_br': _L1_ffn_in['br'], 'L1_ffn_ln_g': _L1_ffn_in['ln_g'], 'L1_ffn_ln_b': _L1_ffn_in['ln_b'], 'L1_ffn_W1': _L1_ffn_in['W1'], 'L1_ffn_b1': _L1_ffn_in['b1'], 'L1_ffn_W2': _L1_ffn_in['W2'], 'L1_ffn_b2': _L1_ffn_in['b2'], 'L2_gnn_W_msg': _L2_gnn_in['W_msg'], 'L2_gnn_W_upd': _L2_gnn_in['W_upd'], 'L2_gnn_bias': _L2_gnn_in['bias'], 'L2_ffn_W_fx': _L2_ffn_in['W_fx'], 'L2_ffn_b_fx': _L2_ffn_in['b_fx'], 'L2_ffn_W_x': _L2_ffn_in['W_x'], 'L2_ffn_b_x': _L2_ffn_in['b_x'], 'L2_ffn_W_slice': _L2_ffn_in['W_slice'], 'L2_ffn_b_slice': _L2_ffn_in['b_slice'], 'L2_ffn_temperature': _L2_ffn_in['temperature'], 'L2_ffn_hy_in_w': _L2_ffn_in['hy_in_w'], 'L2_ffn_hy_conv_w': _L2_ffn_in['hy_conv_w'], 'L2_ffn_hy_conv_b': _L2_ffn_in['hy_conv_b'], 'L2_ffn_hy_dt_bias': _L2_ffn_in['hy_dt_bias'], 'L2_ffn_hy_A_log': _L2_ffn_in['hy_A_log'], 'L2_ffn_hy_D': _L2_ffn_in['hy_D'], 'L2_ffn_hy_fcD_w': _L2_ffn_in['hy_fcD_w'], 'L2_ffn_hy_norm_w': _L2_ffn_in['hy_norm_w'], 'L2_ffn_hy_out_w': _L2_ffn_in['hy_out_w'], 'L2_ffn_out_w': _L2_ffn_in['out_w'], 'L2_ffn_out_b': _L2_ffn_in['out_b'], 'L3_gnn_a0': _L3_gnn_in['a0'], 'L3_gnn_a1': _L3_gnn_in['a1'], 'L3_gnn_a2': _L3_gnn_in['a2'], 'L3_gnn_a3': _L3_gnn_in['a3'], 'L3_gnn_bias': _L3_gnn_in['bias'], 'L3_ffn_Wr': _L3_ffn_in['Wr'], 'L3_ffn_W1s': _L3_ffn_in['W1s'], 'L3_ffn_b1s': _L3_ffn_in['b1s'], 'L3_ffn_W2s': _L3_ffn_in['W2s'], 'L3_ffn_b2s': _L3_ffn_in['b2s'], 'L3_ffn_W1p': _L3_ffn_in['W1p'], 'L3_ffn_b1p': _L3_ffn_in['b1p'], 'L3_ffn_W2p': _L3_ffn_in['W2p'], 'L3_ffn_b2p': _L3_ffn_in['b2p']}

def reference(x, adj, L0_gnn_W, L0_gnn_a, L0_ffn_gamma, L0_ffn_beta, L0_ffn_Wr, L0_ffn_br, L0_ffn_W1, L0_ffn_b1, L0_ffn_W2, L0_ffn_b2, L1_gnn_W_q, L1_gnn_b_q, L1_gnn_W_k, L1_gnn_b_k, L1_gnn_W_v, L1_gnn_b_v, L1_gnn_W_o, L1_gnn_b_o, L1_gnn_dist_scale, L1_ffn_Wr, L1_ffn_br, L1_ffn_ln_g, L1_ffn_ln_b, L1_ffn_W1, L1_ffn_b1, L1_ffn_W2, L1_ffn_b2, L2_gnn_W_msg, L2_gnn_W_upd, L2_gnn_bias, L2_ffn_W_fx, L2_ffn_b_fx, L2_ffn_W_x, L2_ffn_b_x, L2_ffn_W_slice, L2_ffn_b_slice, L2_ffn_temperature, L2_ffn_hy_in_w, L2_ffn_hy_conv_w, L2_ffn_hy_conv_b, L2_ffn_hy_dt_bias, L2_ffn_hy_A_log, L2_ffn_hy_D, L2_ffn_hy_fcD_w, L2_ffn_hy_norm_w, L2_ffn_hy_out_w, L2_ffn_out_w, L2_ffn_out_b, L3_gnn_a0, L3_gnn_a1, L3_gnn_a2, L3_gnn_a3, L3_gnn_bias, L3_ffn_Wr, L3_ffn_W1s, L3_ffn_b1s, L3_ffn_W2s, L3_ffn_b2s, L3_ffn_W1p, L3_ffn_b1p, L3_ffn_W2p, L3_ffn_b2p):
    import jax
    import jax.numpy as jnp

    def _L0_gnn_ref(inp, adj, W, a):
        import jax, jax.numpy as jnp
        import numpy as np
        B, N, F_IN, F_OUT = (8, 1024, 128, 128)
        h = jnp.einsum('bnf,fo->bno', inp, W)
        a1 = a[:F_OUT, 0]
        a2 = a[F_OUT:, 0]
        s1 = h @ a1
        s2 = h @ a2
        e = jax.nn.leaky_relu(s1[:, :, None] + s2[:, None, :], negative_slope=0.4)
        att = jnp.where(adj > 0, e, jnp.float32(-1e+20))
        att = jax.nn.softmax(att, axis=1)
        h_prime = jnp.einsum('bij,bjo->bio', att, h)
        return jax.nn.gelu(h_prime, approximate=False)

    def _L0_ffn_ref(x, gamma, beta, Wr, br, W1, b1, W2, b2):
        import jax, jax.numpy as jnp
        import numpy as np
        E = 8
        K = 2
        D = 128
        H = 256
        DOUT = 128
        EPS = 1e-05
        mu = jnp.mean(x, axis=-1, keepdims=True)
        var = jnp.mean(jnp.square(x - mu), axis=-1, keepdims=True)
        xn = (x - mu) * jax.lax.rsqrt(var + EPS) * gamma + beta
        logits = jnp.einsum('bsd,de->bse', xn, Wr) + br
        top_vals, top_idx = jax.lax.top_k(logits, K)
        w = jax.nn.softmax(top_vals, axis=-1)
        w_full = jnp.einsum('bsk,bske->bse', w, jax.nn.one_hot(top_idx, E, dtype=w.dtype))
        y = jnp.zeros(x.shape[:-1] + (DOUT,), x.dtype)
        for e in range(E):
            h = jax.nn.gelu(jnp.einsum('bsd,dh->bsh', xn, W1[e]) + b1[e], approximate=False)
            y_e = jnp.einsum('bsh,hd->bsd', h, W2[e]) + b2[e]
            y = y + y_e * w_full[..., e, None]
        return y

    def _L1_gnn_ref(X, A, D, W_q, b_q, W_k, b_k, W_v, b_v, W_o, b_o, dist_scale):
        import jax, jax.numpy as jnp
        import numpy as np
        import math
        B, N, IN_DIM, OUT_DIM, H = (8, 512, 128, 128, 8)
        D_K = OUT_DIM // H
        b, n, _ = X.shape
        Q = (X @ W_q + b_q).reshape(b, n, H, D_K).transpose(0, 2, 1, 3)
        K = (X @ W_k + b_k).reshape(b, n, H, D_K).transpose(0, 2, 1, 3)
        V = (X @ W_v + b_v).reshape(b, n, H, D_K).transpose(0, 2, 1, 3)
        scores = jnp.einsum('bhqd,bhkd->bhqk', Q, K) / jnp.sqrt(jnp.float32(D_K))
        scores = scores - dist_scale * D[:, None, :, :]
        scores = jnp.where(A[:, None, :, :] <= 0, jnp.float32(-1000000000.0), scores)
        attn = jax.nn.softmax(scores, axis=-1)
        out = jnp.einsum('bhqk,bhkd->bhqd', attn, V)
        out = out.transpose(0, 2, 1, 3).reshape(b, n, H * D_K)
        return out @ W_o + b_o

    def _L1_ffn_ref(x, Wr, br, ln_g, ln_b, W1, b1, W2, b2):
        import jax, jax.numpy as jnp
        import numpy as np
        TOP_K = 2
        LN_EPS = 1e-05
        B, S, D = x.shape
        N = B * S
        xt = x.reshape(N, D)
        logits = xt @ Wr + br
        probs = jax.nn.softmax(logits, axis=-1)
        top_p, top_idx = jax.lax.top_k(probs, TOP_K)
        weights = top_p / top_p.sum(axis=-1, keepdims=True)
        mu = xt.mean(axis=-1, keepdims=True)
        var = ((xt - mu) ** 2).mean(axis=-1, keepdims=True)
        xn = (xt - mu) * jax.lax.rsqrt(var + LN_EPS)
        xe = xn[None, :, :] * ln_g[:, None, :] + ln_b[:, None, :]
        h = jax.nn.gelu(jnp.einsum('end,edh->enh', xe, W1) + b1[:, None, :], approximate=False)
        y = jnp.einsum('enh,ehd->end', h, W2) + b2[:, None, :]
        y_tok = jnp.transpose(y, (1, 0, 2))
        sel = jnp.take_along_axis(y_tok, top_idx[:, :, None], axis=1)
        out = (weights[:, :, None] * sel).sum(axis=1)
        return out.reshape(B, S, D)

    def _L2_gnn_ref(x, adj, W_msg, W_upd, bias):
        import jax, jax.numpy as jnp
        import numpy as np
        a = adj.astype(x.dtype)
        h = jnp.einsum('bnf,fu->bnu', x, W_msg)
        msg_sum = jnp.einsum('bij,biu->bju', a, h)
        deg = jnp.sum(a, axis=1)
        messages = jnp.where(deg[..., None] > 0, msg_sum / jnp.maximum(deg, 1.0)[..., None], 0.0)
        out = jnp.einsum('bnf,fu->bnu', x, W_upd) + messages + bias
        return jax.nn.relu(out)

    def _L2_ffn_ref(x, W_fx, b_fx, W_x, b_x, W_slice, b_slice, temperature, hy_in_w, hy_conv_w, hy_conv_b, hy_dt_bias, hy_A_log, hy_D, hy_fcD_w, hy_norm_w, hy_out_w, out_w, out_b):
        import jax, jax.numpy as jnp
        import numpy as np
        H, P, G, NS, K = (8, 64, 64, 64, 3)
        D_INNER = H * P
        CONV_DIM = D_INNER + 2 * NS
        D_IN_PROJ = 2 * D_INNER + 2 * NS + 2 * H

        def _hydra(u, in_w, conv_w, conv_b, dt_bias, A_log, Dp, fcD_w, norm_w, out_w):
            Bt, L, _ = u.shape
            zxbcdt = u @ in_w.T
            z = zxbcdt[..., :D_INNER]
            xBC = zxbcdt[..., D_INNER:D_INNER + CONV_DIM]
            dt = zxbcdt[..., -2 * H:]
            dt = jnp.concatenate([dt[..., :H], jnp.flip(dt[..., H:], axis=1)], axis=0)
            dt = jax.nn.softplus(dt + dt_bias)
            xp = jnp.pad(xBC, ((0, 0), (K - 1, 0), (0, 0)))
            xBC = sum((xp[:, k:k + L, :] * conv_w[:, k] for k in range(K))) + conv_b
            xBC = jax.nn.silu(xBC)
            x = xBC[..., :D_INNER]
            Bm = xBC[..., D_INNER:D_INNER + NS]
            Cm = xBC[..., D_INNER + NS:]
            x_og = x
            x2 = jnp.concatenate([x, jnp.flip(x, 1)], 0).reshape(2 * Bt, L, H, P)
            B2 = jnp.concatenate([Bm, jnp.flip(Bm, 1)], 0)
            C2 = jnp.concatenate([Cm, jnp.flip(Cm, 1)], 0)
            dA = jnp.exp(dt * -jnp.exp(A_log))
            dBx = jnp.einsum('blh,bln,blhp->blhpn', dt, B2, x2)

            def step(h, inp):
                dA_t, dBx_t, C_t = inp
                h = h * dA_t[:, :, None, None] + dBx_t
                return (h, jnp.einsum('bhpn,bn->bhp', h, C_t))
            h0 = jnp.zeros((2 * Bt, H, P, NS), u.dtype)
            _, ys = jax.lax.scan(step, h0, (dA.transpose(1, 0, 2), dBx.transpose(1, 0, 2, 3, 4), C2.transpose(1, 0, 2)))
            y = ys.transpose(1, 0, 2, 3).reshape(2 * Bt, L, D_INNER)
            y_fw, y_bw = (y[:Bt], jnp.flip(y[Bt:], 1))
            y = jnp.pad(y_fw[:, :-1], ((0, 0), (1, 0), (0, 0))) + jnp.pad(y_bw[:, 1:], ((0, 0), (0, 1), (0, 0)))
            y = y + x_og * jnp.repeat(x_og @ fcD_w.T + Dp, P, axis=-1)
            yg = y * jax.nn.silu(z)
            yg = yg * jax.lax.rsqrt(jnp.mean(jnp.square(yg), -1, keepdims=True) + 1e-05) * norm_w
            return yg @ out_w.T
        B, N, _ = x.shape
        fx = (x @ W_fx.T + b_fx).reshape(B, N, H, P).transpose(0, 2, 1, 3)
        xm = (x @ W_x.T + b_x).reshape(B, N, H, P).transpose(0, 2, 1, 3)
        temp = jnp.maximum(temperature, 1e-06)
        sw = jax.nn.softmax((xm @ W_slice.T + b_slice) / temp, axis=-1)
        snorm = sw.sum(2)
        st = jnp.einsum('bhnc,bhng->bhgc', fx, sw) / (snorm + 1e-05)[..., None]
        st = st.transpose(0, 2, 1, 3).reshape(B, G, D_INNER)
        ot = _hydra(st, hy_in_w, hy_conv_w, hy_conv_b, hy_dt_bias, hy_A_log, hy_D, hy_fcD_w, hy_norm_w, hy_out_w)
        ot = ot.reshape(B, G, H, P).transpose(0, 2, 1, 3)
        out = jnp.einsum('bhgc,bhng->bhnc', ot, sw).transpose(0, 2, 1, 3).reshape(B, N, D_INNER)
        return out @ out_w.T + out_b

    def _L3_gnn_ref(hidden, adj, a0, a1, a2, a3, bias):
        import jax, jax.numpy as jnp
        import numpy as np
        B, S, D = (64, 256, 128)

        def _leaky(x):
            return jnp.where(x >= 0, x, 0.2 * x)
        h = hidden

        def e_of(a):
            return _leaky(jnp.einsum('bid,bjd->bij', h * a[:, 0], h))
        e0, e1, e2, e3 = (e_of(a0), e_of(a1), e_of(a2), e_of(a3))
        neg_inf = jnp.float32(-jnp.finfo(e0.dtype).max)
        alpha = jnp.where(adj == 1, e0, neg_inf)
        alpha = jnp.where(adj == 2, e1, alpha)
        alpha = jnp.where(adj == 3, e2, alpha)
        alpha = jnp.where(adj == 4, e3, alpha)
        alpha = jax.nn.sigmoid(alpha)
        return jnp.einsum('bij,bjd->bid', alpha, h) + bias

    def _L3_ffn_ref(x, Wr, W1s, b1s, W2s, b2s, W1p, b1p, W2p, b2p):
        import jax, jax.numpy as jnp
        import numpy as np
        B, S, D, F, E, K = (8, 1024, 128, 512, 8, 2)
        gelu = lambda t: jax.nn.gelu(t, approximate=False)
        shared = gelu(x @ W1s + b1s) @ W2s + b2s
        rw = jax.nn.softmax(x @ Wr, axis=-1)
        topw, topi = jax.lax.top_k(rw, K)
        topw = topw / jnp.sum(topw, axis=-1, keepdims=True)
        mask = jnp.sum(jax.nn.one_hot(topi, E, dtype=topw.dtype) * topw[..., None], axis=-2)
        h = gelu(jnp.einsum('bsd,edf->bsef', x, W1p) + b1p)
        priv = jnp.einsum('bsef,efd->bsed', h, W2p) + b2p
        routed = jnp.einsum('bsed,bse->bsd', priv, mask)
        return shared + routed
    x = x + _L0_gnn_ref(_layernorm(x, axis=-1), adj, L0_gnn_W, L0_gnn_a)
    x = x + _L0_ffn_ref(_layernorm(x, axis=-1), L0_ffn_gamma, L0_ffn_beta, L0_ffn_Wr, L0_ffn_br, L0_ffn_W1, L0_ffn_b1, L0_ffn_W2, L0_ffn_b2)
    x = x + _L1_gnn_ref(_layernorm(x, axis=-1), adj, adj, L1_gnn_W_q, L1_gnn_b_q, L1_gnn_W_k, L1_gnn_b_k, L1_gnn_W_v, L1_gnn_b_v, L1_gnn_W_o, L1_gnn_b_o, L1_gnn_dist_scale)
    x = x + _L1_ffn_ref(_layernorm(x, axis=-1), L1_ffn_Wr, L1_ffn_br, L1_ffn_ln_g, L1_ffn_ln_b, L1_ffn_W1, L1_ffn_b1, L1_ffn_W2, L1_ffn_b2)
    x = x + _L2_gnn_ref(_layernorm(x, axis=-1), adj, L2_gnn_W_msg, L2_gnn_W_upd, L2_gnn_bias)
    x = x + _L2_ffn_ref(_layernorm(x, axis=-1), L2_ffn_W_fx, L2_ffn_b_fx, L2_ffn_W_x, L2_ffn_b_x, L2_ffn_W_slice, L2_ffn_b_slice, L2_ffn_temperature, L2_ffn_hy_in_w, L2_ffn_hy_conv_w, L2_ffn_hy_conv_b, L2_ffn_hy_dt_bias, L2_ffn_hy_A_log, L2_ffn_hy_D, L2_ffn_hy_fcD_w, L2_ffn_hy_norm_w, L2_ffn_hy_out_w, L2_ffn_out_w, L2_ffn_out_b)
    x = x + _L3_gnn_ref(_layernorm(x, axis=-1), adj, L3_gnn_a0, L3_gnn_a1, L3_gnn_a2, L3_gnn_a3, L3_gnn_bias)
    x = x + _L3_ffn_ref(_layernorm(x, axis=-1), L3_ffn_Wr, L3_ffn_W1s, L3_ffn_b1s, L3_ffn_W2s, L3_ffn_b2s, L3_ffn_W1p, L3_ffn_b1p, L3_ffn_W2p, L3_ffn_b2p)
    return x

_drawn_inputs = setup_inputs


def setup_inputs(seed=0):
    import zlib

    import numpy as np

    out = dict(_drawn_inputs(seed))
    spreads = {'L0_ffn_br': (0.0, 0.1),
     'L1_ffn_br': (0.0, 0.1),
     'L1_ffn_ln_g': (1.0, 0.2),
     'L1_ffn_ln_b': (0.0, 0.1),
     'L1_ffn_b1': (0.0, 0.1),
     'L1_ffn_b2': (0.0, 0.1),
     'L2_gnn_bias': (0.0, 0.1),
     'L2_ffn_b_fx': (0.0, 0.1),
     'L2_ffn_b_x': (0.0, 0.8),
     'L2_ffn_b_slice': (0.0, 0.8),
     'L2_ffn_temperature': (0.5, 0.6),
     'L2_ffn_hy_conv_b': (0.0, 0.1),
     'L2_ffn_hy_dt_bias': (-4.600166320800781, 0.6),
     'L2_ffn_hy_D': (1.0, 0.6),
     'L2_ffn_hy_norm_w': (1.0, 0.2),
     'L2_ffn_out_b': (0.0, 0.1),
     'L3_gnn_bias': (0.0, 0.417),
     'L3_ffn_b1s': (0.0, 0.8),
     'L3_ffn_b2s': (0.0, 0.39),
     'L3_ffn_b1p': (0.0, 0.8),
     'L3_ffn_b2p': (0.0, 0.542)}
    factors = {'L0_ffn_gamma': 5.684,
     'L0_ffn_beta': 6.182,
     'L0_ffn_b1': 4.147,
     'L1_gnn_b_q': 5.668,
     'L1_gnn_b_k': 8.0,
     'L2_ffn_W_x': 8.0,
     'L2_ffn_W_slice': 8.0,
     'L2_ffn_hy_conv_w': 8.0,
     'L2_ffn_hy_A_log': 8.0,
     'L2_ffn_hy_fcD_w': 8.0,
     'L3_ffn_Wr': 3.636,
     'L3_ffn_W1s': 5.375,
     'L3_ffn_W2s': 5.038,
     'L3_ffn_W1p': 7.475,
     'L3_ffn_W2p': 6.682}
    for name, (base, spread) in spreads.items():
        noise = np.random.default_rng([zlib.crc32(name.encode()), seed]).standard_normal(out[name].shape)
        drawn = base * np.exp(spread * noise) if base else spread * noise
        out[name] = jnp.asarray(drawn.astype(out[name].dtype))
    for name, factor in factors.items():
        out[name] = (out[name] * factor).astype(out[name].dtype)
    return out
```

```python
from contextlib import ExitStack

import concourse.bass as bass
from concourse import mybir

ALU = mybir.AluOpType
ACT = mybir.ActivationFunctionType
F32 = mybir.dt.float32
F32R = mybir.dt.float32r
I32 = mybir.dt.int32
U32 = mybir.dt.uint32
AX_X = mybir.AxisListType.X

P = 128
GB = 4
T = GB * P
S = 2
EPS = 1e-5
E = 8


class Steps:

    def __init__(self, sem, names):
        self.sem, self.names, self.at = sem, names.split(), 0

    def start(self, engine):
        engine.sem_inc(self.sem, 1)

    def done(self, turn, name):
        return turn * len(self.names) + (self.names.index(name) + 2)

    def all_done(self, turns):
        return turns * len(self.names) + 1

    def mark(self, instruction, name):
        assert self.names[self.at % len(self.names)] == name, (name, self.names[self.at % len(self.names)])
        self.at += 1
        instruction.then_inc(self.sem, 1)


class Count:

    def __init__(self, sem, per, credit=0):
        self.sem, self.per, self.credit = sem, per, credit

    def done(self, group, k=0):
        assert k + 1 + self.credit >= 0
        return group * self.per + (k + 1 + self.credit)


class Chip:

    def __init__(self, nc, ctx, io, n_batch):
        self.nc, self.ctx, self.io, self.nb = nc, ctx, io, n_batch
        self.groups = n_batch // GB
        self.sems = []
        self.turns = self.groups // S
        pad = n_batch + GB
        self.x = self.sb("x_all", [P, pad, P])
        self.stats = self.sb("ln_stats", [P, pad, 6])
        self.mean = self.sb("ln_mean", [P, pad])
        self.rstd = self.sb("ln_rstd", [P, pad])
        self.rstd2 = self.sb("ln_rstd2", [P, pad])
        self.ratio = self.sb("ln_ratio", [P, pad])
        self.tmp = [self.sb(f"ln_tmp{k}", [P, pad]) for k in range(3)]
        self.mhalf = self.sb("minus_half", [P, pad])
        self.phalf = self.sb("plus_half", [P, pad])
        self.pace = self.sb("pace", [P, 1])
        self.ident = self.sb("identity", [P, P])
        self.ones = self.sb("ones", [P, P])

    def sb(self, name, shape, dt=F32, ctx=None):
        return (ctx or self.ctx).enter_context(self.nc.sbuf_tensor(name, shape, dt))

    def ps(self, name, ctx, shape=(P, T)):
        return ctx.enter_context(self.nc.psum_tensor(name, list(shape), F32))

    def sem(self, name):
        self.sems.append(self.nc.alloc_semaphore(name=name))
        return self.sems[-1]

    def grouped(self, t):
        if len(t.shape) == 3:
            return t[:, :, :].rearrange("p (g b) f -> p g b f", b=GB)
        return t[:, :].rearrange("p (g b) -> p g b", b=GB)


class Chain:

    def __init__(self, engine, sem):
        self.engine, self.sem, self.n = engine, sem, 0

    def link(self, instruction):
        self.n += 1
        instruction.then_inc(self.sem, 1)
        self.engine.wait_ge(self.sem, self.n)


def load_and_constants(c):
    nc, nb = c.nc, c.nb
    loaded, made, filled, counted = (c.sem(n) for n in ("x_loaded", "const_made", "const_zero", "stats_made"))
    xg, sg = c.grouped(c.x), c.grouped(c.stats)
    with nc.Block() as block:

        @block.sync
        def _(sp):
            n = nb // 4
            for k in range(4):
                sp.dma_start(c.x[:, k * n:(k + 1) * n, :],
                             c.io["x"][k * n:(k + 1) * n].rearrange("b n d -> n b d")).then_inc(loaded, 16)

        @block.gpsimd
        def _(pool):
            pool.memset(c.ident[:], 0.0).then_inc(filled, 1)
            pool.memset(c.ones[:], 1.0).then_inc(made, 1)
            pool.memset(c.mhalf[:], -0.5).then_inc(made, 1)
            pool.memset(c.phalf[:], 0.5).then_inc(made, 1)
            pool.memset(c.x[:, nb:nb + GB, :], 0.0).then_inc(made, 1)
            pool.memset(c.stats[:, nb:nb + GB, :], 0.0).then_inc(made, 1)
            pool.wait_ge(filled, 1)
            pool.affine_select(out=c.ident[:], in_=c.ident[:], compare_op=ALU.not_equal, fill=1.0, base=0,
                               pattern=[[-1, P]], channel_multiplier=1).then_inc(made, 1)
            pool.wait_ge(made, 6)

        @block.vector
        def _(dve):
            dve.wait_ge(loaded, 64)
            with dve.Fori(0, c.groups) as g:
                for b in range(GB):
                    last = dve.bn_stats(sg[:, g, b, :], xg[:, g, b, :])
                last.then_inc(counted, 1)
            dve.wait_ge(counted, c.groups)


def ln_dve(c, dve, chain, powed, double):
    m0, m1 = c.stats[:, :, 1], c.stats[:, :, 4]
    q0, q1 = c.stats[:, :, 2], c.stats[:, :, 5]
    t0, t1, t2 = (t[:] for t in c.tmp)
    link = chain.link
    link(dve.tensor_tensor(t0, m0, m1, ALU.subtract))
    link(dve.tensor_tensor(t1, m0, m1, ALU.add))
    link(dve.tensor_scalar(c.mean[:], t1, 0.5, None, ALU.mult))
    link(dve.tensor_tensor(t1, q0, q1, ALU.add))
    link(dve.tensor_tensor(t2, t0, t0, ALU.mult))
    link(dve.tensor_scalar(t2, t2, 0.25, None, ALU.mult))
    link(dve.scalar_tensor_tensor(t0, t1, 1.0 / P, t2, ALU.mult, ALU.add))
    dve.tensor_scalar(t1, t0, EPS, None, ALU.add).then_inc(powed, 1)
    dve.wait_ge(powed, 2)
    if double:
        link(dve.tensor_tensor(t2, c.rstd[:], c.rstd[:], ALU.mult))
        link(dve.tensor_tensor(t2, t2, t0, ALU.mult))
        dve.tensor_scalar(t2, t2, EPS, None, ALU.add).then_inc(powed, 1)
        dve.wait_ge(powed, 5)
        link(dve.tensor_tensor(c.rstd[:], c.rstd[:], c.rstd2[:], ALU.mult))


def ln_pool(c, pool, powed, double):
    pool.wait_ge(powed, 1)
    pool.tensor_tensor(c.rstd[:], c.tmp[1][:], c.mhalf[:], ALU.pow).then_inc(powed, 1)
    if double:
        pool.wait_ge(powed, 3)
        pool.tensor_tensor(c.rstd2[:], c.tmp[2][:], c.mhalf[:], ALU.pow).then_inc(powed, 1)
        pool.tensor_tensor(c.ratio[:], c.tmp[2][:], c.phalf[:], ALU.pow).then_inc(powed, 1)


def column_attention(c):
    nc, io, turns = c.nc, c.io, c.turns
    xg, sg = c.grouped(c.x), c.grouped(c.stats)
    meang, rstdg = c.grouped(c.mean), c.grouped(c.rstd)
    adjg = io["adj"].rearrange("(g b) i j -> g i b j", b=GB)
    with ExitStack() as ctx:
        sb = lambda name, shape, dt=F32: c.sb("ca_" + name, shape, dt, ctx)
        w, wT, a12, wa, wa1b = sb("w", [P, P]), sb("wT", [P, P]), sb("a12", [P, 2]), sb("wa", [P, 2]), sb("wa1b", [P, P])
        hp = sb("hp", [P, c.nb, P])
        hpg = hp[:, :, :].rearrange("p (g b) f -> p g b f", b=GB)
        adj_i = [sb(f"adj_i{s}", [P, GB, P], I32) for s in range(S)]
        adj_f = [sb(f"adj_f{s}", [P, GB, P]) for s in range(S)]
        xn = [sb(f"xn{s}", [P, GB, P]) for s in range(S)]
        xT = [sb(f"xT{s}", [P, T]) for s in range(S)]
        pen = [sb(f"pen{s}", [P, GB, P]) for s in range(S)]
        score = [sb(f"score{s}", [P, GB, P]) for s in range(S)]
        hs = [sb(f"hs{s}", [P, GB, P]) for s in range(S)]
        s2 = [sb(f"s2{s}", [P, GB]) for s in range(S)]
        nmax = [sb(f"nmax{s}", [P, GB]) for s in range(S)]
        den = [sb(f"den{s}", [P, GB]) for s in range(S)]
        rden = [sb(f"rden{s}", [P, GB]) for s in range(S)]
        bank = [[c.ps(f"ca_bank{s}{k}", ctx) for k in range(4)] for s in range(S)]
        loaded, chain, powed, prepared = (c.sem("ca_" + n) for n in ("loaded", "chain", "powed", "prepared"))
        gelued, added = c.sem("ca_gelued"), c.sem("ca_added")
        adj_in = [c.sem(f"ca_adj_in{s}") for s in range(S)]
        dv = [Steps(c.sem(f"ca_dve{s}"), "adj xn pen s2 masked leaky max rden hs") for s in range(S)]
        ac = [Steps(c.sem(f"ca_act{s}"), "xT exp hp") for s in range(S)]
        pe_ = [Steps(c.sem(f"ca_pe{s}"), "xT adjT h out") for s in range(S)]
        with nc.Block() as block:

            @block.sync
            def _(sp):
                sp.dma_start(w[:], io["L0_gnn_W"]).then_inc(loaded, 16)
                sp.dma_start(a12[:], io["L0_gnn_a"].rearrange("(t d) o -> d (t o)", t=2),
                             allow_slow_non_contiguous=True).then_inc(loaded, 16)
                with sp.Fori(0, turns) as i:
                    for s in range(S):
                        sp.wait_ge(dv[s].sem, dv[s].all_done(i))
                        sp.dma_start(adj_i[s][:], adjg[i * S + s]).then_inc(adj_in[s], 16)

            @block.gpsimd
            def _(pool):
                ln_pool(c, pool, powed, False)

            @block.scalar
            def _(act):
                for s in range(S):
                    ac[s].start(act)
                with act.Fori(0, turns) as i:
                    for s in range(S):
                        act.wait_ge(pe_[s].sem, pe_[s].done(i, "xT"))
                        ac[s].mark(act.activation(xT[s][:], bank[s][0][:], ACT.Copy), "xT")
                    for s in range(S):
                        act.wait_ge(dv[s].sem, dv[s].done(i, "max"))
                        for b in range(GB):
                            last = act.activation(score[s][:, b, :], score[s][:, b, :], ACT.Exp,
                                                  bias=nmax[s][:, b:b + 1], accum_out=den[s][:, b:b + 1])
                        ac[s].mark(last, "exp")
                    for s in range(S):
                        act.wait_ge(pe_[s].sem, pe_[s].done(i, "out"))
                        ac[s].mark(act.activation(hpg[:, i * S + s, :, :], bank[s][1][:, :].rearrange("p (b f) -> p b f", b=GB), ACT.Copy), "hp")
                for s in range(S):
                    act.wait_ge(ac[s].sem, ac[s].all_done(turns))
                with act.Fori(0, c.groups) as g:
                    act.activation(hpg[:, g, :, :], hpg[:, g, :, :], ACT.Gelu).then_inc(gelued, 1)

            @block.vector
            def _(dve):
                for s in range(S):
                    dv[s].start(dve)
                ln_dve(c, dve, Chain(dve, chain), powed, False)
                dve.wait_ge(loaded, 32)
                dve.wait_ge(prepared, 1)
                dve.tensor_copy(wT[:], bank[0][0][:, 0:P]).then_inc(prepared, 1)
                dve.wait_ge(prepared, 3)
                dve.tensor_copy(wa[:], bank[0][0][:, 0:2]).then_inc(prepared, 1)
                dve.wait_ge(prepared, 4)
                dve.tensor_scalar(wa1b[:], c.ones[:], wa[:, 0:1], None, ALU.mult).then_inc(prepared, 1)
                with dve.Fori(0, turns) as i:
                    for s in range(S):
                        dve.wait_ge(ac[s].sem, ac[s].all_done(i))
                        dve.wait_ge(adj_in[s], i * 16 + 16)
                        dv[s].mark(dve.tensor_copy(adj_f[s][:], adj_i[s][:]), "adj")
                        for b in range(GB):
                            last = dve.tensor_scalar(xn[s][:, b, :], xg[:, i * S + s, b, :], meang[:, i * S + s, b:b + 1],
                                                     rstdg[:, i * S + s, b:b + 1], ALU.subtract, ALU.mult)
                        dv[s].mark(last, "xn")
                    for s in range(S):
                        dve.wait_ge(pe_[s].sem, pe_[s].done(i, "adjT"))
                        dv[s].mark(dve.tensor_scalar(pen[s][:].rearrange("p b f -> p (b f)"), bank[s][1][:], 0.0, -1e20 / 0.4,
                                                     ALU.is_le, ALU.mult), "pen")
                    for s in range(S):
                        dve.wait_ge(pe_[s].sem, pe_[s].done(i, "h"))
                        dv[s].mark(dve.tensor_copy(s2[s][:], bank[s][3][:, 0:GB]), "s2")
                    for s in range(S):
                        dve.wait_ge(dv[s].sem, dv[s].done(i, "s2"))
                        for b in range(GB):
                            last = dve.scalar_tensor_tensor(score[s][:, b, :], bank[s][2][:, b * P:(b + 1) * P],
                                                            s2[s][:, b:b + 1], pen[s][:, b, :], ALU.add, ALU.add)
                        dv[s].mark(last, "masked")
                        dve.wait_ge(dv[s].sem, dv[s].done(i, "masked"))
                        dv[s].mark(dve.scalar_tensor_tensor(score[s][:], score[s][:], 0.4, score[s][:],
                                                            ALU.mult, ALU.max), "leaky")
                        dve.wait_ge(dv[s].sem, dv[s].done(i, "leaky"))
                        dv[s].mark(dve.tensor_reduce(nmax[s][:], score[s][:], AX_X, ALU.max, negate=True), "max")
                    for s in range(S):
                        dve.wait_ge(ac[s].sem, ac[s].done(i, "exp"))
                        dv[s].mark(dve.reciprocal(rden[s][:], den[s][:]), "rden")
                        dve.wait_ge(dv[s].sem, dv[s].done(i, "rden"))
                        for b in range(GB):
                            last = dve.tensor_scalar(hs[s][:, b, :], bank[s][0][:, b * P:(b + 1) * P],
                                                     rden[s][:, b:b + 1], None, ALU.mult)
                        dv[s].mark(last, "hs")
                with dve.Fori(0, c.groups) as g:
                    dve.wait_ge(gelued, g + 1)
                    dve.tensor_tensor(xg[:, g, :, :], xg[:, g, :, :], hpg[:, g, :, :], ALU.add).then_inc(added, 1)
                    dve.wait_ge(added, g + 1)
                    for b in range(GB):
                        dve.bn_stats(sg[:, g, b, :], xg[:, g, b, :])

            @block.tensor
            def _(pe):
                for s in range(S):
                    pe_[s].start(pe)
                pe.wait_ge(loaded, 32)
                pe.transpose(bank[0][0][:, 0:P], w[:], c.ident[:]).then_inc(prepared, 1)
                pe.wait_ge(prepared, 2)
                pe.matmul(bank[0][0][:, 0:2], wT[:], a12[:], start=True, stop=True).then_inc(prepared, 1)
                pe.wait_ge(prepared, 5)
                with pe.Fori(0, turns) as i:
                    for s in range(S):
                        pe.wait_ge(dv[s].sem, dv[s].done(i, "xn"))
                        for b in range(GB):
                            last = pe.transpose(bank[s][0][:, b * P:(b + 1) * P], xn[s][:, b, :], c.ident[:])
                        pe_[s].mark(last, "xT")
                        for b in range(GB):
                            last = pe.transpose(bank[s][1][:, b * P:(b + 1) * P], adj_f[s][:, b, :], c.ident[:])
                        pe_[s].mark(last, "adjT")
                    for s in range(S):
                        pe.wait_ge(ac[s].sem, ac[s].done(i, "xT"))
                        pe.matmul(bank[s][2][:], wa1b[:], xT[s][:], start=True, stop=True)
                        for b in range(GB):
                            pe.matmul(bank[s][3][:, b:b + 1], xT[s][:, b * P:(b + 1) * P], wa[:, 1:2],
                                      start=True, stop=True)
                        for b in range(GB):
                            last = pe.matmul(bank[s][0][:, b * P:(b + 1) * P], xT[s][:, b * P:(b + 1) * P], w[:],
                                             start=True, stop=True)
                        pe_[s].mark(last, "h")
                    for s in range(S):
                        pe.wait_ge(dv[s].sem, dv[s].done(i, "hs"))
                        for b in range(GB):
                            last = pe.matmul(bank[s][1][:, b * P:(b + 1) * P], score[s][:, b, :], hs[s][:, b, :],
                                             start=True, stop=True)
                        pe_[s].mark(last, "out")


def experts(c, tag, hidden, w1, b1, w2, b2, wr, br=None, gain=None, shift=None, routed_gain=False, double=False,
            shared=None):
    nc = c.nc
    ch = hidden // P
    first = 1 if shared else 0
    ne = E + first
    nk = ne * ch
    xg, sg = c.grouped(c.x), c.grouped(c.stats)
    meang, rstdg, ratiog = c.grouped(c.mean), c.grouped(c.rstd), c.grouped(c.ratio)
    SLOTS = 4
    PROD1, GELU, SPLIT, PROD2, YCOPY = 5, 4, 4, 2, 1
    NORM, TURN, COPY, CUT, ROUTE, TOP, TANH, PROBS = 0, 1, 2, 3, 3, 5, 7, 8
    assert nk % SLOTS == 0 and ch > YCOPY and PROBS < nk - PROD1 and (br is None or gain is None or True)

    with ExitStack() as ctx:
        sb = lambda name, shape, dt=F32: c.sb(f"{tag}_{name}", shape, dt, ctx)
        sem = lambda name: c.sem(f"{tag}_{name}")
        w1h, w1l = sb("w1_hi", [P, nk, P], F32R), sb("w1_lo", [P, nk, P], F32R)
        w2h, w2l = sb("w2_hi", [P, nk, P], F32R), sb("w2_lo", [P, nk, P], F32R)
        RAW = 4
        raw = [sb(f"raw{k}", [P, ch, P]) for k in range(RAW)]
        b1_rows, b2_rows, gain_rows, shift_rows = sb("b1_rows", [nk, P]), sb("b2_rows", [ne, P]), sb("gain_rows", [E, P]), sb("shift_rows", [E, P])
        b1T, b2T, gainT, shiftT = sb("b1T", [P, nk]), sb("b2T", [P, ne]), sb("gainT", [P, E]), sb("shiftT", [P, E])
        wr_sb, br_row, br_all = sb("wr", [P, E]), sb("br_row", [1, E]), sb("br_all", [P, E])
        iota, iota_i = sb("iota", [P, GB, E]), sb("iota_i", [P, GB, E], I32)
        shift_wide = sb("shift_wide", [P, P])
        xn, xf = sb("xn", [P, GB, P]), sb("xf", [P, T])
        x_hi = [sb(f"x_hi{u}", [P, T], F32R) for u in range(2)]
        x_lo = [sb(f"x_lo{u}", [P, T], F32R) for u in range(2)]
        g_full = [sb(f"g_full{k}", [P, T]) for k in range(SLOTS)]
        g_hi = [sb(f"g_hi{k}", [P, T], F32R) for k in range(SLOTS)]
        g_lo = [sb(f"g_lo{k}", [P, T], F32R) for k in range(SLOTS)]
        yT = [sb(f"yT{k}", [P, T]) for k in range(2)]
        probs = [sb(f"probs{u}", [P, GB, E]) for u in range(2)]
        logit, top = sb("logit", [P, GB, E]), sb("top", [P, GB, E])
        where, wheref = sb("where", [P, GB, E], U32), sb("wheref", [P, GB, E])
        gap, half, pa, pb = sb("gap", [P, GB]), sb("half", [P, GB]), sb("pa", [P, GB]), sb("pb", [P, GB])
        is_a, is_b = sb("is_a", [P, GB, E]), sb("is_b", [P, GB, E])
        hid = [c.ps(f"{tag}_hid{k}", ctx) for k in range(SLOTS)]
        ysum = [c.ps(f"{tag}_ysum{k}", ctx) for k in range(2)]
        yback, misc = c.ps(f"{tag}_yback", ctx), c.ps(f"{tag}_misc", ctx)

        small_in, chain, powed, prep, made = sem("small_in"), sem("chain"), sem("powed"), sem("prep"), sem("made")
        raw_in = [sem(f"raw_in{k}") for k in range(RAW)]
        raw_hi, raw_lo, b1_sum = sem("raw_hi"), sem("raw_lo"), sem("b1_sum")
        hid_ready = Count(sem("hid_ready"), nk)
        gelu_done = Count(sem("gelu_done"), nk, SLOTS)
        lo_done, second = Count(sem("lo_done"), nk, SLOTS), Count(sem("second"), nk, SLOTS)
        hi_done = [Count(sem("hi_even"), nk // 2), Count(sem("hi_odd"), nk // 2)]
        y_copied, turned_back, added = Count(sem("y_copied"), ne, 2), Count(sem("turned_back"), ne, 2), Count(sem("added"), ne, 1)
        xn_ready, xf_ready, gap_ready, tanh_ready = (
            Count(sem(n), 1) for n in ("xn_ready", "xf_ready", "gap_ready", "tanh_ready"))
        xT_ready, logit_ready, x_split, top_ready = (
            Count(sem(n), k, 1) for n, k in (("xT_ready", 1), ("logit_ready", 1), ("x_split", 2), ("top_ready", 5)))
        route = Count(sem("route"), 8)
        small = [(b1_rows[first * ch:nk, :], b1.rearrange("e (c h) -> (e c) h", h=P)), (b2_rows[first:ne, :], b2), (wr_sb[:], wr)]
        if shared:
            small += [(b1_rows[0:ch, :], shared[1].rearrange("(c h) -> c h", h=P)),
                      (b2_rows[0:1, :], shared[3].rearrange("(o d) -> o d", o=1))]
        if br is not None:
            small += [(br_row[:], br.rearrange("(o e) -> o e", o=1))]
        if gain is not None:
            small += [(gain_rows[:], gain), (shift_rows[:], shift)]

        def source(k):
            e = k % ne
            if k < ne:
                w = shared[0] if e < first else w1[e - first]
                return w.rearrange("d (c h) -> d c h", h=P)
            w = shared[2] if e < first else w2[e - first]
            return w.rearrange("(c h) d -> h c d", h=P)

        with nc.Block() as block:

            @block.sync
            def _(sp):
                for dst, src in small:
                    sp.dma_start(dst, src).then_inc(small_in, 16)
                for k in range(2 * ne):
                    if k >= RAW:
                        sp.wait_ge(raw_lo, k - RAW + 1)
                        if gain is not None and k - RAW < ne:
                            sp.wait_ge(b1_sum, k - RAW + 1)
                    sp.dma_start(raw[k % RAW][:], source(k)).then_inc(raw_in[k % RAW], 16)

            @block.gpsimd
            def _(pool):
                pool.iota(iota_i[:], pattern=[[0, GB], [1, E]], base=0, channel_multiplier=0).then_inc(made, 1)
                ln_pool(c, pool, powed, double)

            @block.scalar
            def _(act):
                act.sem_inc(gelu_done.sem, gelu_done.credit)
                act.sem_inc(y_copied.sem, y_copied.credit)

                def copy_xT(g):
                    act.wait_ge(xT_ready.sem, xT_ready.done(g))
                    act.wait_ge(x_split.sem, x_split.done(g, -1))
                    act.wait_ge(logit_ready.sem, logit_ready.done(g, -1))
                    act.activation(xf[:], misc[:], ACT.Copy).then_inc(xf_ready.sem, 1)

                def tanh(g):
                    act.wait_ge(gap_ready.sem, gap_ready.done(g))
                    act.activation(half[:], gap[:], ACT.Tanh, scale=0.5).then_inc(tanh_ready.sem, 1)

                def gelu(g, u, n):
                    act.wait_ge(hid_ready.sem, hid_ready.done(g, n))
                    act.wait_ge(lo_done.sem, lo_done.done(g, n - SLOTS))
                    k = (u * nk + n) % SLOTS
                    act.activation(g_full[k][:], hid[k][:], ACT.Gelu, bias=b1T[:, n % nk:n % nk + 1])\
                        .then_inc(gelu_done.sem, 1)
                    if n % 2:
                        act.wait_ge(gelu_done.sem, gelu_done.done(g, n))
                        act.wait_ge(second.sem, second.done(g, n - SLOTS))
                        act.activation(g_hi[k][:], g_full[k][:], ACT.Copy).then_inc(hi_done[1].sem, 1)

                def copy_y(g, u, e):
                    k = (u * ne + e) % 2
                    act.wait_ge(second.sem, second.done(g, e * ch + ch - 1))
                    act.wait_ge(turned_back.sem, turned_back.done(g, e - 2))
                    act.activation(yT[k][:], ysum[k][:], ACT.Identity, bias=b2T[:, e:e + 1]).then_inc(y_copied.sem, 1)

                for k in range(2 * ne):
                    act.wait_ge(raw_in[k % RAW], 16 * (k // RAW + 1))
                    if k == 0:
                        act.wait_ge(prep, 2)
                    e = k % ne
                    dst = (w1h if k < ne else w2h)[:, e * ch:(e + 1) * ch, :]
                    scale = gainT[:, e - first:e - first + 1] if gain is not None and k < ne and e >= first else 1.0
                    act.activation(dst, raw[k % RAW][:], ACT.Copy, scale=scale).then_inc(raw_hi, 1)
                copy_xT(0)
                tanh(0)
                act.wait_ge(prep, 5)
                for n in range(GELU):
                    gelu(0, 0, n)
                with act.Fori(0, c.turns) as i:
                    for u in range(2):
                        g = i * 2 + u
                        for m in range(nk):
                            gelu(g, u, m + GELU)
                            if (m + YCOPY) % ch == ch - 1 and m + YCOPY < nk:
                                copy_y(g, u, (m + YCOPY) // ch)
                            if m == COPY:
                                copy_xT(g + 1)
                            if m == TANH:
                                tanh(g + 1)

            @block.vector
            def _(dve):
                ln = Chain(dve, chain)
                link = ln.link
                dve.sem_inc(lo_done.sem, lo_done.credit)
                dve.sem_inc(added.sem, added.credit)
                dve.sem_inc(x_split.sem, x_split.credit)
                dve.sem_inc(top_ready.sem, top_ready.credit)
                ln_dve(c, dve, ln, powed, double)

                def normalise(g):
                    dve.wait_ge(xT_ready.sem, xT_ready.done(g, -1))
                    for b in range(GB):
                        last = dve.tensor_scalar(xn[:, b, :], xg[:, g, b, :], meang[:, g, b:b + 1], rstdg[:, g, b:b + 1],
                                                 ALU.subtract, ALU.mult)
                    last.then_inc(xn_ready.sem, 1)

                def cut(g, u):
                    dve.wait_ge(xf_ready.sem, xf_ready.done(g))
                    dve.tensor_copy(x_hi[u][:], xf[:]).then_inc(x_split.sem, 1)
                    dve.wait_ge(x_split.sem, x_split.done(g, 0))
                    dve.tensor_tensor(x_lo[u][:], xf[:], x_hi[u][:].bitcast(F32), ALU.subtract).then_inc(x_split.sem, 1)

                def top_two(g):
                    dve.wait_ge(logit_ready.sem, logit_ready.done(g))
                    for b in range(GB):
                        scale = ratiog[:, g, b:b + 1] if double and not routed_gain else 1.0
                        last = dve.scalar_tensor_tensor(logit[:, b, :], misc[:, b * E:(b + 1) * E], scale, br_all[:],
                                                        ALU.mult, ALU.add)
                    last.then_inc(top_ready.sem, 1)
                    dve.wait_ge(top_ready.sem, top_ready.done(g, 0))
                    dve.memset(c.pace[:], 0.0)
                    for b in range(GB):
                        last = dve.max(top[:, b, :], logit[:, b, :])
                    last.then_inc(top_ready.sem, 1)
                    dve.wait_ge(top_ready.sem, top_ready.done(g, 1))
                    dve.tensor_tensor(gap[:], top[:, :, 0], top[:, :, 1], ALU.subtract).then_inc(gap_ready.sem, 1)
                    for b in range(GB):
                        last = dve.max_index(where[:, b, :], top[:, b, :], logit[:, b, :])
                    last.then_inc(top_ready.sem, 1)
                    dve.wait_ge(top_ready.sem, top_ready.done(g, 2))
                    dve.tensor_copy(wheref[:], where[:]).then_inc(top_ready.sem, 1)
                    dve.wait_ge(top_ready.sem, top_ready.done(g, 3))
                    wide = [P, GB, E]
                    dve.tensor_tensor(is_a[:], iota[:], wheref[:, :, 0:1].to_broadcast(wide), ALU.is_equal)
                    dve.tensor_tensor(is_b[:], iota[:], wheref[:, :, 1:2].to_broadcast(wide), ALU.is_equal)\
                        .then_inc(top_ready.sem, 1)

                def two_probs(g, u):
                    dve.wait_ge(tanh_ready.sem, tanh_ready.done(g))
                    wide = [P, GB, E]
                    dve.tensor_scalar(pa[:], half[:], 0.5, 0.5, ALU.mult, ALU.add)
                    dve.tensor_scalar(pb[:], half[:], -0.5, 0.5, ALU.mult, ALU.add).then_inc(route.sem, 1)
                    dve.wait_ge(route.sem, route.done(g, 0))
                    dve.tensor_tensor(is_a[:], is_a[:], pa[:].unsqueeze(2).to_broadcast(wide), ALU.mult)
                    dve.tensor_tensor(is_b[:], is_b[:], pb[:].unsqueeze(2).to_broadcast(wide), ALU.mult)\
                        .then_inc(route.sem, 1)
                    dve.wait_ge(route.sem, route.done(g, 1))
                    dve.tensor_tensor(probs[u][:], is_a[:], is_b[:], ALU.add).then_inc(route.sem, 6)

                def split(g, u, n):
                    k = (u * nk + n) % SLOTS
                    dve.wait_ge(gelu_done.sem, gelu_done.done(g, n))
                    dve.wait_ge(second.sem, second.done(g, n - SLOTS))
                    if n % 2 == 0:
                        dve.tensor_copy(g_hi[k][:], g_full[k][:]).then_inc(hi_done[0].sem, 1)
                    dve.wait_ge(hi_done[n % 2].sem, hi_done[n % 2].done(g, n // 2))
                    dve.tensor_tensor(g_lo[k][:], g_full[k][:], g_hi[k][:].bitcast(F32), ALU.subtract)\
                        .then_inc(lo_done.sem, 1)

                def add(g, u, e):
                    dve.wait_ge(turned_back.sem, turned_back.done(g, e))
                    dve.wait_ge(added.sem, added.done(g, e - 1))
                    if e == first:
                        dve.wait_ge(route.sem, route.done(g, 7))
                    for b in range(GB):
                        p = 1.0 if e < first else probs[u][:, b, e - first:e - first + 1]
                        last = dve.scalar_tensor_tensor(xg[:, g, b, :], yback[:, b * P:(b + 1) * P], p, xg[:, g, b, :],
                                                        ALU.mult, ALU.add)
                    last.then_inc(added.sem, 1)

                dve.wait_ge(prep, 1)
                dve.wait_ge(made, 1)
                dve.tensor_copy(iota[:], iota_i[:])
                dve.tensor_copy(b2T[:], yback[:, 0:ne])
                if gain is not None:
                    dve.tensor_copy(gainT[:], hid[0][:, 0:E])
                    link(dve.tensor_copy(shiftT[:], hid[1][:, 0:E]))
                if routed_gain:
                    dve.tensor_scalar(shift_wide[:], c.ones[:], shiftT[:, 0:1], None, ALU.mult)
                if br is None:
                    dve.memset(br_all[:], 0.0)
                dve.drain().then_inc(prep, 1)
                dve.wait_ge(prep, 3)
                if br is not None:
                    dve.tensor_copy(br_all[:], hid[2][:, 0:E])
                if routed_gain:
                    dve.tensor_scalar(wr_sb[:], wr_sb[:], gainT[:, 0:1], None, ALU.mult)
                dve.drain().then_inc(prep, 1)
                for k in range(2 * ne):
                    e = k % ne
                    dst, hi = ((w[:, e * ch:(e + 1) * ch, :]) for w in ((w1l, w1h) if k < ne else (w2l, w2h)))
                    dve.wait_ge(raw_hi, k + 1)
                    if gain is not None and k < ne and e >= first:
                        ins = dve.scalar_tensor_tensor(dst, raw[k % RAW][:], gainT[:, e - first:e - first + 1],
                                                       hi.bitcast(F32), ALU.mult, ALU.subtract)
                    else:
                        ins = dve.tensor_tensor(dst, raw[k % RAW][:], hi.bitcast(F32), ALU.subtract)
                    ins.then_inc(raw_lo, 1)
                if gain is not None:
                    dve.wait_ge(b1_sum, ne)
                    link(dve.tensor_copy(b1T[:], misc[:, 0:nk]))
                    dve.tensor_tensor(b1T[:], b1T[:], ysum[0][:, 0:nk], ALU.add).then_inc(prep, 1)
                else:
                    dve.tensor_copy(b1T[:], misc[:, 0:nk]).then_inc(prep, 1)
                normalise(0)
                cut(0, 0)
                top_two(0)
                two_probs(0, 0)
                for n in range(SPLIT):
                    split(0, 0, n)
                with dve.Fori(0, c.turns) as i:
                    for u in range(2):
                        g = i * 2 + u
                        for m in range(nk):
                            split(g, u, m + SPLIT)
                            if m == NORM:
                                normalise(g + 1)
                            if m == CUT:
                                cut(g + 1, 1 - u)
                            if m == TOP:
                                top_two(g + 1)
                            if m == PROBS:
                                two_probs(g + 1, 1 - u)
                            if m % ch == ch - 1:
                                add(g, u, m // ch)
                        dve.wait_ge(added.sem, added.done(g, ne - 1))
                        for b in range(GB):
                            dve.bn_stats(sg[:, g, b, :], xg[:, g, b, :])

            @block.tensor
            def _(pe):
                pe.sem_inc(second.sem, second.credit)
                pe.sem_inc(turned_back.sem, turned_back.credit)
                pe.sem_inc(xT_ready.sem, xT_ready.credit)
                pe.sem_inc(logit_ready.sem, logit_ready.credit)

                def turn(g):
                    pe.wait_ge(xn_ready.sem, xn_ready.done(g))
                    pe.wait_ge(top_ready.sem, top_ready.done(g, -1))
                    for b in range(GB):
                        last = pe.transpose(misc[:, b * P:(b + 1) * P], xn[:, b, :], c.ident[:])
                    last.then_inc(xT_ready.sem, 1)

                def router(g):
                    pe.wait_ge(xf_ready.sem, xf_ready.done(g))
                    for b in range(GB):
                        last = pe.matmul(misc[:, b * E:(b + 1) * E], xf[:, b * P:(b + 1) * P], wr_sb[:], start=True, stop=True)
                    last.then_inc(logit_ready.sem, 1)

                def product(out, hi, lo, x, y, start, stop):
                    pe.matmul(out, hi, x, start=start, stop=False)
                    pe.matmul(out, hi, y, start=False, stop=False)
                    return pe.matmul(out, lo, x, start=False, stop=stop)

                def first_product(g, u, n):
                    k = (u * nk + n) % SLOTS
                    if n % nk == 0:
                        pe.wait_ge(x_split.sem, x_split.done(g, 2 * (n // nk) + 1))
                    pe.wait_ge(gelu_done.sem, gelu_done.done(g, n - SLOTS))
                    v = (u + n // nk) % 2
                    product(hid[k][:], w1h[:, n % nk, :], w1l[:, n % nk, :], x_hi[v][:], x_lo[v][:], True, True)\
                        .then_inc(hid_ready.sem, 1)

                def second_product(g, u, n):
                    k = (u * nk + n) % SLOTS
                    pe.wait_ge(lo_done.sem, lo_done.done(g, n))
                    e = n // ch
                    if n % ch == 0:
                        pe.wait_ge(y_copied.sem, y_copied.done(g, e - 2))
                    product(ysum[(u * ne + e) % 2][:], w2h[:, n % nk, :], w2l[:, n % nk, :], g_hi[k][:], g_lo[k][:],
                            n % ch == 0, n % ch == ch - 1).then_inc(second.sem, 1)

                def turn_back(g, u, e):
                    k = (u * ne + e) % 2
                    pe.wait_ge(y_copied.sem, y_copied.done(g, e))
                    pe.wait_ge(added.sem, added.done(g, e - 1))
                    for b in range(GB):
                        last = pe.transpose(yback[:, b * P:(b + 1) * P], yT[k][:, b * P:(b + 1) * P], c.ident[:])
                    last.then_inc(turned_back.sem, 1)

                pe.wait_ge(small_in, 16 * len(small))
                pe.transpose(misc[:, 0:nk], b1_rows[:], c.ident[0:nk, 0:nk])
                last = pe.transpose(yback[:, 0:ne], b2_rows[:], c.ident[0:ne, 0:ne])
                if gain is not None:
                    pe.transpose(hid[0][:, 0:E], gain_rows[:], c.ident[0:E, 0:E])
                    last = pe.transpose(hid[1][:, 0:E], shift_rows[:], c.ident[0:E, 0:E])
                last.then_inc(prep, 1)
                pe.wait_ge(prep, 2)
                if br is not None:
                    last = pe.matmul(hid[2][:, 0:E], c.ones[0:1, :], br_row[:], start=True, stop=not routed_gain)
                    if routed_gain:
                        last = pe.matmul(hid[2][:, 0:E], shift_wide[:], wr_sb[:], start=False, stop=True)
                    last.then_inc(prep, 1)
                else:
                    pe.sem_inc(prep, 1)
                if gain is not None:
                    for k in range(ne):
                        pe.wait_ge(raw_in[k % RAW], 16 * (k // RAW + 1))
                        for j in range(ch):
                            last = pe.matmul(ysum[0][:, k * ch + j:k * ch + j + 1], raw[k % RAW][:, j, :], shiftT[:, k:k + 1],
                                             start=True, stop=True)
                        last.then_inc(b1_sum, 1)
                pe.wait_ge(prep, 5)
                pe.wait_ge(raw_lo, 2 * ne)
                turn(0)
                router(0)
                for n in range(PROD1):
                    first_product(0, 0, n)
                for n in range(PROD2):
                    second_product(0, 0, n)
                with pe.Fori(0, c.turns) as i:
                    for u in range(2):
                        g = i * 2 + u
                        for m in range(nk):
                            first_product(g, u, m + PROD1)
                            second_product(g, u, m + PROD2)
                            if m == TURN:
                                turn(g + 1)
                            if m == ROUTE:
                                router(g + 1)
                            if m % ch == ch - 1:
                                turn_back(g, u, m // ch)
                if PROD2 % ch:
                    pe.matmul(ysum[0][:], w2h[:, 0, :], g_hi[0][:], start=False, stop=True)


def l0_experts(c):
    io = c.io
    row = lambda v: v.rearrange("(o d) -> o d", o=1).to_broadcast([E, P])
    experts(c, "e0", 256, io["L0_ffn_W1"], io["L0_ffn_b1"], io["L0_ffn_W2"], io["L0_ffn_b2"], io["L0_ffn_Wr"],
            br=io["L0_ffn_br"], gain=row(io["L0_ffn_gamma"]), shift=row(io["L0_ffn_beta"]), routed_gain=True, double=True)


def l1_experts(c):
    io = c.io
    experts(c, "e1", 512, io["L1_ffn_W1"], io["L1_ffn_b1"], io["L1_ffn_W2"], io["L1_ffn_b2"], io["L1_ffn_Wr"],
            br=io["L1_ffn_br"], gain=io["L1_ffn_ln_g"], shift=io["L1_ffn_ln_b"], double=True)


def l3_experts(c):
    io = c.io
    experts(c, "e3", 512, io["L3_ffn_W1p"], io["L3_ffn_b1p"], io["L3_ffn_W2p"], io["L3_ffn_b2p"], io["L3_ffn_Wr"],
            shared=(io["L3_ffn_W1s"], io["L3_ffn_b1s"], io["L3_ffn_W2s"], io["L3_ffn_b2s"]))


HEADS = 8
DK = P // HEADS


def head_attention(c):
    nc, io, turns = c.nc, c.io, c.turns
    xg, sg = c.grouped(c.x), c.grouped(c.stats)
    meang, rstdg = c.grouped(c.mean), c.grouped(c.rstd)
    adjg = io["adj"].rearrange("(g b) i j -> g i b j", b=GB)
    row = lambda v: v.rearrange("(o d) -> o d", o=1)
    with ExitStack() as ctx:
        sb = lambda name, shape, dt=F32: c.sb("ha_" + name, shape, dt, ctx)
        w = {k: sb("w" + k, [P, P]) for k in "qkvo"}
        bias_rows, biasT, biasq4 = sb("bias_rows", [4, P]), sb("biasT", [P, 4]), sb("biasq4", [P, 1])
        bo_row, bv_col, ds, nds = sb("bo_row", [1, P]), sb("bv_col", [P, 1]), sb("ds", [1, 1]), sb("nds", [P, 1])
        head = sb("head", [P, HEADS])
        adj_i = [sb(f"adj_i{s}", [P, GB, P], I32) for s in range(S)]
        adj_f = [sb(f"adj_f{s}", [P, GB, P]) for s in range(S)]
        pen = [sb(f"pen{s}", [P, GB, P]) for s in range(S)]
        xn = [sb(f"xn{s}", [P, GB, P]) for s in range(S)]
        xT = [sb(f"xT{s}", [P, T]) for s in range(S)]
        qT = [sb(f"qT{s}", [P, T]) for s in range(S)]
        kT = [sb(f"kT{s}", [P, T]) for s in range(S)]
        km = [sb(f"km{s}", [P, HEADS, T]) for s in range(S)]
        va = [sb(f"va{s}", [P, GB, HEADS, DK + 1]) for s in range(S)]
        sc = [sb(f"sc{s}", [P, HEADS, P]) for s in range(S)]
        mx = [sb(f"mx{s}", [P, HEADS]) for s in range(S)]
        pT = [sb(f"pT{s}", [P, HEADS, P]) for s in range(S)]
        rd = [sb(f"rd{s}", [P, HEADS, 1]) for s in range(S)]
        on = [sb(f"on{s}", [P, HEADS, DK]) for s in range(S)]
        oT = [sb(f"oT{s}", [P, T]) for s in range(S)]
        bank = [[c.ps(f"ha_bank{s}{k}", ctx) for k in range(4)] for s in range(S)]
        loaded, chain, powed, prep, head_made = (c.sem("ha_" + n) for n in ("loaded", "chain", "powed", "prep", "head_made"))
        adj_in = [c.sem(f"ha_adj_in{s}") for s in range(S)]
        per = lambda names: " ".join(f"{n}{b}" for b in range(GB) for n in names.split())
        dv = [Steps(c.sem(f"ha_dve{s}"), "adj xn pen dist km " + per("raw max pT rd on oT") + " x") for s in range(S)]
        ac = [Steps(c.sem(f"ha_act{s}"), "xT q k v " + per("exp pT")) for s in range(S)]
        po = [Steps(c.sem(f"ha_pool{s}"), per("sub")) for s in range(S)]
        pe_ = [Steps(c.sem(f"ha_pe{s}"), "xT qkv " + per("s pT o oT") + " y") for s in range(S)]
        half = HEADS // 2
        with nc.Block() as block:

            @block.sync
            def _(sp):
                for k in "qkvo":
                    sp.dma_start(w[k][:], io["L1_gnn_W_" + k]).then_inc(loaded, 16)
                for n, k in enumerate("qkvo"):
                    sp.dma_start(bias_rows[n:n + 1, :], row(io["L1_gnn_b_" + k])).then_inc(loaded, 16)
                sp.dma_start(bo_row[:], row(io["L1_gnn_b_o"])).then_inc(loaded, 16)
                sp.dma_start(ds[:], io["L1_gnn_dist_scale"]).then_inc(loaded, 16)
                with sp.Fori(0, turns) as i:
                    for s in range(S):
                        sp.wait_ge(dv[s].sem, dv[s].all_done(i))
                        sp.dma_start(adj_i[s][:], adjg[i * S + s]).then_inc(adj_in[s], 16)

            @block.gpsimd
            def _(pool):
                for s in range(S):
                    po[s].start(pool)
                pool.memset(head[:], 1.0).then_inc(head_made, 1)
                for s in range(S):
                    pool.memset(va[s][:], 1.0).then_inc(head_made, 1)
                pool.wait_ge(head_made, 1)
                pool.affine_select(out=head[:], in_=head[:], compare_op=ALU.is_ge, fill=0.0, base=0,
                                   pattern=[[-DK, HEADS]], channel_multiplier=1).then_inc(head_made, 1)
                pool.wait_ge(head_made, S + 2)
                pool.affine_select(out=head[:], in_=head[:], compare_op=ALU.is_ge, fill=0.0, base=DK - 1,
                                   pattern=[[DK, HEADS]], channel_multiplier=-1).then_inc(head_made, 1)
                ln_pool(c, pool, powed, False)
                with pool.Fori(0, turns) as i:
                    for b in range(GB):
                        for s in range(S):
                            pool.wait_ge(dv[s].sem, dv[s].done(i, f"max{b}"))
                            po[s].mark(pool.tensor_tensor(sc[s][:], sc[s][:], mx[s][:].unsqueeze(2).to_broadcast([P, HEADS, P]),
                                                          ALU.subtract), f"sub{b}")

            @block.scalar
            def _(act):
                for s in range(S):
                    ac[s].start(act)
                act.wait_ge(prep, 4)
                with act.Fori(0, turns) as i:
                    for s in range(S):
                        act.wait_ge(pe_[s].sem, pe_[s].done(i, "xT"))
                        ac[s].mark(act.activation(xT[s][:], bank[s][0][:], ACT.Copy), "xT")
                    for s in range(S):
                        act.wait_ge(pe_[s].sem, pe_[s].done(i, "qkv"))
                        ac[s].mark(act.activation(qT[s][:], bank[s][1][:], ACT.Identity, bias=biasq4[:], scale=DK ** -0.5), "q")
                        ac[s].mark(act.activation(kT[s][:], bank[s][2][:], ACT.Identity, bias=biasT[:, 1:2]), "k")
                        for b in range(GB):
                            last = act.activation(va[s][:, b, :, 0:DK],
                                                  bank[s][3][:, b * P:(b + 1) * P].rearrange("p (h d) -> p h d", h=HEADS), ACT.Copy)
                        ac[s].mark(last, "v")
                    for b in range(GB):
                        for s in range(S):
                            act.wait_ge(po[s].sem, po[s].done(i, f"sub{b}"))
                            ac[s].mark(act.activation(sc[s][:], sc[s][:], ACT.Exp), f"exp{b}")
                        for s in range(S):
                            act.wait_ge(pe_[s].sem, pe_[s].done(i, f"pT{b}"))
                            ac[s].mark(act.activation(pT[s][:, 0:half, :], bank[s][2][:].rearrange("p (h q) -> p h q", q=P),
                                                      ACT.Copy), f"pT{b}")

            @block.vector
            def _(dve):
                for s in range(S):
                    dv[s].start(dve)
                ln = Chain(dve, chain)
                ln_dve(c, dve, ln, powed, False)
                dve.wait_ge(prep, 1)
                dve.tensor_copy(nds[:], bank[0][1][:, 0:1])
                ln.link(dve.tensor_copy(biasT[:], bank[0][0][:, 0:4]))
                ln.link(dve.tensor_scalar(nds[:], nds[:], -1.0, None, ALU.mult))
                dve.tensor_scalar(biasq4[:], biasT[:, 0:1], DK ** -0.5, None, ALU.mult)
                dve.wait_ge(head_made, S + 3)
                dve.tensor_copy(bv_col[:], biasT[:, 2:3]).then_inc(prep, 1)
                dve.wait_ge(prep, 3)
                dve.tensor_tensor(bo_row[:], bo_row[:], bank[0][2][0:1, 0:P], ALU.add).then_inc(prep, 1)
                with dve.Fori(0, turns) as i:
                    for s in range(S):
                        dve.wait_ge(adj_in[s], i * 16 + 16)
                        dv[s].mark(dve.tensor_copy(adj_f[s][:], adj_i[s][:]), "adj")
                        for b in range(GB):
                            last = dve.tensor_scalar(xn[s][:, b, :], xg[:, i * S + s, b, :], meang[:, i * S + s, b:b + 1],
                                                     rstdg[:, i * S + s, b:b + 1], ALU.subtract, ALU.mult)
                        dv[s].mark(last, "xn")
                    for s in range(S):
                        dve.wait_ge(dv[s].sem, dv[s].done(i, "adj"))
                        dv[s].mark(dve.tensor_scalar(pen[s][:], adj_f[s][:], 0.0, -1e9, ALU.is_le, ALU.mult), "pen")
                        dve.wait_ge(dv[s].sem, dv[s].done(i, "pen"))
                        dv[s].mark(dve.scalar_tensor_tensor(pen[s][:], adj_f[s][:], nds[:], pen[s][:], ALU.mult, ALU.add), "dist")
                    for s in range(S):
                        dve.wait_ge(ac[s].sem, ac[s].done(i, "k"))
                        for h in range(HEADS):
                            last = dve.tensor_scalar(km[s][:, h, :], kT[s][:], head[:, h:h + 1], None, ALU.mult)
                        dv[s].mark(last, "km")
                    for b in range(GB):
                        for s in range(S):
                            dve.wait_ge(pe_[s].sem, pe_[s].done(i, f"s{b}"))
                            dve.wait_ge(dv[s].sem, dv[s].done(i, "dist"))
                            for k in range(2):
                                last = dve.tensor_tensor(sc[s][:, k * half:(k + 1) * half, :],
                                                         bank[s][k][:].rearrange("p (h q) -> p h q", q=P),
                                                         pen[s][:, b:b + 1, :].to_broadcast([P, half, P]), ALU.add)
                            dv[s].mark(last, f"raw{b}")
                            dve.wait_ge(dv[s].sem, dv[s].done(i, f"raw{b}"))
                            dv[s].mark(dve.tensor_reduce(mx[s][:], sc[s][:], AX_X, ALU.max), f"max{b}")
                        for s in range(S):
                            dve.wait_ge(pe_[s].sem, pe_[s].done(i, f"pT{b}"))
                            dv[s].mark(dve.tensor_copy(pT[s][:, half:HEADS, :], bank[s][3][:].rearrange("p (h q) -> p h q", q=P)),
                                       f"pT{b}")
                        for s in range(S):
                            o = bank[s][0][:, 0:HEADS * (DK + 1)].rearrange("p (h d) -> p h d", h=HEADS)
                            dve.wait_ge(pe_[s].sem, pe_[s].done(i, f"o{b}"))
                            dv[s].mark(dve.reciprocal(rd[s][:], o[:, :, DK:DK + 1]), f"rd{b}")
                            dve.wait_ge(dv[s].sem, dv[s].done(i, f"rd{b}"))
                            dv[s].mark(dve.tensor_tensor(on[s][:], o[:, :, 0:DK], rd[s][:].to_broadcast([P, HEADS, DK]),
                                                         ALU.mult), f"on{b}")
                        for s in range(S):
                            dve.wait_ge(pe_[s].sem, pe_[s].done(i, f"oT{b}"))
                            dv[s].mark(dve.tensor_copy(oT[s][:, b * P:(b + 1) * P], bank[s][0][:, 2 * P:3 * P]), f"oT{b}")
                    for s in range(S):
                        dve.wait_ge(pe_[s].sem, pe_[s].done(i, "y"))
                        dv[s].mark(dve.tensor_tensor(xg[:, i * S + s, :, :], xg[:, i * S + s, :, :],
                                                     bank[s][0][:].rearrange("p (b f) -> p b f", b=GB), ALU.add), "x")
                        dve.wait_ge(dv[s].sem, dv[s].done(i, "x"))
                        for b in range(GB):
                            dve.bn_stats(sg[:, i * S + s, b, :], xg[:, i * S + s, b, :])

            @block.tensor
            def _(pe):
                for s in range(S):
                    pe_[s].start(pe)
                pe.wait_ge(loaded, 160)
                pe.transpose(bank[0][0][:, 0:4], bias_rows[:], c.ident[0:4, 0:4])
                pe.matmul(bank[0][1][:, 0:1], c.ones[0:1, :], ds[:], start=True, stop=True).then_inc(prep, 1)
                pe.wait_ge(prep, 2)
                pe.matmul(bank[0][2][0:1, 0:P], bv_col[:], w["o"][:], start=True, stop=True).then_inc(prep, 1)
                pe.wait_ge(prep, 4)
                with pe.Fori(0, turns) as i:
                    for s in range(S):
                        pe.wait_ge(dv[s].sem, dv[s].done(i, "xn"))
                        for b in range(GB):
                            last = pe.transpose(bank[s][0][:, b * P:(b + 1) * P], xn[s][:, b, :], c.ident[:])
                        pe_[s].mark(last, "xT")
                    for s in range(S):
                        pe.wait_ge(ac[s].sem, ac[s].done(i, "xT"))
                        pe.matmul(bank[s][1][:], w["q"][:], xT[s][:], start=True, stop=True)
                        pe.matmul(bank[s][2][:], w["k"][:], xT[s][:], start=True, stop=True)
                        for b in range(GB):
                            last = pe.matmul(bank[s][3][:, b * P:(b + 1) * P], xT[s][:, b * P:(b + 1) * P], w["v"][:],
                                             start=True, stop=True)
                        pe_[s].mark(last, "qkv")
                    for b in range(GB):
                        for s in range(S):
                            if b == 0:
                                pe.wait_ge(ac[s].sem, ac[s].done(i, "v"))
                                pe.wait_ge(dv[s].sem, dv[s].done(i, "km"))
                            else:
                                pe.wait_ge(dv[s].sem, dv[s].done(i, f"oT{b - 1}"))
                            for k in range(2):
                                last = pe.matmul(bank[s][k][:], qT[s][:, b * P:(b + 1) * P],
                                                 km[s][:, k * half:(k + 1) * half, b * P:(b + 1) * P], start=True, stop=True)
                            pe_[s].mark(last, f"s{b}")
                        for s in range(S):
                            pe.wait_ge(ac[s].sem, ac[s].done(i, f"exp{b}"))
                            for h in range(HEADS):
                                last = pe.transpose(bank[s][2 + h // half][:, h % half * P:(h % half + 1) * P], sc[s][:, h, :],
                                                    c.ident[:])
                            pe_[s].mark(last, f"pT{b}")
                        for s in range(S):
                            pe.wait_ge(ac[s].sem, ac[s].done(i, f"pT{b}"))
                            pe.wait_ge(dv[s].sem, dv[s].done(i, f"pT{b}"))
                            for h in range(HEADS):
                                last = pe.matmul(bank[s][0][:, h * (DK + 1):(h + 1) * (DK + 1)], pT[s][:, h, :],
                                                 va[s][:, b, h, :], start=True, stop=True)
                            pe_[s].mark(last, f"o{b}")
                        for s in range(S):
                            pe.wait_ge(dv[s].sem, dv[s].done(i, f"on{b}"))
                            pe_[s].mark(pe.transpose(bank[s][0][:, 2 * P:3 * P], on[s][:].rearrange("p h d -> p (h d)"),
                                                     c.ident[:]), f"oT{b}")
                    for s in range(S):
                        pe.wait_ge(dv[s].sem, dv[s].done(i, f"oT{GB - 1}"))
                        for b in range(GB):
                            y = bank[s][0][:, b * P:(b + 1) * P]
                            pe.matmul(y, c.ones[0:1, :], bo_row[:], start=True, stop=False)
                            last = pe.matmul(y, oT[s][:, b * P:(b + 1) * P], w["o"][:], start=False, stop=True)
                        pe_[s].mark(last, "y")


def mean_messages(c):
    nc, io, turns = c.nc, c.io, c.turns
    xg, sg = c.grouped(c.x), c.grouped(c.stats)
    meang, rstdg = c.grouped(c.mean), c.grouped(c.rstd)
    adjg = io["adj"].rearrange("(g b) i j -> g i b j", b=GB)
    with ExitStack() as ctx:
        sb = lambda name, shape, dt=F32: c.sb("mm_" + name, shape, dt, ctx)
        wm, wu, bias = sb("wm", [P, P]), sb("wu", [P, P]), sb("bias", [1, P])
        adj_i = [sb(f"adj_i{s}", [P, GB, P], I32) for s in range(S)]
        adj_f = [sb(f"adj_f{s}", [P, GB, P]) for s in range(S)]
        xn = [sb(f"xn{s}", [P, GB, P]) for s in range(S)]
        xT = [sb(f"xT{s}", [P, T]) for s in range(S)]
        ha = [sb(f"ha{s}", [P, GB, P + 1]) for s in range(S)]
        up = [sb(f"up{s}", [P, GB, P]) for s in range(S)]
        deg = [sb(f"deg{s}", [P, GB]) for s in range(S)]
        rdeg = [sb(f"rdeg{s}", [P, GB]) for s in range(S)]
        bank = [[c.ps(f"mm_bank{s}{k}", ctx) for k in range(4)] for s in range(S)]
        loaded, chain, powed, ones = (c.sem("mm_" + n) for n in ("loaded", "chain", "powed", "ones"))
        adj_in = [c.sem(f"mm_adj_in{s}") for s in range(S)]
        dv = [Steps(c.sem(f"mm_dve{s}"), "adj xn deg rdeg pos scale sum x") for s in range(S)]
        ac = [Steps(c.sem(f"mm_act{s}"), "xT h up") for s in range(S)]
        pe_ = [Steps(c.sem(f"mm_pe{s}"), "xT h msg") for s in range(S)]
        with nc.Block() as block:

            @block.sync
            def _(sp):
                sp.dma_start(wm[:], io["L2_gnn_W_msg"]).then_inc(loaded, 16)
                sp.dma_start(wu[:], io["L2_gnn_W_upd"]).then_inc(loaded, 16)
                sp.dma_start(bias[:], io["L2_gnn_bias"].rearrange("(o d) -> o d", o=1)).then_inc(loaded, 16)
                with sp.Fori(0, turns) as i:
                    for s in range(S):
                        sp.wait_ge(dv[s].sem, dv[s].all_done(i))
                        sp.dma_start(adj_i[s][:], adjg[i * S + s]).then_inc(adj_in[s], 16)

            @block.gpsimd
            def _(pool):
                for s in range(S):
                    pool.memset(ha[s][:], 1.0).then_inc(ones, 1)
                ln_pool(c, pool, powed, False)

            @block.scalar
            def _(act):
                for s in range(S):
                    ac[s].start(act)
                act.wait_ge(ones, S)
                with act.Fori(0, turns) as i:
                    for s in range(S):
                        act.wait_ge(pe_[s].sem, pe_[s].done(i, "xT"))
                        ac[s].mark(act.activation(xT[s][:], bank[s][0][:], ACT.Copy), "xT")
                    for s in range(S):
                        act.wait_ge(pe_[s].sem, pe_[s].done(i, "h"))
                        wide = "p (b f) -> p b f"
                        ac[s].mark(act.activation(ha[s][:, :, 0:P], bank[s][1][:].rearrange(wide, b=GB), ACT.Copy), "h")
                        ac[s].mark(act.activation(up[s][:], bank[s][0][:].rearrange(wide, b=GB), ACT.Copy), "up")

            @block.vector
            def _(dve):
                for s in range(S):
                    dv[s].start(dve)
                ln_dve(c, dve, Chain(dve, chain), powed, False)
                with dve.Fori(0, turns) as i:
                    for s in range(S):
                        dve.wait_ge(adj_in[s], i * 16 + 16)
                        dv[s].mark(dve.tensor_copy(adj_f[s][:], adj_i[s][:]), "adj")
                        for b in range(GB):
                            last = dve.tensor_scalar(xn[s][:, b, :], xg[:, i * S + s, b, :], meang[:, i * S + s, b:b + 1],
                                                     rstdg[:, i * S + s, b:b + 1], ALU.subtract, ALU.mult)
                        dv[s].mark(last, "xn")
                    for s in range(S):
                        msg = lambda b: bank[s][2 + b // 2][:, b % 2 * (P + 1):(b % 2 + 1) * (P + 1)]
                        dve.wait_ge(pe_[s].sem, pe_[s].done(i, "msg"))
                        for b in range(GB):
                            last = dve.tensor_copy(deg[s][:, b:b + 1], msg(b)[:, P:P + 1])
                        dv[s].mark(last, "deg")
                        dve.wait_ge(dv[s].sem, dv[s].done(i, "deg"))
                        dv[s].mark(dve.tensor_scalar(rdeg[s][:], deg[s][:], 1.0, None, ALU.max), "rdeg")
                        dve.wait_ge(dv[s].sem, dv[s].done(i, "rdeg"))
                        dve.reciprocal(rdeg[s][:], rdeg[s][:])
                        dv[s].mark(dve.tensor_scalar(deg[s][:], deg[s][:], 0.0, None, ALU.is_gt), "pos")
                        dve.wait_ge(dv[s].sem, dv[s].done(i, "pos"))
                        dv[s].mark(dve.tensor_tensor(rdeg[s][:], rdeg[s][:], deg[s][:], ALU.mult), "scale")
                        dve.wait_ge(ac[s].sem, ac[s].done(i, "up"))
                        dve.wait_ge(dv[s].sem, dv[s].done(i, "scale"))
                        for b in range(GB):
                            last = dve.scalar_tensor_tensor(up[s][:, b, :], msg(b)[:, 0:P], rdeg[s][:, b:b + 1], up[s][:, b, :],
                                                            ALU.mult, ALU.add)
                        dv[s].mark(last, "sum")
                        dve.wait_ge(dv[s].sem, dv[s].done(i, "sum"))
                        dv[s].mark(dve.scalar_tensor_tensor(xg[:, i * S + s, :, :], up[s][:], 0.0, xg[:, i * S + s, :, :],
                                                            ALU.max, ALU.add), "x")
                        dve.wait_ge(dv[s].sem, dv[s].done(i, "x"))
                        for b in range(GB):
                            dve.bn_stats(sg[:, i * S + s, b, :], xg[:, i * S + s, b, :])

            @block.tensor
            def _(pe):
                for s in range(S):
                    pe_[s].start(pe)
                pe.wait_ge(loaded, 48)
                with pe.Fori(0, turns) as i:
                    for s in range(S):
                        pe.wait_ge(dv[s].sem, dv[s].done(i, "xn"))
                        for b in range(GB):
                            last = pe.transpose(bank[s][0][:, b * P:(b + 1) * P], xn[s][:, b, :], c.ident[:])
                        pe_[s].mark(last, "xT")
                    for s in range(S):
                        pe.wait_ge(ac[s].sem, ac[s].done(i, "xT"))
                        for b in range(GB):
                            at = slice(b * P, (b + 1) * P)
                            pe.matmul(bank[s][1][:, at], xT[s][:, at], wm[:], start=True, stop=True)
                            pe.matmul(bank[s][0][:, at], c.ones[0:1, :], bias[:], start=True, stop=False)
                            last = pe.matmul(bank[s][0][:, at], xT[s][:, at], wu[:], start=False, stop=True)
                        pe_[s].mark(last, "h")
                    for s in range(S):
                        pe.wait_ge(ac[s].sem, ac[s].done(i, "h"))
                        for b in range(GB):
                            last = pe.matmul(bank[s][2 + b // 2][:, b % 2 * (P + 1):(b % 2 + 1) * (P + 1)], adj_f[s][:, b, :],
                                             ha[s][:, b, :], start=True, stop=True)
                        pe_[s].mark(last, "msg")


def edge_gates(c):
    nc, io, turns = c.nc, c.io, c.turns
    xg, sg = c.grouped(c.x), c.grouped(c.stats)
    meang, rstdg = c.grouped(c.mean), c.grouped(c.rstd)
    adjg = io["adj"].rearrange("(g b) i j -> g i b j", b=GB)
    K = 4
    with ExitStack() as ctx:
        sb = lambda name, shape, dt=F32: c.sb("eg_" + name, shape, dt, ctx)
        a, bias = sb("a", [P, K]), sb("bias", [1, P])
        adj_i = [sb(f"adj_i{s}", [P, GB, P], I32) for s in range(S)]
        adj_f = [sb(f"adj_f{s}", [P, GB, P]) for s in range(S)]
        xn = [sb(f"xn{s}", [P, GB, P]) for s in range(S)]
        xT = [sb(f"xT{s}", [P, T]) for s in range(S)]
        ax = [sb(f"ax{s}", [P, K, T]) for s in range(S)]
        adjT = [sb(f"adjT{s}", [P, GB, P]) for s in range(S)]
        kind = [sb(f"kind{s}", [P, K, GB, P], I32) for s in range(S)]
        known = [sb(f"known{s}", [P, GB, P]) for s in range(S)]
        e = [sb(f"e{s}", [P, GB, P]) for s in range(S)]
        bank = [c.ps(f"eg_bank{s}", ctx, (P, 4, T)) for s in range(S)]
        loaded, chain, powed = (c.sem("eg_" + n) for n in ("loaded", "chain", "powed"))
        adj_in = [c.sem(f"eg_adj_in{s}") for s in range(S)]
        dv = [Steps(c.sem(f"eg_dve{s}"), "adj xn known kinds mask ax first pick1 pick2 pick3 leaky alpha x") for s in range(S)]
        ac = [Steps(c.sem(f"eg_act{s}"), "xT adjT sigmoid") for s in range(S)]
        pe_ = [Steps(c.sem(f"eg_pe{s}"), "xT adjT e out") for s in range(S)]
        wide = "p (b f) -> p b f"
        with nc.Block() as block:

            @block.sync
            def _(sp):
                for k in range(K):
                    sp.dma_start(a[:, k:k + 1], io[f"L3_gnn_a{k}"], allow_slow_non_contiguous=True).then_inc(loaded, 16)
                sp.dma_start(bias[:], io["L3_gnn_bias"].rearrange("(o d) -> o d", o=1)).then_inc(loaded, 16)
                with sp.Fori(0, turns) as i:
                    for s in range(S):
                        sp.wait_ge(dv[s].sem, dv[s].all_done(i))
                        sp.dma_start(adj_i[s][:], adjg[i * S + s]).then_inc(adj_in[s], 16)

            @block.gpsimd
            def _(pool):
                ln_pool(c, pool, powed, False)

            @block.scalar
            def _(act):
                for s in range(S):
                    ac[s].start(act)
                with act.Fori(0, turns) as i:
                    for s in range(S):
                        act.wait_ge(pe_[s].sem, pe_[s].done(i, "xT"))
                        ac[s].mark(act.activation(xT[s][:], bank[s][:, 0, :], ACT.Copy), "xT")
                        act.wait_ge(pe_[s].sem, pe_[s].done(i, "adjT"))
                        ac[s].mark(act.activation(adjT[s][:], bank[s][:, 1, :].rearrange(wide, b=GB), ACT.Copy), "adjT")
                    for s in range(S):
                        act.wait_ge(dv[s].sem, dv[s].done(i, "leaky"))
                        ac[s].mark(act.activation(e[s][:], e[s][:], ACT.Sigmoid), "sigmoid")

            @block.vector
            def _(dve):
                for s in range(S):
                    dv[s].start(dve)
                ln_dve(c, dve, Chain(dve, chain), powed, False)
                dve.wait_ge(loaded, 80)
                with dve.Fori(0, turns) as i:
                    for s in range(S):
                        dve.wait_ge(adj_in[s], i * 16 + 16)
                        dv[s].mark(dve.tensor_copy(adj_f[s][:], adj_i[s][:]), "adj")
                        for b in range(GB):
                            last = dve.tensor_scalar(xn[s][:, b, :], xg[:, i * S + s, b, :], meang[:, i * S + s, b:b + 1],
                                                     rstdg[:, i * S + s, b:b + 1], ALU.subtract, ALU.mult)
                        dv[s].mark(last, "xn")
                    for s in range(S):
                        dve.wait_ge(ac[s].sem, ac[s].done(i, "adjT"))
                        dv[s].mark(dve.tensor_scalar(known[s][:], adjT[s][:], 1.0, None, ALU.is_ge), "known")
                        for k in range(1, K):
                            last = dve.tensor_scalar(kind[s][:, k, :, :], adjT[s][:], float(k + 1), None, ALU.is_equal)
                        dv[s].mark(last, "kinds")
                        dve.wait_ge(dv[s].sem, dv[s].done(i, "known"))
                        dv[s].mark(dve.scalar_tensor_tensor(known[s][:], adjT[s][:], float(K), known[s][:], ALU.is_le, ALU.mult),
                                   "mask")
                        for k in range(K):
                            last = dve.tensor_scalar(ax[s][:, k, :], xT[s][:], a[:, k:k + 1], None, ALU.mult)
                        dv[s].mark(last, "ax")
                    for s in range(S):
                        dve.wait_ge(pe_[s].sem, pe_[s].done(i, "e"))
                        ek = lambda k: bank[s][:, :, k * P:(k + 1) * P]
                        dv[s].mark(dve.tensor_copy(e[s][:], ek(0)), "first")
                        for k in range(1, K):
                            dve.wait_ge(dv[s].sem, dv[s].done(i, "first" if k == 1 else f"pick{k - 1}"))
                            dve.memset(c.pace[:], 0.0)
                            dv[s].mark(dve.copy_predicated(e[s][:], kind[s][:, k, :, :], ek(k)), f"pick{k}")
                        dve.wait_ge(dv[s].sem, dv[s].done(i, f"pick{K - 1}"))
                        dv[s].mark(dve.scalar_tensor_tensor(e[s][:], e[s][:], 0.2, e[s][:], ALU.mult, ALU.max), "leaky")
                    for s in range(S):
                        dve.wait_ge(ac[s].sem, ac[s].done(i, "sigmoid"))
                        dv[s].mark(dve.tensor_tensor(e[s][:], e[s][:], known[s][:], ALU.mult), "alpha")
                    for s in range(S):
                        dve.wait_ge(pe_[s].sem, pe_[s].done(i, "out"))
                        dv[s].mark(dve.tensor_tensor(xg[:, i * S + s, :, :], xg[:, i * S + s, :, :],
                                                     bank[s][:, 0, :].rearrange(wide, b=GB), ALU.add), "x")
                        dve.wait_ge(dv[s].sem, dv[s].done(i, "x"))
                        for b in range(GB):
                            dve.bn_stats(sg[:, i * S + s, b, :], xg[:, i * S + s, b, :])

            @block.tensor
            def _(pe):
                for s in range(S):
                    pe_[s].start(pe)
                pe.wait_ge(loaded, 80)
                with pe.Fori(0, turns) as i:
                    for s in range(S):
                        pe.wait_ge(dv[s].sem, dv[s].done(i, "xn"))
                        for b in range(GB):
                            last = pe.transpose(bank[s][:, 0, b * P:(b + 1) * P], xn[s][:, b, :], c.ident[:])
                        pe_[s].mark(last, "xT")
                        for b in range(GB):
                            last = pe.transpose(bank[s][:, 1, b * P:(b + 1) * P], adj_f[s][:, b, :], c.ident[:])
                        pe_[s].mark(last, "adjT")
                    for s in range(S):
                        pe.wait_ge(dv[s].sem, dv[s].done(i, "ax"))
                        for b in range(GB):
                            at = slice(b * P, (b + 1) * P)
                            last = pe.matmul(bank[s][:, b, :], xT[s][:, at], ax[s][:, :, at], start=True, stop=True)
                        pe_[s].mark(last, "e")
                    for s in range(S):
                        pe.wait_ge(dv[s].sem, dv[s].done(i, "alpha"))
                        for b in range(GB):
                            out = bank[s][:, 0, b * P:(b + 1) * P]
                            pe.matmul(out, c.ones[0:1, :], bias[:], start=True, stop=False)
                            last = pe.matmul(out, e[s][:, b, :], xn[s][:, b, :], start=False, stop=True)
                        pe_[s].mark(last, "out")


SH = 8
SP = P // 2
CK = 4
CONV = 3
Z0, X0, B0, C0, B1, DT0, IN_COLS = 0, 512, 1024, 1088, 1152, 1216, 1232


def slices(c):
    nc, io = c.nc, c.io
    xg, sg = c.grouped(c.x), c.grouped(c.stats)
    meang, rstdg = c.grouped(c.mean), c.grouped(c.rstd)
    PAIRS = GB // 2
    W = 2 * P
    row = lambda v: v.rearrange("(o d) -> o d", o=1)
    with ExitStack() as ctx:
        sb = lambda name, shape, dt=F32: c.sb("sl_" + name, shape, dt, ctx)
        sem = lambda name: c.sem("sl_" + name)
        in_t, ho_t, ow_t, fc_t = sb("in_t", [P, CK, IN_COLS]), sb("ho_t", [P, CK, CK * P]), sb("ow_t", [P, CK, P]), sb("fc_t", [P, CK, SH])
        fx_t, wc, bc, bfx = sb("fx_t", [P, CK, P]), sb("wc", [P, SH, SP]), sb("bc", [P, SH, SP]), sb("bfx", [P, CK * P])
        cw, cb = sb("cw", [P, 6, CONV]), sb("cb", [P, 6])
        ob = sb("ob", [1, P])
        heads_all = sb("heads_all", [P, 5, SH])
        a2 = sb("a2", [P, 2, SH])
        up, low = sb("up", [P, SP]), sb("low", [P, SP])
        seg_f, seg_b = sb("seg_f", [P, P]), sb("seg_b", [P, P])
        xn, xT = sb("xn", [P, GB, P]), sb("xT", [P, T])
        sw = [sb(f"sw{b}", [P, SH, SP]) for b in range(GB)]
        fx = [sb(f"fx{b}", [P, CK * P]) for b in range(2)]
        rs = sb("rs", [P, CK])
        std = [sb(f"std{b}", [P, CK, P]) for b in range(2)]
        eye2 = sb("eye2", [P, SP])
        mx, sm = sb("mx", [P, GB, SH]), sb("sm", [P, GB, SH])
        st = [sb(f"st{u}", [P, CK, GB, SP]) for u in range(2)]
        swT = [sb(f"swT{u}", [P, GB, CK, P]) for u in range(2)]
        zs = [sb(f"zs{q}", [P, CK * P]) for q in range(PAIRS)]
        xa, xe = sb("xa", [P, 6, GB, SP]), sb("xe", [P, 6, GB, SP])
        dt, dn, de, dl, du, dc = (sb(n, [P, PAIRS, 2, SH]) for n in ("dt", "dn", "de", "dl", "du", "dc"))
        seg_rhs = [sb(f"seg_rhs{k}", [P, SH, SP]) for k in range(2)]
        dec = [sb(f"dec{q}", [P, SH, SP]) for q in range(PAIRS)]
        bcp = [sb(f"bcp{q}", [P, SP + 2]) for q in range(PAIRS)]
        gu, gd = sb("gu", [P, SP]), sb("gd", [P, SP])
        m1, m2 = sb("m1", [P, SH, SP]), sb("m2", [P, SH, SP])
        mb = [sb(f"mb{q}", [P, SH, P]) for q in range(PAIRS)]
        fcd = sb("fcd", [P, PAIRS, SH])
        xs = [sb(f"xs{q}", [P, SH, SP]) for q in range(PAIRS)]
        y = [sb(f"y{q}", [P, CK * P]) for q in range(PAIRS)]
        ms, rms = sb("ms", [P, PAIRS]), sb("rms", [P, PAIRS])
        yT = sb("yT", [P, CK, PAIRS, P])
        otb = sb("otb", [P, CK, GB, P])
        zz = [sb(f"zz{k}", [P, CK, P]) for k in range(2)]
        bank = [c.ps(f"sl_bank{k}", ctx) for k in range(8)]
        heads8 = lambda ap: ap.rearrange("p (h f) -> p h f", h=SH)

        rows_up, rows_read = sem("rows_up"), sem("rows_read")
        small_in, pre, masks, chain, powed = sem("small_in"), sem("pre"), sem("masks"), sem("chain"), sem("powed")
        with ExitStack() as ctx2:
            sb2 = lambda name, shape, dt=F32: c.sb("sw_" + name, shape, dt, ctx2)
            rows = [sb2(f"rows{k}", [P, CK * P]) for k in range(2)]
            rows_in = [sem(f"rows_in{k}") for k in range(2)]
            vec_rows, vecs = sb2("vec_rows", [2 * CK, P]), sb2("vecs", [P, 2 * CK])
            ws2, wsT = sb2("ws2", [SP, 2, SP]), sb2("wsT", [P, SP])
            wx = sb2("wx", [P, CK, P])
            heads_row = sb2("heads_row", [1, 5, SH])
            bfx_row, bs_row, bs_all = sb2("bfx_row", [1, CK * P]), sb2("bs_row", [1, SP]), sb2("bs_all", [P, SP])
            bx_wide = sb2("bx_wide", [P, CK, P])
            cols = [(io["L2_ffn_hy_in_w"][128 * k:128 * k + 128, :], P, in_t[:, :, 128 * k:128 * k + 128]) for k in range(9)]
            cols += [(io["L2_ffn_hy_in_w"][1152:1168, :], 16, in_t[:, :, DT0:DT0 + 16]),
                     (io["L2_ffn_hy_in_w"][B0:C0, :], SP, in_t[:, :, B1:B1 + SP])]
            cols += [(io["L2_ffn_hy_out_w"][128 * k:128 * k + 128, :], P, ho_t[:, :, 128 * k:128 * k + 128]) for k in range(4)]
            cols += [(io["L2_ffn_out_w"], P, ow_t[:]), (io["L2_ffn_hy_fcD_w"], SH, fc_t[:]),
                     (io["L2_ffn_W_fx"].rearrange("(j p) d -> p j d", p=P), P, fx_t[:])]
            conv_w, conv_b = io["L2_ffn_hy_conv_w"], io["L2_ffn_hy_conv_b"].rearrange("(c o) -> c o", o=1)
            smalls = [(vec_rows[0:CK, :], io["L2_ffn_hy_norm_w"].rearrange("(k p) -> k p", p=P)),
                      (vec_rows[CK:2 * CK, :], io["L2_ffn_b_x"].rearrange("(k p) -> k p", p=P)),
                      (ws2[:, 0, :], io["L2_ffn_W_slice"]), (ws2[:, 1, :], io["L2_ffn_W_slice"]),
                      (wx[:], io["L2_ffn_W_x"].rearrange("(j p) d -> p j d", p=P)),
                      (heads_row[:, 0, :], io["L2_ffn_temperature"].rearrange("a h b c -> a (h b c)")),
                      (heads_row[:, 1, :], row(io["L2_ffn_hy_D"])), (heads_row[:, 2, :], row(io["L2_ffn_hy_dt_bias"])),
                      (heads_row[:, 3, :], row(io["L2_ffn_hy_dt_bias"])), (heads_row[:, 4, :], row(io["L2_ffn_hy_A_log"])),
                      (bfx_row[:], row(io["L2_ffn_b_fx"])), (bs_row[:], row(io["L2_ffn_b_slice"])),
                      (ob[:], row(io["L2_ffn_out_b"]))]
            for j in range(4):
                smalls += [(cw[:, j, :], conv_w[128 * j:128 * j + 128, :]), (cb[:, j:j + 1], conv_b[128 * j:128 * j + 128, :])]
            for p0, j, ch0 in ((0, 4, 512), (SP, 4, 576), (0, 5, 576), (SP, 5, 512)):
                smalls += [(cw[p0:p0 + SP, j, :], conv_w[ch0:ch0 + SP, :]), (cb[p0:p0 + SP, j:j + 1], conv_b[ch0:ch0 + SP, :])]
            with nc.Block() as block:

                @block.sync
                def _(sp):
                    for dst, src in smalls:
                        sp.dma_start(dst, src, allow_slow_non_contiguous=True).then_inc(small_in, 16)
                    for k, (src, n, _) in enumerate(cols):
                        if k >= 2:
                            sp.wait_ge(rows_up, k - 1)
                        dst = rows[k % 2][0:n, :]
                        if len(src.shape) == 3:
                            dst = dst.rearrange("p (j d) -> p j d", d=P)
                        sp.dma_start(dst, src).then_inc(rows_in[k % 2], 16)

                @block.gpsimd
                def _(pool):
                    link = Chain(pool, masks).link
                    pool.memset(up[:], 1.0)
                    pool.memset(low[:], 1.0)
                    pool.memset(seg_f[:], 0.0)
                    pool.memset(seg_b[:], 0.0)
                    for q in range(PAIRS):
                        pool.memset(mb[q][:], 0.0)
                        pool.memset(bcp[q][:], 0.0)
                    for b in range(2):
                        pool.memset(std[b][:], 0.0)
                    link(pool.memset(otb[:], 0.0))
                    for r in range(2):
                        half = slice(SP * r, SP * r + SP)
                        link(pool.affine_select(out=up[half, :], in_=up[half, :], compare_op=ALU.is_gt, fill=0.0, base=0,
                                                pattern=[[1, SP]], channel_multiplier=-1))
                        link(pool.affine_select(out=low[half, :], in_=low[half, :], compare_op=ALU.is_gt, fill=0.0, base=0,
                                                pattern=[[-1, SP]], channel_multiplier=1))
                    for r in range(2):
                        half = slice(SP * r, SP * r + SP)
                        link(pool.tensor_copy(seg_f[half, half], low[half, :]))
                        link(pool.tensor_copy(seg_b[half, half], up[half, :]))
                        link(pool.tensor_copy(eye2[half, :], c.ident[half, half]))
                    ln_pool(c, pool, powed, False)

                @block.scalar
                def _(act):
                    for k, (_, n, dst) in enumerate(cols):
                        act.wait_ge(rows_up, k + 1)
                        act.activation(dst, bank[k % 2][:].rearrange("p (j n) -> p j n", j=CK)[:, :, 0:n], ACT.Copy).then_inc(rows_read, 1)
                    act.wait_ge(pre, 4)
                    for k in range(2):
                        act.activation(a2[:, k, :], heads_all[:, 4, :], ACT.Exp)

                @block.vector
                def _(dve):
                    link = Chain(dve, chain)
                    ln_dve(c, dve, link, powed, False)
                    link = link.link
                    dve.wait_ge(small_in, 16 * len(smalls))
                    link(dve.tensor_scalar(heads_row[:, 0, :], heads_row[:, 0, :], 1e-6, None, ALU.max))
                    dve.reciprocal(heads_row[:, 0, :], heads_row[:, 0, :]).then_inc(pre, 1)
                    dve.wait_ge(pre, 2)
                    dve.tensor_copy(vecs[:], bank[2][:, 0:2 * CK])
                    dve.tensor_copy(wsT[:], bank[3][:, 0:SP])
                    dve.tensor_copy(heads_all[:].rearrange("p k h -> p (k h)"), bank[4][:, 0:5 * SH])
                    dve.tensor_copy(bfx[:], bank[5][:])
                    link(dve.tensor_copy(bs_all[:], bank[6][:, 0:SP]))
                    for k in range(CK):
                        dve.tensor_scalar(bx_wide[:, k, :], c.ones[:], vecs[:, CK + k:CK + k + 1], None, ALU.mult)
                    dve.drain().then_inc(pre, 2)
                    dve.wait_ge(pre, 5)
                    for r in range(2):
                        for n, dst in ((2, wc), (4, bc)):
                            half = dst[:].rearrange("p (k r) g -> p r k g", r=2)[:, r, :, :]
                            temp = heads_all[:, 0, :].rearrange("p (k r) -> p r k", r=2)[:, r, :].unsqueeze(2).to_broadcast([P, CK, SP])
                            src = bank[n + r][:, 0:CK * SP].rearrange("p (k g) -> p k g", k=CK)
                            if dst is bc:
                                link(dve.tensor_tensor(half, src, bs_all[:].unsqueeze(1).to_broadcast([P, CK, SP]), ALU.add))
                                src = half
                            link(dve.tensor_tensor(half, src, temp, ALU.mult))
                    dve.wait_ge(rows_read, len(cols))
                    for k in range(CK):
                        dve.tensor_scalar(ho_t[:, k, :], ho_t[:, k, :], vecs[:, k:k + 1], None, ALU.mult)

                @block.tensor
                def _(pe):
                    pe.wait_ge(small_in, 16 * len(smalls))
                    pe.wait_ge(pre, 1)
                    pe.transpose(bank[2][:, 0:2 * CK], vec_rows[:], c.ident[0:2 * CK, 0:2 * CK])
                    pe.transpose(bank[3][:, 0:SP], ws2[:].rearrange("g r c -> g (r c)"), c.ident[0:SP, 0:SP])
                    pe.matmul(bank[4][:, 0:5 * SH], c.ones[0:1, :], heads_row[:].rearrange("p k h -> p (k h)"), start=True, stop=True)
                    pe.matmul(bank[5][:], c.ones[0:1, :], bfx_row[:], start=True, stop=True)
                    pe.matmul(bank[6][:, 0:SP], c.ones[0:1, :], bs_row[:], start=True, stop=True).then_inc(pre, 1)
                    pe.wait_ge(pre, 4)
                    for r in range(2):
                        half = slice(SP * r, SP * r + SP)
                        for k in range(CK):
                            at = slice(SP * k, SP * k + SP)
                            pe.matmul(bank[2 + r][:, at], wx[half, k, :], wsT[half, :], start=True, stop=True)
                            last = pe.matmul(bank[4 + r][:, at], bx_wide[half, k, :], wsT[half, :], start=True, stop=True)
                    last.then_inc(pre, 1)
                    for k, (_, n, _) in enumerate(cols):
                        pe.wait_ge(rows_in[k % 2], 16 * (k // 2 + 1))
                        if k >= 2:
                            pe.wait_ge(rows_read, k - 1)
                        for j in range(CK):
                            last = pe.transpose(bank[k % 2][:, j * P:j * P + n], rows[k % 2][0:n, j * P:(j + 1) * P], c.ident[0:n, 0:n])
                        last.then_inc(rows_up, 1)

        per = lambda names, n: " ".join(f"{k}{b}" for b in range(n) for k in names.split())
        two = lambda names: " ".join(f"{k}{b}" for k in names.split() for b in range(GB))
        av = Steps(sem("a_dve"), "xn " + two("logit max") + " " + two("sum") + " rsum " + per("fx norm rnorm st", GB))
        aa = Steps(sem("a_act"), "xT " + two("exp") + " " + per("swT st", GB))
        ap = Steps(sem("a_pe"), "xT " + two("logit") + " " + per("swT fx st stT", GB))
        ag = Steps(sem("a_pool"), two("sub") + " " + two("sw"))
        bv = Steps(sem("b_dve"), "zs0 zs1 tap1 tap2 tap45 x dt dneg dabs du dd dc dru dcr dsum dt2 da "
                   + "bcp0 g0 m0 mm0 bcp1 g1 m1 mm1 fcd y0 y1 yg0 yg1 mean ygn0 ygn1 ot x_out")
        ba = Steps(sem("b_act"), "z0 z1 xa xa45 xe de dl dec0 dec1 xs0 xs1 ms0 ms1 yT0 yT1 " + two("z_"))
        bp = Steps(sem("b_pe"), "z0 z1 xbc dtbc seg0 seg1 bc0 bc1 fcd xs0 xs1 y0 y1 yT0 yT1 ot z_0 z_1 out0 z_2 out1 z_3 out2 out3")
        bg = Steps(sem("b_pool"), "seg0f seg0b seg1f seg1b m20 m21 xf0 xf1 rms")

        wide = [P, SH, SP]
        over_t = lambda v: v.unsqueeze(2).to_broadcast(wide)
        over_h = lambda v: v.unsqueeze(1).to_broadcast(wide)
        pair = lambda q: slice(2 * q, 2 * q + 2)
    
        with nc.Block() as block:

            @block.scalar
            def _(act):
                aa.start(act)
                ba.start(act)
                def a1(g):
                    act.wait_ge(ap.sem, ap.done(g, "xT"))
                    aa.mark(act.activation(xT[:], bank[4][:], ACT.Copy), "xT")
                    for b in range(GB):
                        act.wait_ge(ag.sem, ag.done(g, f"sub{b}"))
                        aa.mark(act.activation(sw[b][:], sw[b][:], ACT.Exp), f"exp{b}")

                def a2_(g, u, b_turn):
                    for b in range(GB):
                        act.wait_ge(ap.sem, ap.done(g, f"swT{b}"))
                        if b == 0:
                            act.wait_ge(bv.sem, bv.all_done(b_turn))
                        aa.mark(act.activation(swT[u][:, b, :, :], bank[4][:].rearrange("p (k n) -> p k n", k=CK), ACT.Copy),
                                f"swT{b}")
                        act.wait_ge(ap.sem, ap.done(g, f"stT{b}"))
                        aa.mark(act.activation(st[u][:, :, b, :], bank[6][:, CK * SP:2 * CK * SP].rearrange("p (k g) -> p k g", k=CK),
                                               ACT.Copy), f"st{b}")

                def b1(g):
                    for q in range(PAIRS):
                        act.wait_ge(bp.sem, bp.done(g, f"z{q}"))
                        ba.mark(act.activation(zs[q][:], bank[q][:], ACT.Sigmoid), f"z{q}")
                    act.wait_ge(bp.sem, bp.done(g, "xbc"))
                    for j in range(4):
                        last = act.activation(xa[:, j, :, :], bank[2 + j // 2][:, j % 2 * W:(j % 2 + 1) * W].rearrange("p (b t) -> p b t", b=GB),
                                              ACT.Identity, bias=cb[:, j:j + 1], scale=cw[:, j, 2:3])
                    ba.mark(last, "xa")
                    act.wait_ge(bp.sem, bp.done(g, "dtbc"))
                    for j in range(4, 6):
                        last = act.activation(xa[:, j, :, :], bank[0][:, j % 2 * W:(j % 2 + 1) * W].rearrange("p (b t) -> p b t", b=GB),
                                              ACT.Identity, bias=cb[:, j:j + 1], scale=cw[:, j, 2:3])
                    ba.mark(last, "xa45")
                    act.wait_ge(bv.sem, bv.done(g, "tap45"))
                    ba.mark(act.activation(xe[:], xa[:], ACT.Sigmoid), "xe")
                    act.wait_ge(bv.sem, bv.done(g, "dabs"))
                    ba.mark(act.activation(de[:], dn[:], ACT.Exp, scale=-1.0), "de")
                    act.wait_ge(bv.sem, bv.done(g, "du"))
                    ba.mark(act.activation(dl[:], du[:], ACT.Ln), "dl")

                def b2(g):
                    for q in range(PAIRS):
                        act.wait_ge(bp.sem, bp.done(g, f"seg{q}"))
                        ba.mark(act.activation(dec[q][:], heads8(bank[2 + q][:]), ACT.Exp, scale=-1.0), f"dec{q}")
                    for q in range(PAIRS):
                        act.wait_ge(bp.sem, bp.done(g, f"xs{q}"))
                        ba.mark(act.activation(xs[q][:], heads8(bank[2 + q][:]), ACT.Copy), f"xs{q}")
                    for q in range(PAIRS):
                        act.wait_ge(bv.sem, bv.done(g, f"yg{q}"))
                        ba.mark(act.activation(zs[q][:], y[q][:], ACT.Square, accum_out=ms[:, q:q + 1]), f"ms{q}")

                def b3(g):
                    for q in range(PAIRS):
                        act.wait_ge(bp.sem, bp.done(g, f"yT{q}"))
                        ba.mark(act.activation(yT[:, :, q, :], bank[2 + q][:].rearrange("p (k n) -> p k n", k=CK), ACT.Copy), f"yT{q}")
                    for b in range(GB):
                        act.wait_ge(bp.sem, bp.done(g, f"z_{b}"))
                        if b >= 2:
                            act.wait_ge(bp.sem, bp.done(g, f"out{b - 2}"))
                        ba.mark(act.activation(zz[b % 2][:], bank[2 + b % 2][:].rearrange("p (k n) -> p k n", k=CK), ACT.Copy),
                                f"z_{b}")

                a1(0)
                a2_(0, 0, 0)
                with act.Fori(0, c.turns) as i:
                    for u in range(2):
                        g = i * 2 + u
                        b1(g)
                        a1(g + 1)
                        b2(g)
                        a2_(g + 1, 1 - u, g)
                        b3(g)

            @block.gpsimd
            def _(pool):
                ag.start(pool)
                bg.start(pool)
                def a1(g):
                    for b in range(GB):
                        pool.wait_ge(av.sem, av.done(g, f"max{b}"))
                        ag.mark(pool.tensor_tensor(sw[b][:], sw[b][:], over_t(mx[:, b, :]), ALU.subtract), f"sub{b}")
                    for b in range(GB):
                        pool.wait_ge(av.sem, av.done(g, "rsum"))
                        ag.mark(pool.tensor_tensor(sw[b][:], sw[b][:], over_t(sm[:, b, :]), ALU.mult), f"sw{b}")

                def b2(g):
                    pool.wait_ge(bv.sem, bv.done(g, "da"))
                    for q in range(PAIRS):
                        if q:
                            pool.wait_ge(bp.sem, bp.done(g, f"seg{q - 1}"))
                        bg.mark(pool.tensor_tensor(seg_rhs[0][:], over_t(dn[:, q, 0, :]), over_h(up[:]), ALU.mult), f"seg{q}f")
                        bg.mark(pool.tensor_tensor(seg_rhs[1][:], over_t(dn[:, q, 1, :]), over_h(low[:]), ALU.mult), f"seg{q}b")
                    for q in range(PAIRS):
                        pool.wait_ge(bv.sem, bv.done(g, f"g{q}"))
                        bg.mark(pool.tensor_tensor(m2[:], over_t(dt[:, q, 1, :]), over_h(gd[:]), ALU.mult), f"m2{q}")
                    for q in range(PAIRS):
                        pool.wait_ge(bv.sem, bv.done(g, "fcd"))
                        pool.wait_ge(ba.sem, ba.done(g, f"xs{q}"))
                        bg.mark(pool.tensor_tensor(heads8(y[q][:]), xs[q][:], over_t(fcd[:, q, :]), ALU.mult), f"xf{q}")
                    pool.wait_ge(bv.sem, bv.done(g, "mean"))
                    bg.mark(pool.tensor_tensor(rms[:], ms[:], c.mhalf[:, 0:PAIRS], ALU.pow), "rms")

                a1(0)
                with pool.Fori(0, c.turns) as i:
                    for u in range(2):
                        g = i * 2 + u
                        a1(g + 1)
                        b2(g)

            @block.vector
            def _(dve):
                av.start(dve)
                bv.start(dve)
                def own(steps, g, name):
                    dve.wait_ge(steps.sem, steps.done(g, name))

                def a1(g):
                    dve.wait_ge(ap.sem, ap.all_done(g))
                    for b in range(GB):
                        last = dve.tensor_scalar(xn[:, b, :], xg[:, g, b, :], meang[:, g, b:b + 1], rstdg[:, g, b:b + 1],
                                                 ALU.subtract, ALU.mult)
                    av.mark(last, "xn")
                    for b in range(GB):
                        dve.wait_ge(ap.sem, ap.done(g, f"logit{b}"))
                        av.mark(dve.tensor_tensor(sw[b][:], heads8(bank[4 + b][:]), bc[:], ALU.add), f"logit{b}")
                    for b in range(GB):
                        own(av, g, f"logit{b}")
                        av.mark(dve.tensor_reduce(mx[:, b, :], sw[b][:], AX_X, ALU.max), f"max{b}")
                    for b in range(GB):
                        dve.wait_ge(aa.sem, aa.done(g, f"exp{b}"))
                        av.mark(dve.tensor_reduce(sm[:, b, :], sw[b][:], AX_X, ALU.add), f"sum{b}")
                    own(av, g, f"sum{GB - 1}")
                    av.mark(dve.reciprocal(sm[:], sm[:]), "rsum")

                def a2_(g):
                    for b in range(GB):
                        dve.wait_ge(ap.sem, ap.done(g, f"fx{b}"))
                        av.mark(dve.tensor_tensor(fx[b % 2][:], bank[5][:], bfx[:], ALU.add), f"fx{b}")
                        dve.wait_ge(ap.sem, ap.done(g, f"st{b}"))
                        av.mark(dve.tensor_scalar(rs[:], bank[6][:, 0:CK], 1e-5, None, ALU.add), f"norm{b}")
                        own(av, g, f"norm{b}")
                        av.mark(dve.reciprocal(rs[:], rs[:]), f"rnorm{b}")
                        own(av, g, f"rnorm{b}")
                        for r in range(2):
                            half = slice(SP * r, SP * r + SP)
                            last = dve.tensor_tensor(std[b % 2][half, :, half],
                                                     bank[7][half, :].rearrange("p (k r g) -> p k r g", k=CK, r=2)[:, :, r, :],
                                                     rs[half, :].unsqueeze(2).to_broadcast([SP, CK, SP]), ALU.mult)
                        av.mark(last, f"st{b}")

                def b1(g):
                    for q in range(PAIRS):
                        dve.wait_ge(ba.sem, ba.done(g, f"z{q}"))
                        bv.mark(dve.tensor_tensor(zs[q][:], zs[q][:], bank[q][:], ALU.mult), f"zs{q}")
                    dve.wait_ge(ba.sem, ba.done(g, "xa"))

                    def tap(j, k):
                        src = (bank[2 + j // 2] if j < 4 else bank[0])[:, j % 2 * W:(j % 2 + 1) * W].rearrange("p (b t) -> p b t", b=GB)
                        return dve.scalar_tensor_tensor(xa[:, j, :, k:SP], src[:, :, 0:SP - k], cw[:, j, 2 - k:3 - k],
                                                        xa[:, j, :, k:SP], ALU.mult, ALU.add)

                    for j in range(4):
                        last = tap(j, 1)
                    bv.mark(last, "tap1")
                    own(bv, g, "tap1")
                    for j in range(4):
                        last = tap(j, 2)
                    bv.mark(last, "tap2")
                    dve.wait_ge(ba.sem, ba.done(g, "xa45"))
                    for j in range(4, 6):
                        tap(j, 1)
                    dve.drain()
                    for j in range(4, 6):
                        last = tap(j, 2)
                    bv.mark(last, "tap45")
                    dve.wait_ge(ba.sem, ba.done(g, "xe"))
                    bv.mark(dve.tensor_tensor(xa[:], xa[:], xe[:], ALU.mult), "x")
                    flat = lambda v: v[:].rearrange("p q k h -> p q (k h)")
                    bias = heads_all[:, 2:4, :].rearrange("p k h -> p (k h)").unsqueeze(1).to_broadcast([P, PAIRS, 2 * SH])
                    bv.mark(dve.tensor_tensor(flat(dt), bank[1][:, 0:2 * PAIRS * SH].rearrange("p (q k) -> p q k", q=PAIRS),
                                              bias, ALU.add), "dt")
                    own(bv, g, "dt")
                    bv.mark(dve.tensor_scalar(dn[:], dt[:], -1.0, None, ALU.mult), "dneg")
                    own(bv, g, "dneg")
                    bv.mark(dve.tensor_tensor(dn[:], dt[:], dn[:], ALU.max), "dabs")
                    dve.wait_ge(ba.sem, ba.done(g, "de"))
                    bv.mark(dve.tensor_scalar(du[:], de[:], 1.0, None, ALU.add), "du")
                    own(bv, g, "du")
                    bv.mark(dve.tensor_scalar(dc[:], du[:], -1.0, None, ALU.add), "dd")
                    own(bv, g, "dd")
                    bv.mark(dve.tensor_tensor(dc[:], de[:], dc[:], ALU.subtract), "dc")
                    dve.wait_ge(ba.sem, ba.done(g, "dl"))
                    bv.mark(dve.reciprocal(du[:], du[:]), "dru")
                    own(bv, g, "dru")
                    bv.mark(dve.tensor_tensor(dc[:], dc[:], du[:], ALU.mult), "dcr")
                    own(bv, g, "dcr")
                    bv.mark(dve.tensor_tensor(dc[:], dc[:], dl[:], ALU.add), "dsum")
                    own(bv, g, "dsum")
                    bv.mark(dve.scalar_tensor_tensor(dt[:], dt[:], 0.0, dc[:], ALU.max, ALU.add), "dt2")
                    own(bv, g, "dt2")
                    bv.mark(dve.tensor_tensor(dn[:], dt[:], a2[:].unsqueeze(1).to_broadcast([P, PAIRS, 2, SH]), ALU.mult), "da")

                def b2(g):
                    for q in range(PAIRS):
                        dve.wait_ge(bp.sem, bp.done(g, f"bc{PAIRS - 1}"))
                        for r in range(2):
                            half = slice(SP * r, SP * r + SP)
                            last = dve.tensor_copy(bcp[q][half, 1:SP + 1], bank[0][half, q * P + SP * r:q * P + SP * r + SP])
                        bv.mark(last, f"bcp{q}")
                        own(bv, g, f"bcp{q}")
                        if q:
                            dve.wait_ge(bg.sem, bg.done(g, f"m2{q - 1}"))
                        dve.tensor_tensor(gu[:], bcp[q][:, 0:SP], up[:], ALU.mult)
                        bv.mark(dve.tensor_tensor(gd[:], bcp[q][:, 2:SP + 2], low[:], ALU.mult), f"g{q}")
                        own(bv, g, f"g{q}")
                        dve.tensor_tensor(m1[:], over_t(dt[:, q, 0, :]), over_h(gu[:]), ALU.mult)
                        dve.drain()
                        dve.wait_ge(bg.sem, bg.done(g, f"m2{q}"))
                        bv.mark(dve.tensor_tensor(m1[:], m1[:], m2[:], ALU.add), f"m{q}")
                        own(bv, g, f"m{q}")
                        dve.wait_ge(ba.sem, ba.done(g, f"dec{q}"))
                        for r in range(2):
                            half = slice(SP * r, SP * r + SP)
                            last = dve.tensor_tensor(mb[q][half, :, half], m1[half, :, :], dec[q][half, :, :], ALU.mult)
                        bv.mark(last, f"mm{q}")
                    dve.wait_ge(bp.sem, bp.done(g, "fcd"))
                    bv.mark(dve.tensor_tensor(fcd[:], bank[1][:, 64:64 + PAIRS * SH].rearrange("p (q h) -> p q h", q=PAIRS),
                                              heads_all[:, 1:2, :].to_broadcast([P, PAIRS, SH]), ALU.add), "fcd")
                    for q in range(PAIRS):
                        dve.wait_ge(bp.sem, bp.done(g, f"y{q}"))
                        dve.wait_ge(bg.sem, bg.done(g, f"xf{q}"))
                        bv.mark(dve.tensor_tensor(y[q][:], y[q][:], bank[q][:], ALU.add), f"y{q}")
                    for q in range(PAIRS):
                        own(bv, g, f"y{q}")
                        bv.mark(dve.tensor_tensor(y[q][:], y[q][:], zs[q][:], ALU.mult), f"yg{q}")
                    dve.wait_ge(ba.sem, ba.done(g, f"ms{PAIRS - 1}"))
                    bv.mark(dve.tensor_scalar(ms[:], ms[:], 1.0 / (CK * P), EPS, ALU.mult, ALU.add), "mean")
                    dve.wait_ge(bg.sem, bg.done(g, "rms"))
                    for q in range(PAIRS):
                        bv.mark(dve.tensor_scalar(y[q][:], y[q][:], rms[:, q:q + 1], None, ALU.mult), f"ygn{q}")

                def b3(g):
                    dve.wait_ge(bp.sem, bp.done(g, "ot"))
                    for j in range(0, CK, 2):
                        for r in range(2):
                            half = slice(SP * r, SP * r + SP)
                            last = dve.tensor_copy(otb[half, j:j + 2, :, half],
                                                   bank[j // 2][half, :].rearrange("p (j b t) -> p j b t", j=2, b=GB))
                    bv.mark(last, "ot")
                    dve.wait_ge(bp.sem, bp.done(g, f"out{GB - 1}"))
                    bv.mark(dve.tensor_tensor(xg[:, g, :, :], xg[:, g, :, :], bank[0][:].rearrange("p (b f) -> p b f", b=GB), ALU.add),
                            "x_out")
                    own(bv, g, "x_out")
                    for b in range(GB):
                        dve.bn_stats(sg[:, g, b, :], xg[:, g, b, :])

                a1(0)
                a2_(0)
                with dve.Fori(0, c.turns) as i:
                    for u in range(2):
                        g = i * 2 + u
                        b1(g)
                        a1(g + 1)
                        b2(g)
                        a2_(g + 1)
                        b3(g)

            @block.tensor
            def _(pe):
                ap.start(pe)
                bp.start(pe)
                def a1(g):
                    pe.wait_ge(av.sem, av.done(g, "xn"))
                    pe.wait_ge(aa.sem, aa.all_done(g))
                    for b in range(GB):
                        last = pe.transpose(bank[4][:, b * P:(b + 1) * P], xn[:, b, :], c.ident[:])
                    ap.mark(last, "xT")
                    pe.wait_ge(aa.sem, aa.done(g, "xT"))
                    for b in range(GB):
                        ap.mark(pe.matmul(bank[4 + b][:], xT[:, b * P:(b + 1) * P], wc[:].rearrange("p h g -> p (h g)"),
                                          start=True, stop=True), f"logit{b}")

                def a2_(g):
                    for b in range(GB):
                        pe.wait_ge(ag.sem, ag.done(g, f"sw{b}"))
                        if b:
                            pe.wait_ge(aa.sem, aa.done(g, f"swT{b - 1}"))
                            pe.wait_ge(av.sem, av.done(g, f"st{b - 1}"))
                            pe.wait_ge(aa.sem, aa.done(g, f"st{b - 1}"))
                        else:
                            pe.wait_ge(av.sem, av.done(g, f"logit{GB - 1}"))
                        flat = sw[b][:].rearrange("p h g -> p (h g)")
                        for k in range(CK):
                            last = pe.transpose(bank[4][:, k * P:(k + 1) * P], flat[:, k * P:(k + 1) * P], c.ident[:])
                        ap.mark(last, f"swT{b}")
                        ap.mark(pe.matmul(bank[5][:], xT[:, b * P:(b + 1) * P], fx_t[:].rearrange("p k c -> p (k c)"),
                                          start=True, stop=True), f"fx{b}")
                        pe.wait_ge(av.sem, av.done(g, f"fx{b}"))
                        for k in range(CK):
                            at = slice(k * P, (k + 1) * P)
                            pe.matmul(bank[6][:, k:k + 1], flat[:, at], c.ones[:, 0:1], start=True, stop=True)
                            last = pe.matmul(bank[7][:, at], flat[:, at], fx[b % 2][:, at], start=True, stop=True)
                        ap.mark(last, f"st{b}")
                        pe.wait_ge(av.sem, av.done(g, f"st{b}"))
                        for k in range(CK):
                            last = pe.matmul(bank[6][:, (CK + k) * SP:(CK + k + 1) * SP], std[b % 2][:, k, :], eye2[:],
                                             start=True, stop=True)
                        ap.mark(last, f"stT{b}")

                def b1(g, u):
                    pe.wait_ge(aa.sem, aa.all_done(g + 1))
                    pe.wait_ge(bv.sem, bv.all_done(g))
                    stf = st[u][:].rearrange("p k b t -> p k (b t)")
                    for q in range(PAIRS):
                        for k in range(CK):
                            last = pe.matmul(bank[q][:], stf[:, k, q * P:(q + 1) * P], in_t[:, k, Z0:Z0 + 512],
                                             start=(k == 0), stop=(k == CK - 1))
                        bp.mark(last, f"z{q}")

                    def xbc(out, j):
                        for k in range(CK):
                            last = pe.matmul(out, in_t[:, k, X0 + P * j:X0 + P * (j + 1)] if j < 5 else in_t[:, k, C0:C0 + P],
                                             stf[:, k, :], start=(k == 0), stop=(k == CK - 1))
                        return last

                    for j in range(4):
                        last = xbc(bank[2 + j // 2][:, j % 2 * W:(j % 2 + 1) * W], j)
                    bp.mark(last, "xbc")
                    pe.wait_ge(bv.sem, bv.done(g, "zs1"))
                    for q in range(PAIRS):
                        for k in range(CK):
                            pe.matmul(bank[1][:, q * 2 * SH:(q + 1) * 2 * SH], stf[:, k, q * P:(q + 1) * P],
                                      in_t[:, k, DT0:DT0 + 2 * SH], start=(k == 0), stop=(k == CK - 1))
                    for j in range(4, 6):
                        last = xbc(bank[0][:, j % 2 * W:(j % 2 + 1) * W], j)
                    bp.mark(last, "dtbc")

                def b2(g):
                    for q in range(PAIRS):
                        pe.wait_ge(bg.sem, bg.done(g, f"seg{q}b"))
                        pe.matmul(bank[2 + q][:], seg_f[:], seg_rhs[0][:].rearrange("p h t -> p (h t)"), start=True, stop=False)
                        bp.mark(pe.matmul(bank[2 + q][:], seg_b[:], seg_rhs[1][:].rearrange("p h t -> p (h t)"), start=False, stop=True),
                                f"seg{q}")
                    xaf = xa[:].rearrange("p j b t -> p j (b t)")
                    for q in range(PAIRS):
                        at = slice(q * P, (q + 1) * P)
                        bp.mark(pe.matmul(bank[0][:, at], xaf[0:SP, 4, at], xaf[0:SP, 5, at], start=True, stop=True), f"bc{q}")
                    for q in range(PAIRS):
                        for k in range(CK):
                            last = pe.matmul(bank[1][:, 64 + q * SH:64 + (q + 1) * SH], xaf[:, k, q * P:(q + 1) * P], fc_t[:, k, :],
                                             start=(k == 0), stop=(k == CK - 1))
                    bp.mark(last, "fcd")
                    for q in range(PAIRS):
                        pe.wait_ge(ba.sem, ba.done(g, f"dec{q}"))
                        for k in range(CK):
                            last = pe.transpose(bank[2 + q][:, k * P:(k + 1) * P], xaf[:, k, q * P:(q + 1) * P], c.ident[:])
                        bp.mark(last, f"xs{q}")
                    for q in range(PAIRS):
                        pe.wait_ge(bv.sem, bv.done(g, "fcd"))
                        pe.wait_ge(ba.sem, ba.done(g, f"xs{q}"))
                        for h in range(SH):
                            last = pe.matmul(bank[q][:, h * SP:(h + 1) * SP], mb[q][:, h, :], xs[q][:, h, :], start=True, stop=True)
                        bp.mark(last, f"y{q}")

                def b3(g, u):
                    for q in range(PAIRS):
                        pe.wait_ge(bv.sem, bv.done(g, f"ygn{q}"))
                        for k in range(CK):
                            last = pe.transpose(bank[2 + q][:, k * P:(k + 1) * P], y[q][:, k * P:(k + 1) * P], c.ident[:])
                        bp.mark(last, f"yT{q}")
                    pe.wait_ge(ba.sem, ba.done(g, f"yT{PAIRS - 1}"))
                    for j in range(CK):
                        for k in range(CK):
                            last = pe.matmul(bank[j // 2][:, j % 2 * W:(j % 2 + 1) * W], ho_t[:, k, j * P:(j + 1) * P],
                                             yT[:, k, :, :].rearrange("p q n -> p (q n)"), start=(k == 0), stop=(k == CK - 1))
                    bp.mark(last, "ot")
                    pe.wait_ge(bv.sem, bv.done(g, "ot"))

                    def spread(b):
                        pe.wait_ge(ba.sem, ba.done(g, f"z_{b}"))
                        out = bank[0][:, b * P:(b + 1) * P]
                        pe.matmul(out, c.ones[0:1, :], ob[:], start=True, stop=False)
                        for k in range(CK):
                            last = pe.matmul(out, swT[u][:, b, k, :], zz[b % 2][:, k, :], start=False, stop=(k == CK - 1))
                        bp.mark(last, f"out{b}")

                    for b in range(GB):
                        if b >= 2:
                            pe.wait_ge(ba.sem, ba.done(g, f"z_{b - 2}"))
                        for k in range(CK):
                            last = pe.matmul(bank[2 + b % 2][:, k * P:(k + 1) * P], otb[:, k, b, :], ow_t[:, k, :], start=True, stop=True)
                        bp.mark(last, f"z_{b}")
                        if b >= 1:
                            spread(b - 1)
                    spread(GB - 1)

                a1(0)
                a2_(0)
                with pe.Fori(0, c.turns) as i:
                    for u in range(2):
                        g = i * 2 + u
                        b1(g, u)
                        a1(g + 1)
                        b2(g)
                        a2_(g + 1)
                        b3(g, u)


def store(c):
    stored = c.sem("stored")
    n = c.nb // 4
    with c.nc.Block() as block:

        @block.sync
        def _(sp):
            for k in range(4):
                sp.dma_start(c.io["out"][k * n:(k + 1) * n].rearrange("b n d -> n b d"),
                             c.x[:, k * n:(k + 1) * n, :]).then_inc(stored, 16)
            sp.wait_ge(stored, 64)


def network(nc, io, n_batch=64, phases=None):
    with ExitStack() as ctx:
        c = Chip(nc, ctx, io, n_batch)
        load_and_constants(c)
        for phase in phases or PHASES:
            c.sems = []
            phase(c)
            nc.clear_and_free_semaphores(c.sems)
            nc.all_engine_barrier()
        c.sems = []
        store(c)


PHASES = [column_attention, l0_experts, head_attention, l1_experts, mean_messages, slices, edge_gates, l3_experts]


def kernel(**inputs):
    import numpy as _np
    import concourse.bacc as _bacc
    from concourse import mybir as _mybir
    from concourse.bass_utils import run_bass_kernel_spmd as _run

    nc = _bacc.Bacc("TRN2", target_bir_lowering=False, num_devices=1)
    arrays, io = {}, {}
    for name, value in inputs.items():
        a = _np.ascontiguousarray(value)
        if a.ndim == 0:
            a = a.reshape(1, 1)
        arrays[f"in_{name}"] = a
        io[name] = nc.dram_tensor(f"in_{name}", a.shape, _mybir.dt.from_np(a.dtype), kind="ExternalInput").ap()
    x = io["x"]
    io["out"] = nc.dram_tensor("out_x", x.shape, F32, kind="ExternalOutput").ap()
    network(nc, io, x.shape[0])
    r = _run(nc, [arrays], core_ids=[0])
    return r.results[0]["out_x"]
```

```python
from contextlib import ExitStack

import concourse.bass as bass
from concourse import mybir

ALU = mybir.AluOpType
ACT = mybir.ActivationFunctionType
F32 = mybir.dt.float32
F32R = mybir.dt.float32r
I32 = mybir.dt.int32
U32 = mybir.dt.uint32
AX_X = mybir.AxisListType.X

P = 128
GB = 4
T = GB * P
S = 2
EPS = 1e-5
E = 8


class Steps:

    def __init__(self, sem, names):
        self.sem, self.names, self.at = sem, names.split(), 0

    def start(self, engine):
        engine.sem_inc(self.sem, 1)

    def done(self, turn, name):
        return turn * len(self.names) + (self.names.index(name) + 2)

    def all_done(self, turns):
        return turns * len(self.names) + 1

    def mark(self, instruction, name):
        assert self.names[self.at % len(self.names)] == name, (name, self.names[self.at % len(self.names)])
        self.at += 1
        instruction.then_inc(self.sem, 1)


class Count:

    def __init__(self, sem, per, credit=0):
        self.sem, self.per, self.credit = sem, per, credit

    def done(self, group, k=0):
        assert k + 1 + self.credit >= 0
        return group * self.per + (k + 1 + self.credit)


class Chip:

    def __init__(self, nc, ctx, io, n_batch):
        self.nc, self.ctx, self.io, self.nb = nc, ctx, io, n_batch
        self.groups = n_batch // GB
        self.sems = []
        self.turns = self.groups // S
        pad = n_batch + 2 * GB
        self.x = self.sb("x_all", [P, pad, P])
        self.stats = self.sb("ln_stats", [P, pad, 6])
        self.mean = self.sb("ln_mean", [P, pad])
        self.rstd = self.sb("ln_rstd", [P, pad])
        self.rstd2 = self.sb("ln_rstd2", [P, pad])
        self.ratio = self.sb("ln_ratio", [P, pad])
        self.tmp = [self.sb(f"ln_tmp{k}", [P, pad]) for k in range(3)]
        self.mhalf = self.sb("minus_half", [P, pad])
        self.phalf = self.sb("plus_half", [P, pad])
        self.pace = self.sb("pace", [P, 1])
        self.ident = self.sb("identity", [P, P])
        self.ones = self.sb("ones", [P, P])

    def sb(self, name, shape, dt=F32, ctx=None):
        return (ctx or self.ctx).enter_context(self.nc.sbuf_tensor(name, shape, dt))

    def ps(self, name, ctx, shape=(P, T)):
        return ctx.enter_context(self.nc.psum_tensor(name, list(shape), F32))

    def sem(self, name):
        self.sems.append(self.nc.alloc_semaphore(name=name))
        return self.sems[-1]

    def grouped(self, t):
        if len(t.shape) == 3:
            return t[:, :, :].rearrange("p (g b) f -> p g b f", b=GB)
        return t[:, :].rearrange("p (g b) -> p g b", b=GB)


class Chain:

    def __init__(self, engine, sem):
        self.engine, self.sem, self.n = engine, sem, 0

    def link(self, instruction):
        self.n += 1
        instruction.then_inc(self.sem, 1)
        self.engine.wait_ge(self.sem, self.n)


def load_and_constants(c):
    nc, nb = c.nc, c.nb
    loaded, made, filled, counted = (c.sem(n) for n in ("x_loaded", "const_made", "const_zero", "stats_made"))
    xg, sg = c.grouped(c.x), c.grouped(c.stats)
    with nc.Block() as block:

        @block.sync
        def _(sp):
            n = nb // 4
            for k in range(4):
                sp.dma_start(c.x[:, k * n:(k + 1) * n, :],
                             c.io["x"][k * n:(k + 1) * n].rearrange("b n d -> n b d")).then_inc(loaded, 16)

        @block.gpsimd
        def _(pool):
            pool.memset(c.ident[:], 0.0).then_inc(filled, 1)
            pool.memset(c.ones[:], 1.0).then_inc(made, 1)
            pool.memset(c.mhalf[:], -0.5).then_inc(made, 1)
            pool.memset(c.phalf[:], 0.5).then_inc(made, 1)
            pool.memset(c.x[:, nb:, :], 0.0).then_inc(made, 1)
            pool.memset(c.stats[:, nb:, :], 0.0).then_inc(made, 1)
            pool.wait_ge(filled, 1)
            pool.affine_select(out=c.ident[:], in_=c.ident[:], compare_op=ALU.not_equal, fill=1.0, base=0,
                               pattern=[[-1, P]], channel_multiplier=1).then_inc(made, 1)
            pool.wait_ge(made, 6)

        @block.vector
        def _(dve):
            dve.wait_ge(loaded, 64)
            with dve.Fori(0, c.groups) as g:
                for b in range(GB):
                    last = dve.bn_stats(sg[:, g, b, :], xg[:, g, b, :])
                last.then_inc(counted, 1)
            dve.wait_ge(counted, c.groups)


def ln_dve(c, dve, chain, powed, double):
    m0, m1 = c.stats[:, :, 1], c.stats[:, :, 4]
    q0, q1 = c.stats[:, :, 2], c.stats[:, :, 5]
    t0, t1, t2 = (t[:] for t in c.tmp)
    link = chain.link
    link(dve.tensor_tensor(t0, m0, m1, ALU.subtract))
    link(dve.tensor_tensor(t1, m0, m1, ALU.add))
    link(dve.tensor_scalar(c.mean[:], t1, 0.5, None, ALU.mult))
    link(dve.tensor_tensor(t1, q0, q1, ALU.add))
    link(dve.tensor_tensor(t2, t0, t0, ALU.mult))
    link(dve.tensor_scalar(t2, t2, 0.25, None, ALU.mult))
    link(dve.scalar_tensor_tensor(t0, t1, 1.0 / P, t2, ALU.mult, ALU.add))
    dve.tensor_scalar(t1, t0, EPS, None, ALU.add).then_inc(powed, 1)
    dve.wait_ge(powed, 2)
    if double:
        link(dve.tensor_tensor(t2, c.rstd[:], c.rstd[:], ALU.mult))
        link(dve.tensor_tensor(t2, t2, t0, ALU.mult))
        dve.tensor_scalar(t2, t2, EPS, None, ALU.add).then_inc(powed, 1)
        dve.wait_ge(powed, 5)
        link(dve.tensor_tensor(c.rstd[:], c.rstd[:], c.rstd2[:], ALU.mult))


def ln_pool(c, pool, powed, double):
    pool.wait_ge(powed, 1)
    pool.tensor_tensor(c.rstd[:], c.tmp[1][:], c.mhalf[:], ALU.pow).then_inc(powed, 1)
    if double:
        pool.wait_ge(powed, 3)
        pool.tensor_tensor(c.rstd2[:], c.tmp[2][:], c.mhalf[:], ALU.pow).then_inc(powed, 1)
        pool.tensor_tensor(c.ratio[:], c.tmp[2][:], c.phalf[:], ALU.pow).then_inc(powed, 1)


def column_attention(c):
    nc, io, turns = c.nc, c.io, c.turns
    xg, sg = c.grouped(c.x), c.grouped(c.stats)
    meang, rstdg = c.grouped(c.mean), c.grouped(c.rstd)
    adjg = io["adj"].rearrange("(g b) i j -> g i b j", b=GB)
    with ExitStack() as ctx:
        sb = lambda name, shape, dt=F32: c.sb("ca_" + name, shape, dt, ctx)
        w, wT, a12, wa, wa1b = sb("w", [P, P]), sb("wT", [P, P]), sb("a12", [P, 2]), sb("wa", [P, 2]), sb("wa1b", [P, P])
        hp = sb("hp", [P, c.nb, P])
        hpg = hp[:, :, :].rearrange("p (g b) f -> p g b f", b=GB)
        adj_i = [sb(f"adj_i{s}", [P, GB, P], I32) for s in range(S)]
        adj_f = [sb(f"adj_f{s}", [P, GB, P]) for s in range(S)]
        xn = [sb(f"xn{s}", [P, GB, P]) for s in range(S)]
        xT = [sb(f"xT{s}", [P, T]) for s in range(S)]
        pen = [sb(f"pen{s}", [P, GB, P]) for s in range(S)]
        score = [sb(f"score{s}", [P, GB, P]) for s in range(S)]
        hs = [sb(f"hs{s}", [P, GB, P]) for s in range(S)]
        s2 = [sb(f"s2{s}", [P, GB]) for s in range(S)]
        nmax = [sb(f"nmax{s}", [P, GB]) for s in range(S)]
        den = [sb(f"den{s}", [P, GB]) for s in range(S)]
        rden = [sb(f"rden{s}", [P, GB]) for s in range(S)]
        bank = [[c.ps(f"ca_bank{s}{k}", ctx) for k in range(4)] for s in range(S)]
        loaded, chain, powed, prepared = (c.sem("ca_" + n) for n in ("loaded", "chain", "powed", "prepared"))
        gelued, added = c.sem("ca_gelued"), c.sem("ca_added")
        adj_in = [c.sem(f"ca_adj_in{s}") for s in range(S)]
        dv = [Steps(c.sem(f"ca_dve{s}"), "adj xn pen s2 masked leaky max rden hs") for s in range(S)]
        ac = [Steps(c.sem(f"ca_act{s}"), "xT exp hp") for s in range(S)]
        pe_ = [Steps(c.sem(f"ca_pe{s}"), "xT adjT h out") for s in range(S)]
        with nc.Block() as block:

            @block.sync
            def _(sp):
                sp.dma_start(w[:], io["L0_gnn_W"]).then_inc(loaded, 16)
                sp.dma_start(a12[:], io["L0_gnn_a"].rearrange("(t d) o -> d (t o)", t=2),
                             allow_slow_non_contiguous=True).then_inc(loaded, 16)
                with sp.Fori(0, turns) as i:
                    for s in range(S):
                        sp.wait_ge(dv[s].sem, dv[s].all_done(i))
                        sp.dma_start(adj_i[s][:], adjg[i * S + s]).then_inc(adj_in[s], 16)

            @block.gpsimd
            def _(pool):
                ln_pool(c, pool, powed, False)

            @block.scalar
            def _(act):
                for s in range(S):
                    ac[s].start(act)
                with act.Fori(0, turns) as i:
                    for s in range(S):
                        act.wait_ge(pe_[s].sem, pe_[s].done(i, "xT"))
                        ac[s].mark(act.activation(xT[s][:], bank[s][0][:], ACT.Copy), "xT")
                    for s in range(S):
                        act.wait_ge(dv[s].sem, dv[s].done(i, "max"))
                        for b in range(GB):
                            last = act.activation(score[s][:, b, :], score[s][:, b, :], ACT.Exp,
                                                  bias=nmax[s][:, b:b + 1], accum_out=den[s][:, b:b + 1])
                        ac[s].mark(last, "exp")
                    for s in range(S):
                        act.wait_ge(pe_[s].sem, pe_[s].done(i, "out"))
                        ac[s].mark(act.activation(hpg[:, i * S + s, :, :], bank[s][1][:, :].rearrange("p (b f) -> p b f", b=GB), ACT.Copy), "hp")
                for s in range(S):
                    act.wait_ge(ac[s].sem, ac[s].all_done(turns))
                with act.Fori(0, c.groups) as g:
                    act.activation(hpg[:, g, :, :], hpg[:, g, :, :], ACT.Gelu).then_inc(gelued, 1)

            @block.vector
            def _(dve):
                for s in range(S):
                    dv[s].start(dve)
                ln_dve(c, dve, Chain(dve, chain), powed, False)
                dve.wait_ge(loaded, 32)
                dve.wait_ge(prepared, 1)
                dve.tensor_copy(wT[:], bank[0][0][:, 0:P]).then_inc(prepared, 1)
                dve.wait_ge(prepared, 3)
                dve.tensor_copy(wa[:], bank[0][0][:, 0:2]).then_inc(prepared, 1)
                dve.wait_ge(prepared, 4)
                dve.tensor_scalar(wa1b[:], c.ones[:], wa[:, 0:1], None, ALU.mult).then_inc(prepared, 1)
                with dve.Fori(0, turns) as i:
                    for s in range(S):
                        dve.wait_ge(ac[s].sem, ac[s].all_done(i))
                        dve.wait_ge(adj_in[s], i * 16 + 16)
                        dv[s].mark(dve.tensor_copy(adj_f[s][:], adj_i[s][:]), "adj")
                        for b in range(GB):
                            last = dve.tensor_scalar(xn[s][:, b, :], xg[:, i * S + s, b, :], meang[:, i * S + s, b:b + 1],
                                                     rstdg[:, i * S + s, b:b + 1], ALU.subtract, ALU.mult)
                        dv[s].mark(last, "xn")
                    for s in range(S):
                        dve.wait_ge(pe_[s].sem, pe_[s].done(i, "adjT"))
                        dv[s].mark(dve.tensor_scalar(pen[s][:].rearrange("p b f -> p (b f)"), bank[s][1][:], 0.0, -1e20 / 0.4,
                                                     ALU.is_le, ALU.mult), "pen")
                    for s in range(S):
                        dve.wait_ge(pe_[s].sem, pe_[s].done(i, "h"))
                        dv[s].mark(dve.tensor_copy(s2[s][:], bank[s][3][:, 0:GB]), "s2")
                    for s in range(S):
                        dve.wait_ge(dv[s].sem, dv[s].done(i, "s2"))
                        for b in range(GB):
                            last = dve.scalar_tensor_tensor(score[s][:, b, :], bank[s][2][:, b * P:(b + 1) * P],
                                                            s2[s][:, b:b + 1], pen[s][:, b, :], ALU.add, ALU.add)
                        dv[s].mark(last, "masked")
                        dve.wait_ge(dv[s].sem, dv[s].done(i, "masked"))
                        dv[s].mark(dve.scalar_tensor_tensor(score[s][:], score[s][:], 0.4, score[s][:],
                                                            ALU.mult, ALU.max), "leaky")
                        dve.wait_ge(dv[s].sem, dv[s].done(i, "leaky"))
                        dv[s].mark(dve.tensor_reduce(nmax[s][:], score[s][:], AX_X, ALU.max, negate=True), "max")
                    for s in range(S):
                        dve.wait_ge(ac[s].sem, ac[s].done(i, "exp"))
                        dv[s].mark(dve.reciprocal(rden[s][:], den[s][:]), "rden")
                        dve.wait_ge(dv[s].sem, dv[s].done(i, "rden"))
                        for b in range(GB):
                            last = dve.tensor_scalar(hs[s][:, b, :], bank[s][0][:, b * P:(b + 1) * P],
                                                     rden[s][:, b:b + 1], None, ALU.mult)
                        dv[s].mark(last, "hs")
                with dve.Fori(0, c.groups) as g:
                    dve.wait_ge(gelued, g + 1)
                    dve.tensor_tensor(xg[:, g, :, :], xg[:, g, :, :], hpg[:, g, :, :], ALU.add).then_inc(added, 1)
                    dve.wait_ge(added, g + 1)
                    for b in range(GB):
                        dve.bn_stats(sg[:, g, b, :], xg[:, g, b, :])

            @block.tensor
            def _(pe):
                for s in range(S):
                    pe_[s].start(pe)
                pe.wait_ge(loaded, 32)
                pe.transpose(bank[0][0][:, 0:P], w[:], c.ident[:]).then_inc(prepared, 1)
                pe.wait_ge(prepared, 2)
                pe.matmul(bank[0][0][:, 0:2], wT[:], a12[:], start=True, stop=True).then_inc(prepared, 1)
                pe.wait_ge(prepared, 5)
                with pe.Fori(0, turns) as i:
                    for s in range(S):
                        pe.wait_ge(dv[s].sem, dv[s].done(i, "xn"))
                        for b in range(GB):
                            last = pe.transpose(bank[s][0][:, b * P:(b + 1) * P], xn[s][:, b, :], c.ident[:])
                        pe_[s].mark(last, "xT")
                        for b in range(GB):
                            last = pe.transpose(bank[s][1][:, b * P:(b + 1) * P], adj_f[s][:, b, :], c.ident[:])
                        pe_[s].mark(last, "adjT")
                    for s in range(S):
                        pe.wait_ge(ac[s].sem, ac[s].done(i, "xT"))
                        pe.matmul(bank[s][2][:], wa1b[:], xT[s][:], start=True, stop=True)
                        for b in range(GB):
                            pe.matmul(bank[s][3][:, b:b + 1], xT[s][:, b * P:(b + 1) * P], wa[:, 1:2],
                                      start=True, stop=True)
                        for b in range(GB):
                            last = pe.matmul(bank[s][0][:, b * P:(b + 1) * P], xT[s][:, b * P:(b + 1) * P], w[:],
                                             start=True, stop=True)
                        pe_[s].mark(last, "h")
                    for s in range(S):
                        pe.wait_ge(dv[s].sem, dv[s].done(i, "hs"))
                        for b in range(GB):
                            last = pe.matmul(bank[s][1][:, b * P:(b + 1) * P], score[s][:, b, :], hs[s][:, b, :],
                                             start=True, stop=True)
                        pe_[s].mark(last, "out")


def experts(c, tag, hidden, w1, b1, w2, b2, wr, br=None, gain=None, shift=None, routed_gain=False, double=False,
            shared=None):
    nc = c.nc
    ch = hidden // P
    first = 1 if shared else 0
    ne = E + first
    nk = ne * ch
    xg, sg = c.grouped(c.x), c.grouped(c.stats)
    meang, rstdg, ratiog = c.grouped(c.mean), c.grouped(c.rstd), c.grouped(c.ratio)
    SLOTS = 4
    PROD1, GELU, SPLIT, PROD2, YCOPY = 5, 4, 4, 2, 1
    NORM, TURN, COPY, CUT, ROUTE, TOP, TANH, PROBS = 0, 2, 3, 5, 5, 7, 9, 10
    assert nk % SLOTS == 0 and ch > YCOPY and PROBS < nk - PROD1 and (br is None or gain is None or True)

    with ExitStack() as ctx:
        sb = lambda name, shape, dt=F32: c.sb(f"{tag}_{name}", shape, dt, ctx)
        sem = lambda name: c.sem(f"{tag}_{name}")
        w1h, w1l = sb("w1_hi", [P, nk, P], F32R), sb("w1_lo", [P, nk, P], F32R)
        w2h, w2l = sb("w2_hi", [P, nk, P], F32R), sb("w2_lo", [P, nk, P], F32R)
        RAW = 4
        raw = [sb(f"raw{k}", [P, ch, P]) for k in range(RAW)]
        b1_rows, b2_rows, gain_rows, shift_rows = sb("b1_rows", [nk, P]), sb("b2_rows", [ne, P]), sb("gain_rows", [E, P]), sb("shift_rows", [E, P])
        b1T, b2T, gainT, shiftT = sb("b1T", [P, nk]), sb("b2T", [P, ne]), sb("gainT", [P, E]), sb("shiftT", [P, E])
        wr_sb, br_row, br_all = sb("wr", [P, E]), sb("br_row", [1, E]), sb("br_all", [P, E])
        iota, iota_i = sb("iota", [P, GB, E]), sb("iota_i", [P, GB, E], I32)
        shift_wide = sb("shift_wide", [P, P])
        xn, xf = sb("xn", [P, GB, P]), sb("xf", [P, T])
        x_hi = [sb(f"x_hi{u}", [P, T], F32R) for u in range(2)]
        x_lo = [sb(f"x_lo{u}", [P, T], F32R) for u in range(2)]
        g_full = [sb(f"g_full{k}", [P, T]) for k in range(SLOTS)]
        g_hi = [sb(f"g_hi{k}", [P, T], F32R) for k in range(SLOTS)]
        g_lo = [sb(f"g_lo{k}", [P, T], F32R) for k in range(SLOTS)]
        yT = [sb(f"yT{k}", [P, T]) for k in range(2)]
        probs = [sb(f"probs{u}", [P, GB, E]) for u in range(2)]
        logit, top = sb("logit", [P, GB, E]), sb("top", [P, GB, E])
        where, wheref = sb("where", [P, GB, E], U32), sb("wheref", [P, GB, E])
        gap, half, pa, pb = sb("gap", [P, GB]), sb("half", [P, GB]), sb("pa", [P, GB]), sb("pb", [P, GB])
        is_a, is_b = sb("is_a", [P, GB, E]), sb("is_b", [P, GB, E])
        hid = [c.ps(f"{tag}_hid{k}", ctx) for k in range(SLOTS)]
        ysum = [c.ps(f"{tag}_ysum{k}", ctx) for k in range(2)]
        yback, misc = c.ps(f"{tag}_yback", ctx), c.ps(f"{tag}_misc", ctx)

        small_in, chain, powed, prep, made = sem("small_in"), sem("chain"), sem("powed"), sem("prep"), sem("made")
        raw_in = [sem(f"raw_in{k}") for k in range(RAW)]
        raw_hi, raw_lo, b1_sum = sem("raw_hi"), sem("raw_lo"), sem("b1_sum")
        hid_ready = Count(sem("hid_ready"), nk)
        gelu_done = Count(sem("gelu_done"), nk, SLOTS)
        lo_done, second = Count(sem("lo_done"), nk, SLOTS), Count(sem("second"), nk, SLOTS)
        hi_done = [Count(sem("hi_even"), nk // 2), Count(sem("hi_odd"), nk // 2)]
        y_copied, turned_back, added = Count(sem("y_copied"), ne, 2), Count(sem("turned_back"), ne, 2), Count(sem("added"), ne, 1)
        xn_ready, xf_ready, gap_ready, tanh_ready = (
            Count(sem(n), 1) for n in ("xn_ready", "xf_ready", "gap_ready", "tanh_ready"))
        xT_ready, logit_ready, x_split, top_ready = (
            Count(sem(n), k, 1) for n, k in (("xT_ready", 1), ("logit_ready", 1), ("x_split", 2), ("top_ready", 5)))
        route = Count(sem("route"), 8)
        small = [(b1_rows[first * ch:nk, :], b1.rearrange("e (c h) -> (e c) h", h=P)), (b2_rows[first:ne, :], b2), (wr_sb[:], wr)]
        if shared:
            small += [(b1_rows[0:ch, :], shared[1].rearrange("(c h) -> c h", h=P)),
                      (b2_rows[0:1, :], shared[3].rearrange("(o d) -> o d", o=1))]
        if br is not None:
            small += [(br_row[:], br.rearrange("(o e) -> o e", o=1))]
        if gain is not None:
            small += [(gain_rows[:], gain), (shift_rows[:], shift)]

        def source(k):
            e = k % ne
            if k < ne:
                w = shared[0] if e < first else w1[e - first]
                return w.rearrange("d (c h) -> d c h", h=P)
            w = shared[2] if e < first else w2[e - first]
            return w.rearrange("(c h) d -> h c d", h=P)

        with nc.Block() as block:

            @block.sync
            def _(sp):
                for dst, src in small:
                    sp.dma_start(dst, src).then_inc(small_in, 16)
                for k in range(2 * ne):
                    if k >= RAW:
                        sp.wait_ge(raw_lo, k - RAW + 1)
                        if gain is not None and k - RAW < ne:
                            sp.wait_ge(b1_sum, k - RAW + 1)
                    sp.dma_start(raw[k % RAW][:], source(k)).then_inc(raw_in[k % RAW], 16)

            @block.gpsimd
            def _(pool):
                pool.iota(iota_i[:], pattern=[[0, GB], [1, E]], base=0, channel_multiplier=0).then_inc(made, 1)
                ln_pool(c, pool, powed, double)

            @block.scalar
            def _(act):
                act.sem_inc(gelu_done.sem, gelu_done.credit)
                act.sem_inc(y_copied.sem, y_copied.credit)

                def copy_xT(g):
                    act.wait_ge(xT_ready.sem, xT_ready.done(g))
                    act.wait_ge(x_split.sem, x_split.done(g, -1))
                    act.wait_ge(logit_ready.sem, logit_ready.done(g, -1))
                    act.activation(xf[:], misc[:], ACT.Copy).then_inc(xf_ready.sem, 1)

                def tanh(g):
                    act.wait_ge(gap_ready.sem, gap_ready.done(g))
                    act.activation(half[:], gap[:], ACT.Tanh, scale=0.5).then_inc(tanh_ready.sem, 1)

                def gelu(g, u, n):
                    act.wait_ge(hid_ready.sem, hid_ready.done(g, n))
                    act.wait_ge(lo_done.sem, lo_done.done(g, n - SLOTS))
                    k = (u * nk + n) % SLOTS
                    act.activation(g_full[k][:], hid[k][:], ACT.Gelu, bias=b1T[:, n % nk:n % nk + 1])\
                        .then_inc(gelu_done.sem, 1)
                    if n % 2:
                        act.wait_ge(gelu_done.sem, gelu_done.done(g, n))
                        act.wait_ge(second.sem, second.done(g, n - SLOTS))
                        act.activation(g_hi[k][:], g_full[k][:], ACT.Copy).then_inc(hi_done[1].sem, 1)

                def copy_y(g, u, e):
                    k = (u * ne + e) % 2
                    act.wait_ge(second.sem, second.done(g, e * ch + ch - 1))
                    act.wait_ge(turned_back.sem, turned_back.done(g, e - 2))
                    act.activation(yT[k][:], ysum[k][:], ACT.Identity, bias=b2T[:, e:e + 1]).then_inc(y_copied.sem, 1)

                for k in range(2 * ne):
                    act.wait_ge(raw_in[k % RAW], 16 * (k // RAW + 1))
                    if k == 0:
                        act.wait_ge(prep, 2)
                    e = k % ne
                    dst = (w1h if k < ne else w2h)[:, e * ch:(e + 1) * ch, :]
                    scale = gainT[:, e - first:e - first + 1] if gain is not None and k < ne and e >= first else 1.0
                    act.activation(dst, raw[k % RAW][:], ACT.Copy, scale=scale).then_inc(raw_hi, 1)
                copy_xT(0)
                tanh(0)
                act.wait_ge(prep, 5)
                for n in range(GELU):
                    gelu(0, 0, n)
                with act.Fori(0, c.turns) as i:
                    for u in range(2):
                        g = i * 2 + u
                        for m in range(nk):
                            gelu(g, u, m + GELU)
                            if (m + YCOPY) % ch == ch - 1 and m + YCOPY < nk:
                                copy_y(g, u, (m + YCOPY) // ch)
                            if m == COPY:
                                copy_xT(g + 1)
                            if m == TANH:
                                tanh(g + 1)

            @block.vector
            def _(dve):
                ln = Chain(dve, chain)
                link = ln.link
                dve.sem_inc(lo_done.sem, lo_done.credit)
                dve.sem_inc(added.sem, added.credit)
                dve.sem_inc(x_split.sem, x_split.credit)
                dve.sem_inc(top_ready.sem, top_ready.credit)
                ln_dve(c, dve, ln, powed, double)

                def normalise(g):
                    dve.wait_ge(xT_ready.sem, xT_ready.done(g, -1))
                    for b in range(GB):
                        last = dve.tensor_scalar(xn[:, b, :], xg[:, g, b, :], meang[:, g, b:b + 1], rstdg[:, g, b:b + 1],
                                                 ALU.subtract, ALU.mult)
                    last.then_inc(xn_ready.sem, 1)

                def cut(g, u):
                    dve.wait_ge(xf_ready.sem, xf_ready.done(g))
                    dve.tensor_copy(x_hi[u][:], xf[:]).then_inc(x_split.sem, 1)
                    dve.wait_ge(x_split.sem, x_split.done(g, 0))
                    dve.tensor_tensor(x_lo[u][:], xf[:], x_hi[u][:].bitcast(F32), ALU.subtract).then_inc(x_split.sem, 1)

                def top_two(g):
                    dve.wait_ge(logit_ready.sem, logit_ready.done(g))
                    for b in range(GB):
                        scale = ratiog[:, g, b:b + 1] if double and not routed_gain else 1.0
                        last = dve.scalar_tensor_tensor(logit[:, b, :], misc[:, b * E:(b + 1) * E], scale, br_all[:],
                                                        ALU.mult, ALU.add)
                    last.then_inc(top_ready.sem, 1)
                    dve.wait_ge(top_ready.sem, top_ready.done(g, 0))
                    dve.memset(c.pace[:], 0.0)
                    for b in range(GB):
                        last = dve.max(top[:, b, :], logit[:, b, :])
                    last.then_inc(top_ready.sem, 1)
                    dve.wait_ge(top_ready.sem, top_ready.done(g, 1))
                    dve.tensor_tensor(gap[:], top[:, :, 0], top[:, :, 1], ALU.subtract).then_inc(gap_ready.sem, 1)
                    for b in range(GB):
                        last = dve.max_index(where[:, b, :], top[:, b, :], logit[:, b, :])
                    last.then_inc(top_ready.sem, 1)
                    dve.wait_ge(top_ready.sem, top_ready.done(g, 2))
                    dve.tensor_copy(wheref[:], where[:]).then_inc(top_ready.sem, 1)
                    dve.wait_ge(top_ready.sem, top_ready.done(g, 3))
                    wide = [P, GB, E]
                    dve.tensor_tensor(is_a[:], iota[:], wheref[:, :, 0:1].to_broadcast(wide), ALU.is_equal)
                    dve.tensor_tensor(is_b[:], iota[:], wheref[:, :, 1:2].to_broadcast(wide), ALU.is_equal)\
                        .then_inc(top_ready.sem, 1)

                def two_probs(g, u):
                    dve.wait_ge(tanh_ready.sem, tanh_ready.done(g))
                    wide = [P, GB, E]
                    dve.tensor_scalar(pa[:], half[:], 0.5, 0.5, ALU.mult, ALU.add)
                    dve.tensor_scalar(pb[:], half[:], -0.5, 0.5, ALU.mult, ALU.add).then_inc(route.sem, 1)
                    dve.wait_ge(route.sem, route.done(g, 0))
                    dve.tensor_tensor(is_a[:], is_a[:], pa[:].unsqueeze(2).to_broadcast(wide), ALU.mult)
                    dve.tensor_tensor(is_b[:], is_b[:], pb[:].unsqueeze(2).to_broadcast(wide), ALU.mult)\
                        .then_inc(route.sem, 1)
                    dve.wait_ge(route.sem, route.done(g, 1))
                    dve.tensor_tensor(probs[u][:], is_a[:], is_b[:], ALU.add).then_inc(route.sem, 6)

                def split(g, u, n):
                    k = (u * nk + n) % SLOTS
                    dve.wait_ge(gelu_done.sem, gelu_done.done(g, n))
                    dve.wait_ge(second.sem, second.done(g, n - SLOTS))
                    if n % 2 == 0:
                        dve.tensor_copy(g_hi[k][:], g_full[k][:]).then_inc(hi_done[0].sem, 1)
                    dve.wait_ge(hi_done[n % 2].sem, hi_done[n % 2].done(g, n // 2))
                    dve.tensor_tensor(g_lo[k][:], g_full[k][:], g_hi[k][:].bitcast(F32), ALU.subtract)\
                        .then_inc(lo_done.sem, 1)

                def add(g, u, e):
                    dve.wait_ge(turned_back.sem, turned_back.done(g, e))
                    dve.wait_ge(added.sem, added.done(g, e - 1))
                    if e == first:
                        dve.wait_ge(route.sem, route.done(g, 7))
                    for b in range(GB):
                        p = 1.0 if e < first else probs[u][:, b, e - first:e - first + 1]
                        last = dve.scalar_tensor_tensor(xg[:, g, b, :], yback[:, b * P:(b + 1) * P], p, xg[:, g, b, :],
                                                        ALU.mult, ALU.add)
                    last.then_inc(added.sem, 1)

                dve.wait_ge(prep, 1)
                dve.wait_ge(made, 1)
                dve.tensor_copy(iota[:], iota_i[:])
                dve.tensor_copy(b2T[:], yback[:, 0:ne])
                if gain is not None:
                    dve.tensor_copy(gainT[:], hid[0][:, 0:E])
                    link(dve.tensor_copy(shiftT[:], hid[1][:, 0:E]))
                if routed_gain:
                    dve.tensor_scalar(shift_wide[:], c.ones[:], shiftT[:, 0:1], None, ALU.mult)
                if br is None:
                    dve.memset(br_all[:], 0.0)
                dve.drain().then_inc(prep, 1)
                dve.wait_ge(prep, 3)
                if br is not None:
                    dve.tensor_copy(br_all[:], hid[2][:, 0:E])
                if routed_gain:
                    dve.tensor_scalar(wr_sb[:], wr_sb[:], gainT[:, 0:1], None, ALU.mult)
                dve.drain().then_inc(prep, 1)
                for k in range(2 * ne):
                    e = k % ne
                    dst, hi = ((w[:, e * ch:(e + 1) * ch, :]) for w in ((w1l, w1h) if k < ne else (w2l, w2h)))
                    dve.wait_ge(raw_hi, k + 1)
                    if gain is not None and k < ne and e >= first:
                        ins = dve.scalar_tensor_tensor(dst, raw[k % RAW][:], gainT[:, e - first:e - first + 1],
                                                       hi.bitcast(F32), ALU.mult, ALU.subtract)
                    else:
                        ins = dve.tensor_tensor(dst, raw[k % RAW][:], hi.bitcast(F32), ALU.subtract)
                    ins.then_inc(raw_lo, 1)
                if gain is not None:
                    dve.wait_ge(b1_sum, ne)
                    link(dve.tensor_copy(b1T[:], misc[:, 0:nk]))
                    dve.tensor_tensor(b1T[:], b1T[:], ysum[0][:, 0:nk], ALU.add).then_inc(prep, 1)
                else:
                    dve.tensor_copy(b1T[:], misc[:, 0:nk]).then_inc(prep, 1)
                normalise(0)
                cut(0, 0)
                top_two(0)
                two_probs(0, 0)
                for n in range(SPLIT):
                    split(0, 0, n)
                with dve.Fori(0, c.turns) as i:
                    for u in range(2):
                        g = i * 2 + u
                        for m in range(nk):
                            split(g, u, m + SPLIT)
                            if m == NORM:
                                normalise(g + 1)
                            if m == CUT:
                                cut(g + 1, 1 - u)
                            if m == TOP:
                                top_two(g + 1)
                            if m == PROBS:
                                two_probs(g + 1, 1 - u)
                            if m % ch == ch - 1:
                                add(g, u, m // ch)
                        dve.wait_ge(added.sem, added.done(g, ne - 1))
                        for b in range(GB):
                            dve.bn_stats(sg[:, g, b, :], xg[:, g, b, :])

            @block.tensor
            def _(pe):
                pe.sem_inc(second.sem, second.credit)
                pe.sem_inc(turned_back.sem, turned_back.credit)
                pe.sem_inc(xT_ready.sem, xT_ready.credit)
                pe.sem_inc(logit_ready.sem, logit_ready.credit)

                def turn(g):
                    pe.wait_ge(xn_ready.sem, xn_ready.done(g))
                    pe.wait_ge(top_ready.sem, top_ready.done(g, -1))
                    for b in range(GB):
                        last = pe.transpose(misc[:, b * P:(b + 1) * P], xn[:, b, :], c.ident[:])
                    last.then_inc(xT_ready.sem, 1)

                def router(g):
                    pe.wait_ge(xf_ready.sem, xf_ready.done(g))
                    for b in range(GB):
                        last = pe.matmul(misc[:, b * E:(b + 1) * E], xf[:, b * P:(b + 1) * P], wr_sb[:], start=True, stop=True)
                    last.then_inc(logit_ready.sem, 1)

                def product(out, hi, lo, x, y, start, stop):
                    pe.matmul(out, hi, x, start=start, stop=False)
                    pe.matmul(out, hi, y, start=False, stop=False)
                    return pe.matmul(out, lo, x, start=False, stop=stop)

                def first_product(g, u, n):
                    k = (u * nk + n) % SLOTS
                    if n % nk == 0:
                        pe.wait_ge(x_split.sem, x_split.done(g, 2 * (n // nk) + 1))
                    pe.wait_ge(gelu_done.sem, gelu_done.done(g, n - SLOTS))
                    v = (u + n // nk) % 2
                    product(hid[k][:], w1h[:, n % nk, :], w1l[:, n % nk, :], x_hi[v][:], x_lo[v][:], True, True)\
                        .then_inc(hid_ready.sem, 1)

                def second_product(g, u, n):
                    k = (u * nk + n) % SLOTS
                    pe.wait_ge(lo_done.sem, lo_done.done(g, n))
                    e = n // ch
                    if n % ch == 0:
                        pe.wait_ge(y_copied.sem, y_copied.done(g, e - 2))
                    product(ysum[(u * ne + e) % 2][:], w2h[:, n % nk, :], w2l[:, n % nk, :], g_hi[k][:], g_lo[k][:],
                            n % ch == 0, n % ch == ch - 1).then_inc(second.sem, 1)

                def turn_back(g, u, e):
                    k = (u * ne + e) % 2
                    pe.wait_ge(y_copied.sem, y_copied.done(g, e))
                    pe.wait_ge(added.sem, added.done(g, e - 1))
                    for b in range(GB):
                        last = pe.transpose(yback[:, b * P:(b + 1) * P], yT[k][:, b * P:(b + 1) * P], c.ident[:])
                    last.then_inc(turned_back.sem, 1)

                pe.wait_ge(small_in, 16 * len(small))
                pe.transpose(misc[:, 0:nk], b1_rows[:], c.ident[0:nk, 0:nk])
                last = pe.transpose(yback[:, 0:ne], b2_rows[:], c.ident[0:ne, 0:ne])
                if gain is not None:
                    pe.transpose(hid[0][:, 0:E], gain_rows[:], c.ident[0:E, 0:E])
                    last = pe.transpose(hid[1][:, 0:E], shift_rows[:], c.ident[0:E, 0:E])
                last.then_inc(prep, 1)
                pe.wait_ge(prep, 2)
                if br is not None:
                    last = pe.matmul(hid[2][:, 0:E], c.ones[0:1, :], br_row[:], start=True, stop=not routed_gain)
                    if routed_gain:
                        last = pe.matmul(hid[2][:, 0:E], shift_wide[:], wr_sb[:], start=False, stop=True)
                    last.then_inc(prep, 1)
                else:
                    pe.sem_inc(prep, 1)
                if gain is not None:
                    for k in range(ne):
                        pe.wait_ge(raw_in[k % RAW], 16 * (k // RAW + 1))
                        for j in range(ch):
                            last = pe.matmul(ysum[0][:, k * ch + j:k * ch + j + 1], raw[k % RAW][:, j, :], shiftT[:, k:k + 1],
                                             start=True, stop=True)
                        last.then_inc(b1_sum, 1)
                pe.wait_ge(prep, 5)
                pe.wait_ge(raw_lo, 2 * ne)
                turn(0)
                router(0)
                for n in range(PROD1):
                    first_product(0, 0, n)
                for n in range(PROD2):
                    second_product(0, 0, n)
                with pe.Fori(0, c.turns) as i:
                    for u in range(2):
                        g = i * 2 + u
                        for m in range(nk):
                            first_product(g, u, m + PROD1)
                            second_product(g, u, m + PROD2)
                            if m == TURN:
                                turn(g + 1)
                            if m == ROUTE:
                                router(g + 1)
                            if m % ch == ch - 1:
                                turn_back(g, u, m // ch)
                if PROD2 % ch:
                    pe.matmul(ysum[0][:], w2h[:, 0, :], g_hi[0][:], start=False, stop=True)


def l0_experts(c):
    io = c.io
    row = lambda v: v.rearrange("(o d) -> o d", o=1).to_broadcast([E, P])
    experts(c, "e0", 256, io["L0_ffn_W1"], io["L0_ffn_b1"], io["L0_ffn_W2"], io["L0_ffn_b2"], io["L0_ffn_Wr"],
            br=io["L0_ffn_br"], gain=row(io["L0_ffn_gamma"]), shift=row(io["L0_ffn_beta"]), routed_gain=True, double=True)


def l1_experts(c):
    io = c.io
    experts(c, "e1", 512, io["L1_ffn_W1"], io["L1_ffn_b1"], io["L1_ffn_W2"], io["L1_ffn_b2"], io["L1_ffn_Wr"],
            br=io["L1_ffn_br"], gain=io["L1_ffn_ln_g"], shift=io["L1_ffn_ln_b"], double=True)


def l3_experts(c):
    io = c.io
    experts(c, "e3", 512, io["L3_ffn_W1p"], io["L3_ffn_b1p"], io["L3_ffn_W2p"], io["L3_ffn_b2p"], io["L3_ffn_Wr"],
            shared=(io["L3_ffn_W1s"], io["L3_ffn_b1s"], io["L3_ffn_W2s"], io["L3_ffn_b2s"]))


HEADS = 8
DK = P // HEADS


def head_attention(c):
    nc, io = c.nc, c.io
    xg, sg = c.grouped(c.x), c.grouped(c.stats)
    meang, rstdg = c.grouped(c.mean), c.grouped(c.rstd)
    adjg = io["adj"].rearrange("(g b) i j -> g i b j", b=GB)
    row = lambda v: v.rearrange("(o d) -> o d", o=1)
    with ExitStack() as ctx:
        sb = lambda name, shape, dt=F32: c.sb("ha_" + name, shape, dt, ctx)
        sem = lambda name: c.sem("ha_" + name)
        w = {k: sb("w" + k, [P, P]) for k in "qkvo"}
        bias_rows, biasT, biasq4 = sb("bias_rows", [4, P]), sb("biasT", [P, 4]), sb("biasq4", [P, 1])
        bo_row, bv_col, ds, nds = sb("bo_row", [1, P]), sb("bv_col", [P, 1]), sb("ds", [1, 1]), sb("nds", [P, 1])
        head = sb("head", [P, HEADS])
        adj_i = [sb(f"adj_i{u}", [P, GB, P], I32) for u in range(2)]
        pen = [sb(f"pen{u}", [P, GB, P]) for u in range(2)]
        qT = [sb(f"qT{u}", [P, T]) for u in range(2)]
        km = [sb(f"km{u}", [P, HEADS, T]) for u in range(2)]
        va = [sb(f"va{u}", [P, GB, HEADS, DK + 1]) for u in range(2)]
        xn, xT, kT, oT = sb("xn", [P, GB, P]), sb("xT", [P, T]), sb("kT", [P, T]), sb("oT", [P, T])
        sc = [sb(f"sc{k}", [P, HEADS, P]) for k in range(2)]
        mx = [sb(f"mx{k}", [P, HEADS]) for k in range(2)]
        pT = [sb(f"pT{k}", [P, HEADS, P]) for k in range(2)]
        rd, on = sb("rd", [P, HEADS, 1]), sb("on", [P, HEADS, DK])
        scores = [c.ps(f"ha_scores{k}", ctx, (P, HEADS, P)) for k in range(2)]
        turned_w = c.ps("ha_turned_w", ctx, (P, HEADS, P))
        out, misc = c.ps("ha_out", ctx), c.ps("ha_misc", ctx)
        heads_o = out[:, 0:HEADS * (DK + 1)].rearrange("p (h d) -> p h d", h=HEADS)
        turned_o = out[:, 2 * P:3 * P]
        loaded, chain, powed, prep, head_made = (sem(n) for n in ("loaded", "chain", "powed", "prep", "head_made"))
        adj_in = [sem(f"adj_in{u}") for u in range(2)]
        score_ready, masked, max_done, sub_done, exp_done, wT_ready, wT_copied, o_ready, inv_done, on_done, oT_ready = (
            Count(sem(n), GB) for n in ("score_ready", "masked", "max_done", "sub_done", "exp_done", "wT_ready",
                                        "wT_copied", "o_ready", "inv_done", "on_done", "oT_ready"))
        oT_copied = Count(sem("oT_copied"), GB, 1)
        xn_ready, xT_ready, xT_copied, k_ready, k_copied, q_ready, q_copied, v_ready, v_copied, y_ready = (
            Count(sem(n), 1) for n in ("xn_ready", "xT_ready", "xT_copied", "k_ready", "k_copied", "q_ready", "q_copied",
                                       "v_ready", "v_copied", "y_ready"))
        far, pen_done, km_low, km_high = (Count(sem(n), 1) for n in ("far", "pen_done", "km_low", "km_high"))
        x_added = Count(sem("x_added"), 1, 1)
        half = HEADS // 2
        with nc.Block() as block:

            @block.sync
            def _(sp):
                for k in "qkvo":
                    sp.dma_start(w[k][:], io["L1_gnn_W_" + k]).then_inc(loaded, 16)
                for n, k in enumerate("qkvo"):
                    sp.dma_start(bias_rows[n:n + 1, :], row(io["L1_gnn_b_" + k])).then_inc(loaded, 16)
                sp.dma_start(bo_row[:], row(io["L1_gnn_b_o"])).then_inc(loaded, 16)
                sp.dma_start(ds[:], io["L1_gnn_dist_scale"]).then_inc(loaded, 16)
                for u in range(2):
                    sp.dma_start(adj_i[u][:], adjg[u]).then_inc(adj_in[u], 16)
                if c.turns > 1:
                    with sp.Fori(0, c.turns - 1) as i:
                        for u in range(2):
                            sp.wait_ge(pen_done.sem, pen_done.done(i * 2 + u))
                            sp.dma_start(adj_i[u][:], adjg[i * 2 + u + 2]).then_inc(adj_in[u], 16)
                sp.wait_ge(pen_done.sem, pen_done.done(c.groups - 2))
                sp.dma_start(adj_i[0][:], adjg[0]).then_inc(adj_in[0], 16)

            @block.gpsimd
            def _(pool):
                def subtract(g, b):
                    k = b % 2
                    pool.wait_ge(max_done.sem, max_done.done(g, b))
                    pool.tensor_tensor(sc[k][:], sc[k][:], mx[k][:].unsqueeze(2).to_broadcast([P, HEADS, P]), ALU.subtract)\
                        .then_inc(sub_done.sem, 1)

                pool.memset(head[:], 1.0).then_inc(head_made, 1)
                for u in range(2):
                    pool.memset(va[u][:], 1.0).then_inc(head_made, 1)
                pool.wait_ge(head_made, 1)
                pool.affine_select(out=head[:], in_=head[:], compare_op=ALU.is_ge, fill=0.0, base=0,
                                   pattern=[[-DK, HEADS]], channel_multiplier=1).then_inc(head_made, 1)
                pool.wait_ge(head_made, 4)
                pool.affine_select(out=head[:], in_=head[:], compare_op=ALU.is_ge, fill=0.0, base=DK - 1,
                                   pattern=[[DK, HEADS]], channel_multiplier=-1).then_inc(head_made, 1)
                ln_pool(c, pool, powed, False)
                subtract(0, 0)
                subtract(0, 1)
                with pool.Fori(0, c.turns) as i:
                    for u in range(2):
                        for b in range(GB):
                            subtract(i * 2 + u, b + 2)

            @block.scalar
            def _(act):
                act.sem_inc(oT_copied.sem, oT_copied.credit)

                def exponentials(g, b):
                    act.wait_ge(sub_done.sem, sub_done.done(g, b))
                    act.activation(sc[b % 2][:], sc[b % 2][:], ACT.Exp).then_inc(exp_done.sem, 1)

                def copy_turned(g, b):
                    act.wait_ge(wT_ready.sem, wT_ready.done(g, b))
                    act.activation(pT[b % 2][:], turned_w[:], ACT.Copy).then_inc(wT_copied.sem, 1)

                def copy_xT(g):
                    act.wait_ge(xT_ready.sem, xT_ready.done(g))
                    act.activation(xT[:], misc[:], ACT.Copy).then_inc(xT_copied.sem, 1)

                def copy_k(g, u):
                    act.wait_ge(k_ready.sem, k_ready.done(g))
                    act.activation(kT[:], misc[:], ACT.Identity, bias=biasT[:, 1:2]).then_inc(k_copied.sem, 1)
                    act.wait_ge(k_copied.sem, k_copied.done(g))
                    for h in range(half, HEADS):
                        last = act.activation(km[u][:, h, :], kT[:], ACT.Copy, scale=head[:, h:h + 1])
                    last.then_inc(km_high.sem, 1)

                def copy_q(g, u):
                    act.wait_ge(q_ready.sem, q_ready.done(g))
                    act.activation(qT[u][:], misc[:], ACT.Identity, bias=biasq4[:], scale=DK ** -0.5).then_inc(q_copied.sem, 1)

                def copy_v(g, u):
                    act.wait_ge(v_ready.sem, v_ready.done(g))
                    for b in range(GB):
                        last = act.activation(va[u][:, b, :, 0:DK], misc[:, b * P:(b + 1) * P].rearrange("p (h d) -> p h d", h=HEADS),
                                              ACT.Copy)
                    last.then_inc(v_copied.sem, 1)

                act.wait_ge(prep, 4)
                copy_xT(0)
                copy_k(0, 0)
                copy_q(0, 0)
                copy_v(0, 0)
                copy_xT(1)
                exponentials(0, 0)
                copy_turned(0, 0)
                exponentials(0, 1)
                with act.Fori(0, c.turns) as i:
                    for u in range(2):
                        g = i * 2 + u
                        for b in range(GB):
                            if b == 0:
                                copy_k(g + 1, 1 - u)
                                copy_q(g + 1, 1 - u)
                            if b == 1:
                                copy_v(g + 1, 1 - u)
                            if b == 2:
                                copy_xT(g + 2)
                            copy_turned(g, b + 1)
                            act.wait_ge(oT_ready.sem, oT_ready.done(g, b))
                            act.activation(oT[:, b * P:(b + 1) * P], turned_o, ACT.Copy).then_inc(oT_copied.sem, 1)
                            exponentials(g, b + 2)

            @block.vector
            def _(dve):
                ln = Chain(dve, chain)
                ln_dve(c, dve, ln, powed, False)
                dve.sem_inc(x_added.sem, x_added.credit)

                def normalise(g):
                    for b in range(GB):
                        last = dve.tensor_scalar(xn[:, b, :], xg[:, g, b, :], meang[:, g, b:b + 1], rstdg[:, g, b:b + 1],
                                                 ALU.subtract, ALU.mult)
                    last.then_inc(xn_ready.sem, 1)

                def penalty(g, u, nth):
                    dve.wait_ge(adj_in[u], nth * 16 + 16)
                    dve.tensor_scalar(pen[u][:], adj_i[u][:], 0.0, -1e9, ALU.is_le, ALU.mult).then_inc(far.sem, 1)
                    dve.wait_ge(far.sem, far.done(g))
                    dve.scalar_tensor_tensor(pen[u][:], adj_i[u][:], nds[:], pen[u][:], ALU.mult, ALU.add)\
                        .then_inc(pen_done.sem, 1)

                def mask_k(g, u):
                    dve.wait_ge(k_copied.sem, k_copied.done(g))
                    for h in range(half):
                        last = dve.tensor_scalar(km[u][:, h, :], kT[:], head[:, h:h + 1], None, ALU.mult)
                    last.then_inc(km_low.sem, 1)

                def maxima(g, u, b):
                    k = b % 2
                    v = (u + b // GB) % 2
                    dve.wait_ge(score_ready.sem, score_ready.done(g, b))
                    if b % GB == 0:
                        dve.wait_ge(pen_done.sem, pen_done.done(g + b // GB))
                    dve.tensor_tensor(sc[k][:], scores[k][:], pen[v][:, b % GB:b % GB + 1, :].to_broadcast([P, HEADS, P]), ALU.add)\
                        .then_inc(masked.sem, 1)
                    dve.wait_ge(masked.sem, masked.done(g, b))
                    dve.tensor_reduce(mx[k][:], sc[k][:], AX_X, ALU.max).then_inc(max_done.sem, 1)

                dve.wait_ge(prep, 1)
                dve.tensor_copy(nds[:], misc[:, 4:5])
                ln.link(dve.tensor_copy(biasT[:], misc[:, 0:4]))
                ln.link(dve.tensor_scalar(nds[:], nds[:], -1.0, None, ALU.mult))
                dve.tensor_scalar(biasq4[:], biasT[:, 0:1], DK ** -0.5, None, ALU.mult)
                dve.wait_ge(head_made, 5)
                dve.tensor_copy(bv_col[:], biasT[:, 2:3]).then_inc(prep, 1)
                dve.wait_ge(prep, 3)
                dve.tensor_tensor(bo_row[:], bo_row[:], misc[0:1, 8:8 + P], ALU.add).then_inc(prep, 1)
                normalise(0)
                penalty(0, 0, 0)
                dve.wait_ge(xT_ready.sem, xT_ready.done(0))
                normalise(1)
                mask_k(0, 0)
                maxima(0, 0, 0)
                maxima(0, 0, 1)
                with dve.Fori(0, c.turns) as i:
                    for u in range(2):
                        g = i * 2 + u
                        for b in range(GB):
                            dve.wait_ge(o_ready.sem, o_ready.done(g, b))
                            dve.reciprocal(rd[:], heads_o[:, :, DK:DK + 1]).then_inc(inv_done.sem, 1)
                            dve.wait_ge(inv_done.sem, inv_done.done(g, b))
                            dve.tensor_tensor(on[:], heads_o[:, :, 0:DK], rd[:].to_broadcast([P, HEADS, DK]), ALU.mult)\
                                .then_inc(on_done.sem, 1)
                            if b == 1:
                                mask_k(g + 1, 1 - u)
                            dve.wait_ge(wT_ready.sem, wT_ready.done(g, b))
                            maxima(g, u, b + 2)
                            if b == 0:
                                penalty(g + 1, 1 - u, i + u)
                            if b == 1:
                                normalise(g + 2)
                        dve.wait_ge(y_ready.sem, y_ready.done(g))
                        dve.tensor_tensor(xg[:, g, :, :], xg[:, g, :, :], misc[:].rearrange("p (b f) -> p b f", b=GB), ALU.add)\
                            .then_inc(x_added.sem, 1)
                        dve.wait_ge(x_added.sem, x_added.done(g))
                        for b in range(GB):
                            dve.bn_stats(sg[:, g, b, :], xg[:, g, b, :])

            @block.tensor
            def _(pe):
                def turn(g):
                    pe.wait_ge(xn_ready.sem, xn_ready.done(g))
                    for b in range(GB):
                        last = pe.transpose(misc[:, b * P:(b + 1) * P], xn[:, b, :], c.ident[:])
                    last.then_inc(xT_ready.sem, 1)

                def make_k(g):
                    pe.wait_ge(xT_copied.sem, xT_copied.done(g))
                    pe.matmul(misc[:], w["k"][:], xT[:], start=True, stop=True).then_inc(k_ready.sem, 1)

                def make_q(g):
                    pe.wait_ge(k_copied.sem, k_copied.done(g))
                    pe.matmul(misc[:], w["q"][:], xT[:], start=True, stop=True).then_inc(q_ready.sem, 1)

                def make_v(g):
                    pe.wait_ge(q_copied.sem, q_copied.done(g))
                    for b in range(GB):
                        last = pe.matmul(misc[:, b * P:(b + 1) * P], xT[:, b * P:(b + 1) * P], w["v"][:], start=True, stop=True)
                    last.then_inc(v_ready.sem, 1)

                def take_scores(g, u, b):
                    v = (u + b // GB) % 2
                    at = slice(b % GB * P, b % GB * P + P)
                    if b % GB == 0:
                        for ready in (q_copied, km_low, km_high):
                            pe.wait_ge(ready.sem, ready.done(g + b // GB))
                    for k in range(2):
                        last = pe.matmul(scores[b % 2][:, k * half:(k + 1) * half, :], qT[v][:, at],
                                         km[v][:, k * half:(k + 1) * half, at], start=True, stop=True)
                    last.then_inc(score_ready.sem, 1)

                def turn_weights(g, b):
                    pe.wait_ge(exp_done.sem, exp_done.done(g, b))
                    for h in range(HEADS):
                        last = pe.transpose(turned_w[:, h, :], sc[b % 2][:, h, :], c.ident[:])
                    last.then_inc(wT_ready.sem, 1)

                pe.wait_ge(loaded, 160)
                pe.transpose(misc[:, 0:4], bias_rows[:], c.ident[0:4, 0:4])
                pe.matmul(misc[:, 4:5], c.ones[0:1, :], ds[:], start=True, stop=True).then_inc(prep, 1)
                pe.wait_ge(prep, 2)
                pe.matmul(misc[0:1, 8:8 + P], bv_col[:], w["o"][:], start=True, stop=True).then_inc(prep, 1)
                pe.wait_ge(prep, 4)
                turn(0)
                make_k(0)
                make_q(0)
                make_v(0)
                pe.wait_ge(v_copied.sem, v_copied.done(0))
                turn(1)
                take_scores(0, 0, 0)
                take_scores(0, 0, 1)
                turn_weights(0, 0)
                take_scores(0, 0, 2)
                with pe.Fori(0, c.turns) as i:
                    for u in range(2):
                        g = i * 2 + u
                        for b in range(GB):
                            pe.wait_ge(wT_copied.sem, wT_copied.done(g, b))
                            pe.wait_ge(oT_copied.sem, oT_copied.done(g, b - 1))
                            for h in range(HEADS):
                                last = pe.matmul(heads_o[:, h, :], pT[b % 2][:, h, :], va[u][:, b, h, :], start=True, stop=True)
                            last.then_inc(o_ready.sem, 1)
                            if b == 0:
                                pe.wait_ge(x_added.sem, x_added.done(g, -1))
                                make_k(g + 1)
                            turn_weights(g, b + 1)
                            pe.wait_ge(on_done.sem, on_done.done(g, b))
                            pe.transpose(turned_o, on[:].rearrange("p h d -> p (h d)"), c.ident[:]).then_inc(oT_ready.sem, 1)
                            if b == 0:
                                make_q(g + 1)
                            if b == 1:
                                make_v(g + 1)
                            if b == 2:
                                pe.wait_ge(v_copied.sem, v_copied.done(g + 1))
                                turn(g + 2)
                            take_scores(g, u, b + 3)
                        pe.wait_ge(oT_copied.sem, oT_copied.done(g, GB - 1))
                        pe.wait_ge(xT_copied.sem, xT_copied.done(g + 2))
                        for b in range(GB):
                            at = slice(b * P, (b + 1) * P)
                            pe.matmul(misc[:, at], c.ones[0:1, :], bo_row[:], start=True, stop=False)
                            last = pe.matmul(misc[:, at], oT[:, at], w["o"][:], start=False, stop=True)
                        last.then_inc(y_ready.sem, 1)


def mean_messages(c):
    nc, io, turns = c.nc, c.io, c.turns
    xg, sg = c.grouped(c.x), c.grouped(c.stats)
    meang, rstdg = c.grouped(c.mean), c.grouped(c.rstd)
    adjg = io["adj"].rearrange("(g b) i j -> g i b j", b=GB)
    with ExitStack() as ctx:
        sb = lambda name, shape, dt=F32: c.sb("mm_" + name, shape, dt, ctx)
        wm, wu, bias = sb("wm", [P, P]), sb("wu", [P, P]), sb("bias", [1, P])
        adj_i = [sb(f"adj_i{s}", [P, GB, P], I32) for s in range(S)]
        adj_f = [sb(f"adj_f{s}", [P, GB, P]) for s in range(S)]
        xn = [sb(f"xn{s}", [P, GB, P]) for s in range(S)]
        xT = [sb(f"xT{s}", [P, T]) for s in range(S)]
        ha = [sb(f"ha{s}", [P, GB, P + 1]) for s in range(S)]
        up = [sb(f"up{s}", [P, GB, P]) for s in range(S)]
        deg = [sb(f"deg{s}", [P, GB]) for s in range(S)]
        rdeg = [sb(f"rdeg{s}", [P, GB]) for s in range(S)]
        bank = [[c.ps(f"mm_bank{s}{k}", ctx) for k in range(4)] for s in range(S)]
        loaded, chain, powed, ones = (c.sem("mm_" + n) for n in ("loaded", "chain", "powed", "ones"))
        adj_in = [c.sem(f"mm_adj_in{s}") for s in range(S)]
        dv = [Steps(c.sem(f"mm_dve{s}"), "adj xn deg rdeg pos scale sum x") for s in range(S)]
        ac = [Steps(c.sem(f"mm_act{s}"), "xT h up") for s in range(S)]
        pe_ = [Steps(c.sem(f"mm_pe{s}"), "xT h msg") for s in range(S)]
        with nc.Block() as block:

            @block.sync
            def _(sp):
                sp.dma_start(wm[:], io["L2_gnn_W_msg"]).then_inc(loaded, 16)
                sp.dma_start(wu[:], io["L2_gnn_W_upd"]).then_inc(loaded, 16)
                sp.dma_start(bias[:], io["L2_gnn_bias"].rearrange("(o d) -> o d", o=1)).then_inc(loaded, 16)
                with sp.Fori(0, turns) as i:
                    for s in range(S):
                        sp.wait_ge(dv[s].sem, dv[s].all_done(i))
                        sp.dma_start(adj_i[s][:], adjg[i * S + s]).then_inc(adj_in[s], 16)

            @block.gpsimd
            def _(pool):
                for s in range(S):
                    pool.memset(ha[s][:], 1.0).then_inc(ones, 1)
                ln_pool(c, pool, powed, False)

            @block.scalar
            def _(act):
                for s in range(S):
                    ac[s].start(act)
                act.wait_ge(ones, S)
                with act.Fori(0, turns) as i:
                    for s in range(S):
                        act.wait_ge(pe_[s].sem, pe_[s].done(i, "xT"))
                        ac[s].mark(act.activation(xT[s][:], bank[s][0][:], ACT.Copy), "xT")
                    for s in range(S):
                        act.wait_ge(pe_[s].sem, pe_[s].done(i, "h"))
                        wide = "p (b f) -> p b f"
                        ac[s].mark(act.activation(ha[s][:, :, 0:P], bank[s][1][:].rearrange(wide, b=GB), ACT.Copy), "h")
                        ac[s].mark(act.activation(up[s][:], bank[s][0][:].rearrange(wide, b=GB), ACT.Copy), "up")

            @block.vector
            def _(dve):
                for s in range(S):
                    dv[s].start(dve)
                ln_dve(c, dve, Chain(dve, chain), powed, False)
                with dve.Fori(0, turns) as i:
                    for s in range(S):
                        dve.wait_ge(adj_in[s], i * 16 + 16)
                        dv[s].mark(dve.tensor_copy(adj_f[s][:], adj_i[s][:]), "adj")
                        for b in range(GB):
                            last = dve.tensor_scalar(xn[s][:, b, :], xg[:, i * S + s, b, :], meang[:, i * S + s, b:b + 1],
                                                     rstdg[:, i * S + s, b:b + 1], ALU.subtract, ALU.mult)
                        dv[s].mark(last, "xn")
                    for s in range(S):
                        msg = lambda b: bank[s][2 + b // 2][:, b % 2 * (P + 1):(b % 2 + 1) * (P + 1)]
                        dve.wait_ge(pe_[s].sem, pe_[s].done(i, "msg"))
                        for b in range(GB):
                            last = dve.tensor_copy(deg[s][:, b:b + 1], msg(b)[:, P:P + 1])
                        dv[s].mark(last, "deg")
                        dve.wait_ge(dv[s].sem, dv[s].done(i, "deg"))
                        dv[s].mark(dve.tensor_scalar(rdeg[s][:], deg[s][:], 1.0, None, ALU.max), "rdeg")
                        dve.wait_ge(dv[s].sem, dv[s].done(i, "rdeg"))
                        dve.reciprocal(rdeg[s][:], rdeg[s][:])
                        dv[s].mark(dve.tensor_scalar(deg[s][:], deg[s][:], 0.0, None, ALU.is_gt), "pos")
                        dve.wait_ge(dv[s].sem, dv[s].done(i, "pos"))
                        dv[s].mark(dve.tensor_tensor(rdeg[s][:], rdeg[s][:], deg[s][:], ALU.mult), "scale")
                        dve.wait_ge(ac[s].sem, ac[s].done(i, "up"))
                        dve.wait_ge(dv[s].sem, dv[s].done(i, "scale"))
                        for b in range(GB):
                            last = dve.scalar_tensor_tensor(up[s][:, b, :], msg(b)[:, 0:P], rdeg[s][:, b:b + 1], up[s][:, b, :],
                                                            ALU.mult, ALU.add)
                        dv[s].mark(last, "sum")
                        dve.wait_ge(dv[s].sem, dv[s].done(i, "sum"))
                        dv[s].mark(dve.scalar_tensor_tensor(xg[:, i * S + s, :, :], up[s][:], 0.0, xg[:, i * S + s, :, :],
                                                            ALU.max, ALU.add), "x")
                        dve.wait_ge(dv[s].sem, dv[s].done(i, "x"))
                        for b in range(GB):
                            dve.bn_stats(sg[:, i * S + s, b, :], xg[:, i * S + s, b, :])

            @block.tensor
            def _(pe):
                for s in range(S):
                    pe_[s].start(pe)
                pe.wait_ge(loaded, 48)
                with pe.Fori(0, turns) as i:
                    for s in range(S):
                        pe.wait_ge(dv[s].sem, dv[s].done(i, "xn"))
                        for b in range(GB):
                            last = pe.transpose(bank[s][0][:, b * P:(b + 1) * P], xn[s][:, b, :], c.ident[:])
                        pe_[s].mark(last, "xT")
                    for s in range(S):
                        pe.wait_ge(ac[s].sem, ac[s].done(i, "xT"))
                        for b in range(GB):
                            at = slice(b * P, (b + 1) * P)
                            pe.matmul(bank[s][1][:, at], xT[s][:, at], wm[:], start=True, stop=True)
                            pe.matmul(bank[s][0][:, at], c.ones[0:1, :], bias[:], start=True, stop=False)
                            last = pe.matmul(bank[s][0][:, at], xT[s][:, at], wu[:], start=False, stop=True)
                        pe_[s].mark(last, "h")
                    for s in range(S):
                        pe.wait_ge(ac[s].sem, ac[s].done(i, "h"))
                        for b in range(GB):
                            last = pe.matmul(bank[s][2 + b // 2][:, b % 2 * (P + 1):(b % 2 + 1) * (P + 1)], adj_f[s][:, b, :],
                                             ha[s][:, b, :], start=True, stop=True)
                        pe_[s].mark(last, "msg")


def edge_gates(c):
    nc, io, turns = c.nc, c.io, c.turns
    xg, sg = c.grouped(c.x), c.grouped(c.stats)
    meang, rstdg = c.grouped(c.mean), c.grouped(c.rstd)
    adjg = io["adj"].rearrange("(g b) i j -> g i b j", b=GB)
    K = 4
    with ExitStack() as ctx:
        sb = lambda name, shape, dt=F32: c.sb("eg_" + name, shape, dt, ctx)
        a, bias = sb("a", [P, K]), sb("bias", [1, P])
        adj_i = [sb(f"adj_i{s}", [P, GB, P], I32) for s in range(S)]
        adj_f = [sb(f"adj_f{s}", [P, GB, P]) for s in range(S)]
        xn = [sb(f"xn{s}", [P, GB, P]) for s in range(S)]
        xT = [sb(f"xT{s}", [P, T]) for s in range(S)]
        ax = [sb(f"ax{s}", [P, K, T]) for s in range(S)]
        adjT = [sb(f"adjT{s}", [P, GB, P]) for s in range(S)]
        kind = [sb(f"kind{s}", [P, K, GB, P], I32) for s in range(S)]
        known = [sb(f"known{s}", [P, GB, P]) for s in range(S)]
        e = [sb(f"e{s}", [P, GB, P]) for s in range(S)]
        bank = [c.ps(f"eg_bank{s}", ctx, (P, 4, T)) for s in range(S)]
        loaded, chain, powed = (c.sem("eg_" + n) for n in ("loaded", "chain", "powed"))
        adj_in = [c.sem(f"eg_adj_in{s}") for s in range(S)]
        dv = [Steps(c.sem(f"eg_dve{s}"), "adj xn known kinds mask ax first pick1 pick2 pick3 leaky alpha x") for s in range(S)]
        ac = [Steps(c.sem(f"eg_act{s}"), "xT adjT sigmoid") for s in range(S)]
        pe_ = [Steps(c.sem(f"eg_pe{s}"), "xT adjT e out") for s in range(S)]
        wide = "p (b f) -> p b f"
        with nc.Block() as block:

            @block.sync
            def _(sp):
                for k in range(K):
                    sp.dma_start(a[:, k:k + 1], io[f"L3_gnn_a{k}"], allow_slow_non_contiguous=True).then_inc(loaded, 16)
                sp.dma_start(bias[:], io["L3_gnn_bias"].rearrange("(o d) -> o d", o=1)).then_inc(loaded, 16)
                with sp.Fori(0, turns) as i:
                    for s in range(S):
                        sp.wait_ge(dv[s].sem, dv[s].all_done(i))
                        sp.dma_start(adj_i[s][:], adjg[i * S + s]).then_inc(adj_in[s], 16)

            @block.gpsimd
            def _(pool):
                ln_pool(c, pool, powed, False)

            @block.scalar
            def _(act):
                for s in range(S):
                    ac[s].start(act)
                with act.Fori(0, turns) as i:
                    for s in range(S):
                        act.wait_ge(pe_[s].sem, pe_[s].done(i, "xT"))
                        ac[s].mark(act.activation(xT[s][:], bank[s][:, 0, :], ACT.Copy), "xT")
                        act.wait_ge(pe_[s].sem, pe_[s].done(i, "adjT"))
                        ac[s].mark(act.activation(adjT[s][:], bank[s][:, 1, :].rearrange(wide, b=GB), ACT.Copy), "adjT")
                    for s in range(S):
                        act.wait_ge(dv[s].sem, dv[s].done(i, "leaky"))
                        ac[s].mark(act.activation(e[s][:], e[s][:], ACT.Sigmoid), "sigmoid")

            @block.vector
            def _(dve):
                for s in range(S):
                    dv[s].start(dve)
                ln_dve(c, dve, Chain(dve, chain), powed, False)
                dve.wait_ge(loaded, 80)
                with dve.Fori(0, turns) as i:
                    for s in range(S):
                        dve.wait_ge(adj_in[s], i * 16 + 16)
                        dv[s].mark(dve.tensor_copy(adj_f[s][:], adj_i[s][:]), "adj")
                        for b in range(GB):
                            last = dve.tensor_scalar(xn[s][:, b, :], xg[:, i * S + s, b, :], meang[:, i * S + s, b:b + 1],
                                                     rstdg[:, i * S + s, b:b + 1], ALU.subtract, ALU.mult)
                        dv[s].mark(last, "xn")
                    for s in range(S):
                        dve.wait_ge(ac[s].sem, ac[s].done(i, "adjT"))
                        dv[s].mark(dve.tensor_scalar(known[s][:], adjT[s][:], 1.0, None, ALU.is_ge), "known")
                        for k in range(1, K):
                            last = dve.tensor_scalar(kind[s][:, k, :, :], adjT[s][:], float(k + 1), None, ALU.is_equal)
                        dv[s].mark(last, "kinds")
                        dve.wait_ge(dv[s].sem, dv[s].done(i, "known"))
                        dv[s].mark(dve.scalar_tensor_tensor(known[s][:], adjT[s][:], float(K), known[s][:], ALU.is_le, ALU.mult),
                                   "mask")
                        for k in range(K):
                            last = dve.tensor_scalar(ax[s][:, k, :], xT[s][:], a[:, k:k + 1], None, ALU.mult)
                        dv[s].mark(last, "ax")
                    for s in range(S):
                        dve.wait_ge(pe_[s].sem, pe_[s].done(i, "e"))
                        ek = lambda k: bank[s][:, :, k * P:(k + 1) * P]
                        dv[s].mark(dve.tensor_copy(e[s][:], ek(0)), "first")
                        for k in range(1, K):
                            dve.wait_ge(dv[s].sem, dv[s].done(i, "first" if k == 1 else f"pick{k - 1}"))
                            dve.memset(c.pace[:], 0.0)
                            dv[s].mark(dve.copy_predicated(e[s][:], kind[s][:, k, :, :], ek(k)), f"pick{k}")
                        dve.wait_ge(dv[s].sem, dv[s].done(i, f"pick{K - 1}"))
                        dv[s].mark(dve.scalar_tensor_tensor(e[s][:], e[s][:], 0.2, e[s][:], ALU.mult, ALU.max), "leaky")
                    for s in range(S):
                        dve.wait_ge(ac[s].sem, ac[s].done(i, "sigmoid"))
                        dv[s].mark(dve.tensor_tensor(e[s][:], e[s][:], known[s][:], ALU.mult), "alpha")
                    for s in range(S):
                        dve.wait_ge(pe_[s].sem, pe_[s].done(i, "out"))
                        dv[s].mark(dve.tensor_tensor(xg[:, i * S + s, :, :], xg[:, i * S + s, :, :],
                                                     bank[s][:, 0, :].rearrange(wide, b=GB), ALU.add), "x")
                        dve.wait_ge(dv[s].sem, dv[s].done(i, "x"))
                        for b in range(GB):
                            dve.bn_stats(sg[:, i * S + s, b, :], xg[:, i * S + s, b, :])

            @block.tensor
            def _(pe):
                for s in range(S):
                    pe_[s].start(pe)
                pe.wait_ge(loaded, 80)
                with pe.Fori(0, turns) as i:
                    for s in range(S):
                        pe.wait_ge(dv[s].sem, dv[s].done(i, "xn"))
                        for b in range(GB):
                            last = pe.transpose(bank[s][:, 0, b * P:(b + 1) * P], xn[s][:, b, :], c.ident[:])
                        pe_[s].mark(last, "xT")
                        for b in range(GB):
                            last = pe.transpose(bank[s][:, 1, b * P:(b + 1) * P], adj_f[s][:, b, :], c.ident[:])
                        pe_[s].mark(last, "adjT")
                    for s in range(S):
                        pe.wait_ge(dv[s].sem, dv[s].done(i, "ax"))
                        for b in range(GB):
                            at = slice(b * P, (b + 1) * P)
                            last = pe.matmul(bank[s][:, b, :], xT[s][:, at], ax[s][:, :, at], start=True, stop=True)
                        pe_[s].mark(last, "e")
                    for s in range(S):
                        pe.wait_ge(dv[s].sem, dv[s].done(i, "alpha"))
                        for b in range(GB):
                            out = bank[s][:, 0, b * P:(b + 1) * P]
                            pe.matmul(out, c.ones[0:1, :], bias[:], start=True, stop=False)
                            last = pe.matmul(out, e[s][:, b, :], xn[s][:, b, :], start=False, stop=True)
                        pe_[s].mark(last, "out")


SH = 8
SP = P // 2
CK = 4
CONV = 3
Z0, X0, B0, C0, B1, DT0, IN_COLS = 0, 512, 1024, 1088, 1152, 1216, 1232


def slices(c):
    nc, io = c.nc, c.io
    xg, sg = c.grouped(c.x), c.grouped(c.stats)
    meang, rstdg = c.grouped(c.mean), c.grouped(c.rstd)
    PAIRS = GB // 2
    W = 2 * P
    row = lambda v: v.rearrange("(o d) -> o d", o=1)
    with ExitStack() as ctx:
        sb = lambda name, shape, dt=F32: c.sb("sl_" + name, shape, dt, ctx)
        sem = lambda name: c.sem("sl_" + name)
        in_t, ho_t, ow_t, fc_t = sb("in_t", [P, CK, IN_COLS]), sb("ho_t", [P, CK, CK * P]), sb("ow_t", [P, CK, P]), sb("fc_t", [P, CK, SH])
        fx_t, wc, bc, bfx = sb("fx_t", [P, CK, P]), sb("wc", [P, SH, SP]), sb("bc", [P, SH, SP]), sb("bfx", [P, CK * P])
        cw, cb = sb("cw", [P, 6, CONV]), sb("cb", [P, 6])
        ob = sb("ob", [1, P])
        heads_all = sb("heads_all", [P, 5, SH])
        a2 = sb("a2", [P, 2, SH])
        up, low = sb("up", [P, SP]), sb("low", [P, SP])
        seg_f, seg_b = sb("seg_f", [P, P]), sb("seg_b", [P, P])
        xn, xT = sb("xn", [P, GB, P]), sb("xT", [P, T])
        sw = [sb(f"sw{b}", [P, SH, SP]) for b in range(GB)]
        fx = [sb(f"fx{b}", [P, CK * P]) for b in range(2)]
        rs = sb("rs", [P, CK])
        inv = sb("inv", [P, CK, SP])
        eye2, same = sb("eye2", [P, SP]), sb("same", [P, P])
        mx, sm = sb("mx", [P, GB, SH]), sb("sm", [P, GB, SH])
        st = [sb(f"st{u}", [P, CK, GB, SP]) for u in range(2)]
        swT = [sb(f"swT{u}", [P, GB, CK, P]) for u in range(2)]
        zs = [sb(f"zs{q}", [P, CK * P]) for q in range(PAIRS)]
        xa, xe = sb("xa", [P, 6, GB, SP]), sb("xe", [P, 6, GB, SP])
        dt, dn, de, dl, du, dc = (sb(n, [P, PAIRS, 2, SH]) for n in ("dt", "dn", "de", "dl", "du", "dc"))
        seg_rhs = [sb(f"seg_rhs{k}", [P, SH, SP]) for k in range(2)]
        dec = [sb(f"dec{q}", [P, SH, SP]) for q in range(PAIRS)]
        bcp = [sb(f"bcp{q}", [P, SP + 2]) for q in range(PAIRS)]
        gu, gd = sb("gu", [P, SP]), sb("gd", [P, SP])
        m1, m2 = sb("m1", [P, SH, SP]), sb("m2", [P, SH, SP])
        mb = [sb(f"mb{q}", [P, SH, P]) for q in range(PAIRS)]
        fcd = sb("fcd", [P, PAIRS, SH])
        xs = [sb(f"xs{q}", [P, SH, SP]) for q in range(PAIRS)]
        y = [sb(f"y{q}", [P, CK * P]) for q in range(PAIRS)]
        ms, rms = sb("ms", [P, PAIRS]), sb("rms", [P, PAIRS])
        yT = sb("yT", [P, CK, PAIRS, P])
        otb = sb("otb", [P, CK, GB, P])
        zz = [sb(f"zz{k}", [P, CK, P]) for k in range(2)]
        bank = [c.ps(f"sl_bank{k}", ctx) for k in range(8)]
        heads8 = lambda ap: ap.rearrange("p (h f) -> p h f", h=SH)

        rows_up, rows_read = sem("rows_up"), sem("rows_read")
        small_in, pre, masks, chain, powed = sem("small_in"), sem("pre"), sem("masks"), sem("chain"), sem("powed")
        with ExitStack() as ctx2:
            sb2 = lambda name, shape, dt=F32: c.sb("sw_" + name, shape, dt, ctx2)
            rows = [sb2(f"rows{k}", [P, CK * P]) for k in range(2)]
            rows_in = [sem(f"rows_in{k}") for k in range(2)]
            vec_rows, vecs = sb2("vec_rows", [2 * CK, P]), sb2("vecs", [P, 2 * CK])
            ws2, wsT = sb2("ws2", [SP, 2, SP]), sb2("wsT", [P, SP])
            wx = sb2("wx", [P, CK, P])
            heads_row = sb2("heads_row", [1, 5, SH])
            bfx_row, bs_row, bs_all = sb2("bfx_row", [1, CK * P]), sb2("bs_row", [1, SP]), sb2("bs_all", [P, SP])
            bx_wide = sb2("bx_wide", [P, CK, P])
            cols = [(io["L2_ffn_hy_in_w"][128 * k:128 * k + 128, :], P, in_t[:, :, 128 * k:128 * k + 128]) for k in range(9)]
            cols += [(io["L2_ffn_hy_in_w"][1152:1168, :], 16, in_t[:, :, DT0:DT0 + 16]),
                     (io["L2_ffn_hy_in_w"][B0:C0, :], SP, in_t[:, :, B1:B1 + SP])]
            cols += [(io["L2_ffn_hy_out_w"][128 * k:128 * k + 128, :], P, ho_t[:, :, 128 * k:128 * k + 128]) for k in range(4)]
            cols += [(io["L2_ffn_out_w"], P, ow_t[:]), (io["L2_ffn_hy_fcD_w"], SH, fc_t[:]),
                     (io["L2_ffn_W_fx"].rearrange("(j p) d -> p j d", p=P), P, fx_t[:])]
            conv_w, conv_b = io["L2_ffn_hy_conv_w"], io["L2_ffn_hy_conv_b"].rearrange("(c o) -> c o", o=1)
            smalls = [(vec_rows[0:CK, :], io["L2_ffn_hy_norm_w"].rearrange("(k p) -> k p", p=P)),
                      (vec_rows[CK:2 * CK, :], io["L2_ffn_b_x"].rearrange("(k p) -> k p", p=P)),
                      (ws2[:, 0, :], io["L2_ffn_W_slice"]), (ws2[:, 1, :], io["L2_ffn_W_slice"]),
                      (wx[:], io["L2_ffn_W_x"].rearrange("(j p) d -> p j d", p=P)),
                      (heads_row[:, 0, :], io["L2_ffn_temperature"].rearrange("a h b c -> a (h b c)")),
                      (heads_row[:, 1, :], row(io["L2_ffn_hy_D"])), (heads_row[:, 2, :], row(io["L2_ffn_hy_dt_bias"])),
                      (heads_row[:, 3, :], row(io["L2_ffn_hy_dt_bias"])), (heads_row[:, 4, :], row(io["L2_ffn_hy_A_log"])),
                      (bfx_row[:], row(io["L2_ffn_b_fx"])), (bs_row[:], row(io["L2_ffn_b_slice"])),
                      (ob[:], row(io["L2_ffn_out_b"]))]
            for j in range(4):
                smalls += [(cw[:, j, :], conv_w[128 * j:128 * j + 128, :]), (cb[:, j:j + 1], conv_b[128 * j:128 * j + 128, :])]
            for p0, j, ch0 in ((0, 4, 512), (SP, 4, 576), (0, 5, 576), (SP, 5, 512)):
                smalls += [(cw[p0:p0 + SP, j, :], conv_w[ch0:ch0 + SP, :]), (cb[p0:p0 + SP, j:j + 1], conv_b[ch0:ch0 + SP, :])]
            with nc.Block() as block:

                @block.sync
                def _(sp):
                    for dst, src in smalls:
                        sp.dma_start(dst, src, allow_slow_non_contiguous=True).then_inc(small_in, 16)
                    for k, (src, n, _) in enumerate(cols):
                        if k >= 2:
                            sp.wait_ge(rows_up, k - 1)
                        dst = rows[k % 2][0:n, :]
                        if len(src.shape) == 3:
                            dst = dst.rearrange("p (j d) -> p j d", d=P)
                        sp.dma_start(dst, src).then_inc(rows_in[k % 2], 16)

                @block.gpsimd
                def _(pool):
                    link = Chain(pool, masks).link
                    pool.memset(up[:], 1.0)
                    pool.memset(low[:], 1.0)
                    pool.memset(seg_f[:], 0.0)
                    pool.memset(seg_b[:], 0.0)
                    for q in range(PAIRS):
                        pool.memset(mb[q][:], 0.0)
                        pool.memset(bcp[q][:], 0.0)
                    pool.memset(same[:], 0.0)
                    link(pool.memset(otb[:], 0.0))
                    for r in range(2):
                        half = slice(SP * r, SP * r + SP)
                        link(pool.affine_select(out=up[half, :], in_=up[half, :], compare_op=ALU.is_gt, fill=0.0, base=0,
                                                pattern=[[1, SP]], channel_multiplier=-1))
                        link(pool.affine_select(out=low[half, :], in_=low[half, :], compare_op=ALU.is_gt, fill=0.0, base=0,
                                                pattern=[[-1, SP]], channel_multiplier=1))
                    for r in range(2):
                        half = slice(SP * r, SP * r + SP)
                        link(pool.tensor_copy(seg_f[half, half], low[half, :]))
                        link(pool.tensor_copy(seg_b[half, half], up[half, :]))
                        link(pool.tensor_copy(same[half, half], c.ones[half, half]))
                        link(pool.tensor_copy(eye2[half, :], c.ident[half, half]))
                    ln_pool(c, pool, powed, False)

                @block.scalar
                def _(act):
                    for k, (_, n, dst) in enumerate(cols):
                        act.wait_ge(rows_up, k + 1)
                        act.activation(dst, bank[k % 2][:].rearrange("p (j n) -> p j n", j=CK)[:, :, 0:n], ACT.Copy).then_inc(rows_read, 1)
                    act.wait_ge(pre, 4)
                    for k in range(2):
                        act.activation(a2[:, k, :], heads_all[:, 4, :], ACT.Exp)

                @block.vector
                def _(dve):
                    link = Chain(dve, chain)
                    ln_dve(c, dve, link, powed, False)
                    link = link.link
                    dve.wait_ge(small_in, 16 * len(smalls))
                    link(dve.tensor_scalar(heads_row[:, 0, :], heads_row[:, 0, :], 1e-6, None, ALU.max))
                    dve.reciprocal(heads_row[:, 0, :], heads_row[:, 0, :]).then_inc(pre, 1)
                    dve.wait_ge(pre, 2)
                    dve.tensor_copy(vecs[:], bank[2][:, 0:2 * CK])
                    dve.tensor_copy(wsT[:], bank[3][:, 0:SP])
                    dve.tensor_copy(heads_all[:].rearrange("p k h -> p (k h)"), bank[4][:, 0:5 * SH])
                    dve.tensor_copy(bfx[:], bank[5][:])
                    link(dve.tensor_copy(bs_all[:], bank[6][:, 0:SP]))
                    for k in range(CK):
                        dve.tensor_scalar(bx_wide[:, k, :], c.ones[:], vecs[:, CK + k:CK + k + 1], None, ALU.mult)
                    dve.drain().then_inc(pre, 2)
                    dve.wait_ge(pre, 5)
                    for r in range(2):
                        for n, dst in ((2, wc), (4, bc)):
                            half = dst[:].rearrange("p (k r) g -> p r k g", r=2)[:, r, :, :]
                            temp = heads_all[:, 0, :].rearrange("p (k r) -> p r k", r=2)[:, r, :].unsqueeze(2).to_broadcast([P, CK, SP])
                            src = bank[n + r][:, 0:CK * SP].rearrange("p (k g) -> p k g", k=CK)
                            if dst is bc:
                                link(dve.tensor_tensor(half, src, bs_all[:].unsqueeze(1).to_broadcast([P, CK, SP]), ALU.add))
                                src = half
                            link(dve.tensor_tensor(half, src, temp, ALU.mult))
                    dve.wait_ge(rows_read, len(cols))
                    for k in range(CK):
                        dve.tensor_scalar(ho_t[:, k, :], ho_t[:, k, :], vecs[:, k:k + 1], None, ALU.mult)

                @block.tensor
                def _(pe):
                    pe.wait_ge(small_in, 16 * len(smalls))
                    pe.wait_ge(pre, 1)
                    pe.transpose(bank[2][:, 0:2 * CK], vec_rows[:], c.ident[0:2 * CK, 0:2 * CK])
                    pe.transpose(bank[3][:, 0:SP], ws2[:].rearrange("g r c -> g (r c)"), c.ident[0:SP, 0:SP])
                    pe.matmul(bank[4][:, 0:5 * SH], c.ones[0:1, :], heads_row[:].rearrange("p k h -> p (k h)"), start=True, stop=True)
                    pe.matmul(bank[5][:], c.ones[0:1, :], bfx_row[:], start=True, stop=True)
                    pe.matmul(bank[6][:, 0:SP], c.ones[0:1, :], bs_row[:], start=True, stop=True).then_inc(pre, 1)
                    pe.wait_ge(pre, 4)
                    for r in range(2):
                        half = slice(SP * r, SP * r + SP)
                        for k in range(CK):
                            at = slice(SP * k, SP * k + SP)
                            pe.matmul(bank[2 + r][:, at], wx[half, k, :], wsT[half, :], start=True, stop=True)
                            last = pe.matmul(bank[4 + r][:, at], bx_wide[half, k, :], wsT[half, :], start=True, stop=True)
                    last.then_inc(pre, 1)
                    for k, (_, n, _) in enumerate(cols):
                        pe.wait_ge(rows_in[k % 2], 16 * (k // 2 + 1))
                        if k >= 2:
                            pe.wait_ge(rows_read, k - 1)
                        for j in range(CK):
                            last = pe.transpose(bank[k % 2][:, j * P:j * P + n], rows[k % 2][0:n, j * P:(j + 1) * P], c.ident[0:n, 0:n])
                        last.then_inc(rows_up, 1)

        per = lambda names, n: " ".join(f"{k}{b}" for b in range(n) for k in names.split())
        two = lambda names: " ".join(f"{k}{b}" for k in names.split() for b in range(GB))
        xn_ready = Count(sem("xn_ready"), 1)
        av = Steps(sem("a_dve"), two("logit max") + " " + two("sum") + " rsum " + per("fx norm rnorm inv st", GB))
        aa = Steps(sem("a_act"), "xT " + two("exp") + " " + two("swT"))
        ap = Steps(sem("a_pe"), "xT " + two("logit") + " " + per("swT fx total st inv", GB))
        ag = Steps(sem("a_pool"), two("sub") + " " + two("sw"))
        bv = Steps(sem("b_dve"), "zs0 zs1 tap1 tap2 tap45 dt dneg dabs x du dd dc dru dcr dsum dt2 da seg0b seg1b "
                   + "bcp0 g0 m0 mm0 bcp1 g1 m1 mm1 fcd y0 y1 yg0 yg1 mean ygn0 ygn1 ot x_out")
        ba = Steps(sem("b_act"), "z0 z1 xa xa45 xe de dl dec0 dec1 xs0 xs1 ms0 ms1 yT0 yT1 " + two("z_"))
        bp = Steps(sem("b_pe"), "z0 z1 xbc dtbc seg0 seg1 bc0 bc1 fcd xs0 xs1 y0 y1 yT0 yT1 ot z_0 z_1 out0 z_2 out1 z_3 out2 out3")
        bg = Steps(sem("b_pool"), "seg0f seg1f m20 m21 xf0 xf1 rms")

        wide = [P, SH, SP]
        over_t = lambda v: v.unsqueeze(2).to_broadcast(wide)
        over_h = lambda v: v.unsqueeze(1).to_broadcast(wide)
        pair = lambda q: slice(2 * q, 2 * q + 2)
    
        with nc.Block() as block:

            @block.scalar
            def _(act):
                aa.start(act)
                ba.start(act)
                def turn(g):
                    act.wait_ge(ap.sem, ap.done(g, "xT"))
                    aa.mark(act.activation(xT[:], bank[4][:], ACT.Copy), "xT")

                def soften(g):
                    for b in range(GB):
                        act.wait_ge(ag.sem, ag.done(g, f"sub{b}"))
                        aa.mark(act.activation(sw[b][:], sw[b][:], ACT.Exp), f"exp{b}")

                def copy_weights(g, u, b, before=None):
                    act.wait_ge(ap.sem, ap.done(g, f"swT{b}"))
                    if b == 0 and before is not None:
                        act.wait_ge(bv.sem, bv.all_done(before))
                    aa.mark(act.activation(swT[u][:, b, :, :], bank[4][:].rearrange("p (k n) -> p k n", k=CK), ACT.Copy),
                            f"swT{b}")

                def convolve(g):
                    for q in range(PAIRS):
                        act.wait_ge(bp.sem, bp.done(g, f"z{q}"))
                        ba.mark(act.activation(zs[q][:], bank[q][:], ACT.Sigmoid), f"z{q}")
                    act.wait_ge(bp.sem, bp.done(g, "xbc"))
                    for j in range(4):
                        last = act.activation(xa[:, j, :, :], bank[2 + j // 2][:, j % 2 * W:(j % 2 + 1) * W].rearrange("p (b t) -> p b t", b=GB),
                                              ACT.Identity, bias=cb[:, j:j + 1], scale=cw[:, j, 2:3])
                    ba.mark(last, "xa")
                    act.wait_ge(bp.sem, bp.done(g, "dtbc"))
                    for j in range(4, 6):
                        last = act.activation(xa[:, j, :, :], bank[0][:, j % 2 * W:(j % 2 + 1) * W].rearrange("p (b t) -> p b t", b=GB),
                                              ACT.Identity, bias=cb[:, j:j + 1], scale=cw[:, j, 2:3])
                    ba.mark(last, "xa45")
                    act.wait_ge(bv.sem, bv.done(g, "tap45"))
                    ba.mark(act.activation(xe[:], xa[:], ACT.Sigmoid), "xe")

                def steps(g):
                    act.wait_ge(bv.sem, bv.done(g, "dabs"))
                    ba.mark(act.activation(de[:], dn[:], ACT.Exp, scale=-1.0), "de")
                    act.wait_ge(bv.sem, bv.done(g, "du"))
                    ba.mark(act.activation(dl[:], du[:], ACT.Ln), "dl")

                def model(g):
                    for q in range(PAIRS):
                        act.wait_ge(bp.sem, bp.done(g, f"seg{q}"))
                        ba.mark(act.activation(dec[q][:], heads8(bank[2 + q][:]), ACT.Exp, scale=-1.0), f"dec{q}")
                    for q in range(PAIRS):
                        act.wait_ge(bp.sem, bp.done(g, f"xs{q}"))
                        ba.mark(act.activation(xs[q][:], heads8(bank[2 + q][:]), ACT.Copy), f"xs{q}")

                def squares(g):
                    for q in range(PAIRS):
                        act.wait_ge(bv.sem, bv.done(g, f"yg{q}"))
                        ba.mark(act.activation(zs[q][:], y[q][:], ACT.Square, accum_out=ms[:, q:q + 1]), f"ms{q}")

                def turn_y(g):
                    for q in range(PAIRS):
                        act.wait_ge(bp.sem, bp.done(g, f"yT{q}"))
                        ba.mark(act.activation(yT[:, :, q, :], bank[2 + q][:].rearrange("p (k n) -> p k n", k=CK), ACT.Copy), f"yT{q}")

                def spread(g):
                    for b in range(GB):
                        act.wait_ge(bp.sem, bp.done(g, f"z_{b}"))
                        if b >= 2:
                            act.wait_ge(bp.sem, bp.done(g, f"out{b - 2}"))
                        ba.mark(act.activation(zz[b % 2][:], bank[2 + b % 2][:].rearrange("p (k n) -> p k n", k=CK), ACT.Copy),
                                f"z_{b}")

                turn(0)
                soften(0)
                for b in range(GB):
                    copy_weights(0, 0, b)
                turn(1)
                soften(1)
                with act.Fori(0, c.turns) as i:
                    for u in range(2):
                        g = i * 2 + u
                        convolve(g)
                        steps(g)
                        copy_weights(g + 1, 1 - u, 0, g)
                        copy_weights(g + 1, 1 - u, 1)
                        model(g)
                        copy_weights(g + 1, 1 - u, 2)
                        copy_weights(g + 1, 1 - u, 3)
                        turn(g + 2)
                        squares(g)
                        turn_y(g)
                        spread(g)
                        soften(g + 2)

            @block.gpsimd
            def _(pool):
                ag.start(pool)
                bg.start(pool)
                def soften(g):
                    for b in range(GB):
                        pool.wait_ge(av.sem, av.done(g, f"max{b}"))
                        ag.mark(pool.tensor_tensor(sw[b][:], sw[b][:], over_t(mx[:, b, :]), ALU.subtract), f"sub{b}")

                def weights(g):
                    for b in range(GB):
                        pool.wait_ge(av.sem, av.done(g, "rsum"))
                        ag.mark(pool.tensor_tensor(sw[b][:], sw[b][:], over_t(sm[:, b, :]), ALU.mult), f"sw{b}")

                def model(g):
                    for q in range(PAIRS):
                        pool.wait_ge(bv.sem, bv.done(g, "da"))
                        if q:
                            pool.wait_ge(bp.sem, bp.done(g, f"seg{q - 1}"))
                        bg.mark(pool.tensor_tensor(seg_rhs[0][:], over_t(dn[:, q, 0, :]), over_h(up[:]), ALU.mult), f"seg{q}f")
                    for q in range(PAIRS):
                        pool.wait_ge(bv.sem, bv.done(g, f"g{q}"))
                        bg.mark(pool.tensor_tensor(m2[:], over_t(dt[:, q, 1, :]), over_h(gd[:]), ALU.mult), f"m2{q}")
                    for q in range(PAIRS):
                        pool.wait_ge(bv.sem, bv.done(g, "fcd"))
                        pool.wait_ge(ba.sem, ba.done(g, f"xs{q}"))
                        bg.mark(pool.tensor_tensor(heads8(y[q][:]), xs[q][:], over_t(fcd[:, q, :]), ALU.mult), f"xf{q}")
                    pool.wait_ge(bv.sem, bv.done(g, "mean"))
                    bg.mark(pool.tensor_tensor(rms[:], ms[:], c.mhalf[:, 0:PAIRS], ALU.pow), "rms")

                soften(0)
                weights(0)
                soften(1)
                with pool.Fori(0, c.turns) as i:
                    for u in range(2):
                        g = i * 2 + u
                        weights(g + 1)
                        model(g)
                        soften(g + 2)

            @block.vector
            def _(dve):
                av.start(dve)
                bv.start(dve)
                def own(steps, g, name):
                    dve.wait_ge(steps.sem, steps.done(g, name))

                def normalise(g, before=None):
                    if before is not None:
                        dve.wait_ge(ap.sem, ap.done(before, "xT"))
                    for b in range(GB):
                        last = dve.tensor_scalar(xn[:, b, :], xg[:, g, b, :], meang[:, g, b:b + 1], rstdg[:, g, b:b + 1],
                                                 ALU.subtract, ALU.mult)
                    last.then_inc(xn_ready.sem, 1)

                def logits(g, batches):
                    for b in batches:
                        dve.wait_ge(ap.sem, ap.done(g, f"logit{b}"))
                        av.mark(dve.tensor_tensor(sw[b][:], heads8(bank[4 + b][:]), bc[:], ALU.add), f"logit{b}")

                def maxima(g):
                    for b in range(GB):
                        own(av, g, f"logit{b}")
                        av.mark(dve.tensor_reduce(mx[:, b, :], sw[b][:], AX_X, ALU.max), f"max{b}")

                def soften(g):
                    for b in range(GB):
                        dve.wait_ge(aa.sem, aa.done(g, f"exp{b}"))
                        av.mark(dve.tensor_reduce(sm[:, b, :], sw[b][:], AX_X, ALU.add), f"sum{b}")
                    own(av, g, f"sum{GB - 1}")
                    av.mark(dve.reciprocal(sm[:], sm[:]), "rsum")

                def lift(g, b):
                    dve.wait_ge(ap.sem, ap.done(g, f"fx{b}"))
                    av.mark(dve.tensor_tensor(fx[b % 2][:], bank[5][:], bfx[:], ALU.add), f"fx{b}")

                def totals(g, b):
                    dve.wait_ge(ap.sem, ap.done(g, f"total{b}"))
                    av.mark(dve.tensor_scalar(rs[:], bank[6][:, 0:CK], 1e-5, None, ALU.add), f"norm{b}")
                    own(av, g, f"norm{b}")
                    av.mark(dve.reciprocal(rs[:], rs[:]), f"rnorm{b}")
                    own(av, g, f"rnorm{b}")
                    av.mark(dve.tensor_tensor(inv[:], eye2[:].unsqueeze(1).to_broadcast([P, CK, SP]),
                                              rs[:].unsqueeze(2).to_broadcast([P, CK, SP]), ALU.mult), f"inv{b}")

                def slices_of(g, u, b):
                    dve.wait_ge(ap.sem, ap.done(g, f"inv{b}"))
                    for r in range(2):
                        half = slice(SP * r, SP * r + SP)
                        dve.tensor_copy(st[u][half, :, b, :], bank[7][half, :].rearrange("p (k r g) -> p k r g", k=CK, r=2)[:, :, r, :])
                    dve.drain()
                    av.mark(dve.tensor_tensor(st[u][:, :, b, :], st[u][:, :, b, :],
                                              bank[6][:, CK * SP:2 * CK * SP].rearrange("p (k g) -> p k g", k=CK), ALU.mult), f"st{b}")

                def gates(g):
                    for q in range(PAIRS):
                        dve.wait_ge(ba.sem, ba.done(g, f"z{q}"))
                        bv.mark(dve.tensor_tensor(zs[q][:], zs[q][:], bank[q][:], ALU.mult), f"zs{q}")

                def convolve(g):
                    dve.wait_ge(ba.sem, ba.done(g, "xa"))

                    def tap(j, k):
                        src = (bank[2 + j // 2] if j < 4 else bank[0])[:, j % 2 * W:(j % 2 + 1) * W].rearrange("p (b t) -> p b t", b=GB)
                        return dve.scalar_tensor_tensor(xa[:, j, :, k:SP], src[:, :, 0:SP - k], cw[:, j, 2 - k:3 - k],
                                                        xa[:, j, :, k:SP], ALU.mult, ALU.add)

                    for j in range(4):
                        last = tap(j, 1)
                    bv.mark(last, "tap1")
                    own(bv, g, "tap1")
                    for j in range(4):
                        last = tap(j, 2)
                    bv.mark(last, "tap2")
                    dve.wait_ge(ba.sem, ba.done(g, "xa45"))
                    for j in range(4, 6):
                        tap(j, 1)
                    dve.drain()
                    for j in range(4, 6):
                        last = tap(j, 2)
                    bv.mark(last, "tap45")
                    flat = lambda v: v[:].rearrange("p q k h -> p q (k h)")
                    bias = heads_all[:, 2:4, :].rearrange("p k h -> p (k h)").unsqueeze(1).to_broadcast([P, PAIRS, 2 * SH])
                    bv.mark(dve.tensor_tensor(flat(dt), bank[1][:, 0:2 * PAIRS * SH].rearrange("p (q k) -> p q k", q=PAIRS),
                                              bias, ALU.add), "dt")
                    own(bv, g, "dt")
                    bv.mark(dve.tensor_scalar(dn[:], dt[:], -1.0, None, ALU.mult), "dneg")
                    own(bv, g, "dneg")
                    bv.mark(dve.tensor_tensor(dn[:], dt[:], dn[:], ALU.max), "dabs")

                def silu(g):
                    dve.wait_ge(ba.sem, ba.done(g, "xe"))
                    bv.mark(dve.tensor_tensor(xa[:], xa[:], xe[:], ALU.mult), "x")

                def steps(g):
                    dve.wait_ge(ba.sem, ba.done(g, "de"))
                    bv.mark(dve.tensor_scalar(du[:], de[:], 1.0, None, ALU.add), "du")
                    own(bv, g, "du")
                    bv.mark(dve.tensor_scalar(dc[:], du[:], -1.0, None, ALU.add), "dd")
                    own(bv, g, "dd")
                    bv.mark(dve.tensor_tensor(dc[:], de[:], dc[:], ALU.subtract), "dc")
                    dve.wait_ge(ba.sem, ba.done(g, "dl"))
                    bv.mark(dve.reciprocal(du[:], du[:]), "dru")
                    own(bv, g, "dru")
                    bv.mark(dve.tensor_tensor(dc[:], dc[:], du[:], ALU.mult), "dcr")
                    own(bv, g, "dcr")
                    bv.mark(dve.tensor_tensor(dc[:], dc[:], dl[:], ALU.add), "dsum")
                    own(bv, g, "dsum")
                    bv.mark(dve.scalar_tensor_tensor(dt[:], dt[:], 0.0, dc[:], ALU.max, ALU.add), "dt2")
                    own(bv, g, "dt2")
                    bv.mark(dve.tensor_tensor(dn[:], dt[:], a2[:].unsqueeze(1).to_broadcast([P, PAIRS, 2, SH]), ALU.mult), "da")
                    own(bv, g, "da")
                    backward(g, 0)

                def backward(g, q):
                    if q:
                        dve.wait_ge(bp.sem, bp.done(g, f"seg{q - 1}"))
                    bv.mark(dve.tensor_tensor(seg_rhs[1][:], over_t(dn[:, q, 1, :]), over_h(low[:]), ALU.mult), f"seg{q}b")

                def model(g, q):
                    dve.wait_ge(bp.sem, bp.done(g, f"bc{PAIRS - 1}"))
                    for r in range(2):
                        half = slice(SP * r, SP * r + SP)
                        last = dve.tensor_copy(bcp[q][half, 1:SP + 1], bank[0][half, q * P + SP * r:q * P + SP * r + SP])
                    bv.mark(last, f"bcp{q}")
                    own(bv, g, f"bcp{q}")
                    if q:
                        dve.wait_ge(bg.sem, bg.done(g, f"m2{q - 1}"))
                    dve.tensor_tensor(gu[:], bcp[q][:, 0:SP], up[:], ALU.mult)
                    bv.mark(dve.tensor_tensor(gd[:], bcp[q][:, 2:SP + 2], low[:], ALU.mult), f"g{q}")
                    own(bv, g, f"g{q}")
                    dve.tensor_tensor(m1[:], over_t(dt[:, q, 0, :]), over_h(gu[:]), ALU.mult)
                    dve.drain()
                    dve.wait_ge(bg.sem, bg.done(g, f"m2{q}"))
                    bv.mark(dve.tensor_tensor(m1[:], m1[:], m2[:], ALU.add), f"m{q}")
                    own(bv, g, f"m{q}")
                    dve.wait_ge(ba.sem, ba.done(g, f"dec{q}"))
                    for r in range(2):
                        half = slice(SP * r, SP * r + SP)
                        last = dve.tensor_tensor(mb[q][half, :, half], m1[half, :, :], dec[q][half, :, :], ALU.mult)
                    bv.mark(last, f"mm{q}")

                def skips(g):
                    dve.wait_ge(bp.sem, bp.done(g, "fcd"))
                    bv.mark(dve.tensor_tensor(fcd[:], bank[1][:, 64:64 + PAIRS * SH].rearrange("p (q h) -> p q h", q=PAIRS),
                                              heads_all[:, 1:2, :].to_broadcast([P, PAIRS, SH]), ALU.add), "fcd")

                def gate(g):
                    for q in range(PAIRS):
                        dve.wait_ge(bp.sem, bp.done(g, f"y{q}"))
                        dve.wait_ge(bg.sem, bg.done(g, f"xf{q}"))
                        bv.mark(dve.tensor_tensor(y[q][:], y[q][:], bank[q][:], ALU.add), f"y{q}")
                    for q in range(PAIRS):
                        own(bv, g, f"y{q}")
                        bv.mark(dve.tensor_tensor(y[q][:], y[q][:], zs[q][:], ALU.mult), f"yg{q}")

                def scale(g):
                    dve.wait_ge(ba.sem, ba.done(g, f"ms{PAIRS - 1}"))
                    bv.mark(dve.tensor_scalar(ms[:], ms[:], 1.0 / (CK * P), EPS, ALU.mult, ALU.add), "mean")
                    dve.wait_ge(bg.sem, bg.done(g, "rms"))
                    for q in range(PAIRS):
                        bv.mark(dve.tensor_scalar(y[q][:], y[q][:], rms[:, q:q + 1], None, ALU.mult), f"ygn{q}")

                def turned(g):
                    dve.wait_ge(bp.sem, bp.done(g, "ot"))
                    for j in range(0, CK, 2):
                        for r in range(2):
                            half = slice(SP * r, SP * r + SP)
                            last = dve.tensor_copy(otb[half, j:j + 2, :, half],
                                                   bank[j // 2][half, :].rearrange("p (j b t) -> p j b t", j=2, b=GB))
                    bv.mark(last, "ot")

                def finish(g):
                    dve.wait_ge(bp.sem, bp.done(g, f"out{GB - 1}"))
                    bv.mark(dve.tensor_tensor(xg[:, g, :, :], xg[:, g, :, :], bank[0][:].rearrange("p (b f) -> p b f", b=GB), ALU.add),
                            "x_out")
                    own(bv, g, "x_out")
                    for b in range(GB):
                        dve.bn_stats(sg[:, g, b, :], xg[:, g, b, :])

                normalise(0)
                logits(0, range(GB))
                maxima(0)
                soften(0)
                for b in range(GB):
                    lift(0, b)
                    totals(0, b)
                    slices_of(0, 0, b)
                normalise(1, 0)
                logits(1, range(GB))
                maxima(1)
                with dve.Fori(0, c.turns) as i:
                    for u in range(2):
                        g = i * 2 + u
                        n = g + 1
                        normalise(g + 2, n)
                        gates(g)
                        soften(n)
                        convolve(g)
                        lift(n, 0)
                        totals(n, 0)
                        silu(g)
                        steps(g)
                        slices_of(n, 1 - u, 0)
                        lift(n, 1)
                        totals(n, 1)
                        backward(g, 1)
                        slices_of(n, 1 - u, 1)
                        lift(n, 2)
                        totals(n, 2)
                        slices_of(n, 1 - u, 2)
                        model(g, 0)
                        lift(n, 3)
                        totals(n, 3)
                        model(g, 1)
                        skips(g)
                        slices_of(n, 1 - u, 3)
                        gate(g)
                        scale(g)
                        logits(g + 2, range(2))
                        turned(g)
                        logits(g + 2, range(2, 3))
                        finish(g)
                        logits(g + 2, range(3, GB))
                        maxima(g + 2)

            @block.tensor
            def _(pe):
                ap.start(pe)
                bp.start(pe)
                def turn(g):
                    pe.wait_ge(xn_ready.sem, xn_ready.done(g))
                    pe.wait_ge(aa.sem, aa.all_done(g))
                    for b in range(GB):
                        last = pe.transpose(bank[4][:, b * P:(b + 1) * P], xn[:, b, :], c.ident[:])
                    ap.mark(last, "xT")

                def logits(g, batches):
                    pe.wait_ge(aa.sem, aa.done(g, "xT"))
                    for b in batches:
                        ap.mark(pe.matmul(bank[4 + b][:], xT[:, b * P:(b + 1) * P], wc[:].rearrange("p h g -> p (h g)"),
                                          start=True, stop=True), f"logit{b}")

                def pool_tokens(g, b):
                    flat = sw[b][:].rearrange("p h g -> p (h g)")
                    pe.wait_ge(ag.sem, ag.done(g, f"sw{b}"))
                    if b:
                        pe.wait_ge(aa.sem, aa.done(g, f"swT{b - 1}"))
                    else:
                        pe.wait_ge(av.sem, av.done(g, f"logit{GB - 1}"))
                    for k in range(CK):
                        last = pe.transpose(bank[4][:, k * P:(k + 1) * P], flat[:, k * P:(k + 1) * P], c.ident[:])
                    ap.mark(last, f"swT{b}")
                    if b:
                        pe.wait_ge(av.sem, av.done(g, f"fx{b - 1}"))
                    ap.mark(pe.matmul(bank[5][:], xT[:, b * P:(b + 1) * P], fx_t[:].rearrange("p k c -> p (k c)"),
                                      start=True, stop=True), f"fx{b}")
                    if b:
                        pe.wait_ge(av.sem, av.done(g, f"st{b - 1}"))
                    for k in range(CK):
                        last = pe.matmul(bank[6][:, k:k + 1], flat[:, k * P:(k + 1) * P], c.ones[:, 0:1], start=True, stop=True)
                    ap.mark(last, f"total{b}")
                    pe.wait_ge(av.sem, av.done(g, f"fx{b}"))
                    for k in range(CK):
                        at = slice(k * P, (k + 1) * P)
                        last = pe.matmul(bank[7][:, at], fx[b % 2][:, at], flat[:, at], start=True, stop=True)
                    ap.mark(last, f"st{b}")
                    pe.wait_ge(av.sem, av.done(g, f"inv{b}"))
                    ap.mark(pe.matmul(bank[6][:, CK * SP:2 * CK * SP], same[:], inv[:].rearrange("p k g -> p (k g)"),
                                      start=True, stop=True), f"inv{b}")

                def project(g, u):
                    pe.wait_ge(av.sem, av.all_done(g + 1))
                    stf = st[u][:].rearrange("p k b t -> p k (b t)")
                    pe.wait_ge(bv.sem, bv.all_done(g))
                    for q in range(PAIRS):
                        for k in range(CK):
                            last = pe.matmul(bank[q][:], stf[:, k, q * P:(q + 1) * P], in_t[:, k, Z0:Z0 + 512],
                                             start=(k == 0), stop=(k == CK - 1))
                        bp.mark(last, f"z{q}")

                    def xbc(out, j):
                        for k in range(CK):
                            last = pe.matmul(out, in_t[:, k, X0 + P * j:X0 + P * (j + 1)] if j < 5 else in_t[:, k, C0:C0 + P],
                                             stf[:, k, :], start=(k == 0), stop=(k == CK - 1))
                        return last

                    for j in range(4):
                        last = xbc(bank[2 + j // 2][:, j % 2 * W:(j % 2 + 1) * W], j)
                    bp.mark(last, "xbc")
                    pe.wait_ge(bv.sem, bv.done(g, "zs1"))
                    for q in range(PAIRS):
                        for k in range(CK):
                            pe.matmul(bank[1][:, q * 2 * SH:(q + 1) * 2 * SH], stf[:, k, q * P:(q + 1) * P],
                                      in_t[:, k, DT0:DT0 + 2 * SH], start=(k == 0), stop=(k == CK - 1))
                    for j in range(4, 6):
                        last = xbc(bank[0][:, j % 2 * W:(j % 2 + 1) * W], j)
                    bp.mark(last, "dtbc")

                def decays(g):
                    for q in range(PAIRS):
                        pe.wait_ge(bg.sem, bg.done(g, f"seg{q}f"))
                        pe.wait_ge(bv.sem, bv.done(g, f"seg{q}b"))
                        pe.matmul(bank[2 + q][:], seg_f[:], seg_rhs[0][:].rearrange("p h t -> p (h t)"), start=True, stop=False)
                        bp.mark(pe.matmul(bank[2 + q][:], seg_b[:], seg_rhs[1][:].rearrange("p h t -> p (h t)"), start=False, stop=True),
                                f"seg{q}")

                def model(g):
                    xaf = xa[:].rearrange("p j b t -> p j (b t)")
                    for q in range(PAIRS):
                        at = slice(q * P, (q + 1) * P)
                        bp.mark(pe.matmul(bank[0][:, at], xaf[0:SP, 4, at], xaf[0:SP, 5, at], start=True, stop=True), f"bc{q}")
                    for q in range(PAIRS):
                        for k in range(CK):
                            last = pe.matmul(bank[1][:, 64 + q * SH:64 + (q + 1) * SH], xaf[:, k, q * P:(q + 1) * P], fc_t[:, k, :],
                                             start=(k == 0), stop=(k == CK - 1))
                    bp.mark(last, "fcd")
                    for q in range(PAIRS):
                        pe.wait_ge(ba.sem, ba.done(g, f"dec{q}"))
                        for k in range(CK):
                            last = pe.transpose(bank[2 + q][:, k * P:(k + 1) * P], xaf[:, k, q * P:(q + 1) * P], c.ident[:])
                        bp.mark(last, f"xs{q}")

                def weigh(g):
                    for q in range(PAIRS):
                        pe.wait_ge(bv.sem, bv.done(g, "fcd"))
                        pe.wait_ge(ba.sem, ba.done(g, f"xs{q}"))
                        for h in range(SH):
                            last = pe.matmul(bank[q][:, h * SP:(h + 1) * SP], mb[q][:, h, :], xs[q][:, h, :], start=True, stop=True)
                        bp.mark(last, f"y{q}")

                def project_back(g):
                    for q in range(PAIRS):
                        pe.wait_ge(bv.sem, bv.done(g, f"ygn{q}"))
                        for k in range(CK):
                            last = pe.transpose(bank[2 + q][:, k * P:(k + 1) * P], y[q][:, k * P:(k + 1) * P], c.ident[:])
                        bp.mark(last, f"yT{q}")
                    pe.wait_ge(ba.sem, ba.done(g, f"yT{PAIRS - 1}"))
                    for j in range(CK):
                        for k in range(CK):
                            last = pe.matmul(bank[j // 2][:, j % 2 * W:(j % 2 + 1) * W], ho_t[:, k, j * P:(j + 1) * P],
                                             yT[:, k, :, :].rearrange("p q n -> p (q n)"), start=(k == 0), stop=(k == CK - 1))
                    bp.mark(last, "ot")

                def spread_slices(g, u):
                    pe.wait_ge(aa.sem, aa.all_done(g + 1))
                    pe.wait_ge(bv.sem, bv.done(g, "ot"))

                    def spread(b):
                        pe.wait_ge(ba.sem, ba.done(g, f"z_{b}"))
                        out = bank[0][:, b * P:(b + 1) * P]
                        pe.matmul(out, c.ones[0:1, :], ob[:], start=True, stop=False)
                        for k in range(CK):
                            last = pe.matmul(out, swT[u][:, b, k, :], zz[b % 2][:, k, :], start=False, stop=(k == CK - 1))
                        bp.mark(last, f"out{b}")

                    for b in range(GB):
                        if b >= 2:
                            pe.wait_ge(ba.sem, ba.done(g, f"z_{b - 2}"))
                        for k in range(CK):
                            last = pe.matmul(bank[2 + b % 2][:, k * P:(k + 1) * P], otb[:, k, b, :], ow_t[:, k, :], start=True, stop=True)
                        bp.mark(last, f"z_{b}")
                        if b >= 1:
                            spread(b - 1)
                    spread(GB - 1)

                turn(0)
                logits(0, range(GB))
                for b in range(GB):
                    pool_tokens(0, b)
                turn(1)
                logits(1, range(GB))
                with pe.Fori(0, c.turns) as i:
                    for u in range(2):
                        g = i * 2 + u
                        project(g, u)
                        pool_tokens(g + 1, 0)
                        pool_tokens(g + 1, 1)
                        decays(g)
                        pool_tokens(g + 1, 2)
                        model(g)
                        pool_tokens(g + 1, 3)
                        turn(g + 2)
                        weigh(g)
                        logits(g + 2, range(2))
                        project_back(g)
                        logits(g + 2, range(2, 3))
                        spread_slices(g, u)
                        logits(g + 2, range(3, GB))

def store(c):
    stored = c.sem("stored")
    n = c.nb // 4
    with c.nc.Block() as block:

        @block.sync
        def _(sp):
            for k in range(4):
                sp.dma_start(c.io["out"][k * n:(k + 1) * n].rearrange("b n d -> n b d"),
                             c.x[:, k * n:(k + 1) * n, :]).then_inc(stored, 16)
            sp.wait_ge(stored, 64)


def network(nc, io, n_batch=64, phases=None):
    with ExitStack() as ctx:
        c = Chip(nc, ctx, io, n_batch)
        load_and_constants(c)
        for phase in phases or PHASES:
            c.sems = []
            phase(c)
            nc.clear_and_free_semaphores(c.sems)
            nc.all_engine_barrier()
        c.sems = []
        store(c)


PHASES = [column_attention, l0_experts, head_attention, l1_experts, mean_messages, slices, edge_gates, l3_experts]


def kernel(**inputs):
    import numpy as _np
    import concourse.bacc as _bacc
    from concourse import mybir as _mybir
    from concourse.bass_utils import run_bass_kernel_spmd as _run

    nc = _bacc.Bacc("TRN2", target_bir_lowering=False, num_devices=1)
    arrays, io = {}, {}
    for name, value in inputs.items():
        a = _np.ascontiguousarray(value)
        if a.ndim == 0:
            a = a.reshape(1, 1)
        arrays[f"in_{name}"] = a
        io[name] = nc.dram_tensor(f"in_{name}", a.shape, _mybir.dt.from_np(a.dtype), kind="ExternalInput").ap()
    x = io["x"]
    io["out"] = nc.dram_tensor("out_x", x.shape, F32, kind="ExternalOutput").ap()
    network(nc, io, x.shape[0])
    r = _run(nc, [arrays], core_ids=[0])
    return r.results[0]["out_x"]
```

```python
from contextlib import ExitStack

import concourse.bass as bass
from concourse import mybir

ALU = mybir.AluOpType
ACT = mybir.ActivationFunctionType
F32 = mybir.dt.float32
F32R = mybir.dt.float32r
I32 = mybir.dt.int32
U32 = mybir.dt.uint32
AX_X = mybir.AxisListType.X

P = 128
GB = 4
T = GB * P
S = 2
EPS = 1e-5
E = 8


class Steps:

    def __init__(self, sem, names):
        self.sem, self.names, self.at = sem, names.split(), 0

    def start(self, engine):
        engine.sem_inc(self.sem, 1)

    def done(self, turn, name):
        return turn * len(self.names) + (self.names.index(name) + 2)

    def all_done(self, turns):
        return turns * len(self.names) + 1

    def mark(self, instruction, name):
        assert self.names[self.at % len(self.names)] == name, (name, self.names[self.at % len(self.names)])
        self.at += 1
        instruction.then_inc(self.sem, 1)


class Count:

    def __init__(self, sem, per, credit=0):
        self.sem, self.per, self.credit = sem, per, credit

    def done(self, group, k=0):
        assert k + 1 + self.credit >= 0
        return group * self.per + (k + 1 + self.credit)


class Chip:

    def __init__(self, nc, ctx, io, n_batch):
        self.nc, self.ctx, self.io, self.nb = nc, ctx, io, n_batch
        self.groups = n_batch // GB
        self.sems = []
        self.turns = self.groups // S
        pad = n_batch + 2 * GB
        self.x = self.sb("x_all", [P, pad, P])
        self.stats = self.sb("ln_stats", [P, pad, 6])
        self.mean = self.sb("ln_mean", [P, pad])
        self.rstd = self.sb("ln_rstd", [P, pad])
        self.rstd2 = self.sb("ln_rstd2", [P, pad])
        self.ratio = self.sb("ln_ratio", [P, pad])
        self.tmp = [self.sb(f"ln_tmp{k}", [P, pad]) for k in range(3)]
        self.mhalf = self.sb("minus_half", [P, pad])
        self.pace = self.sb("pace", [P, 1])
        self.ident = self.sb("identity", [P, P])
        self.ones = self.sb("ones", [P, P])

    def sb(self, name, shape, dt=F32, ctx=None):
        return (ctx or self.ctx).enter_context(self.nc.sbuf_tensor(name, shape, dt))

    def ps(self, name, ctx, shape=(P, T)):
        return ctx.enter_context(self.nc.psum_tensor(name, list(shape), F32))

    def sem(self, name):
        self.sems.append(self.nc.alloc_semaphore(name=name))
        return self.sems[-1]

    def grouped(self, t):
        if len(t.shape) == 3:
            return t[:, :, :].rearrange("p (g b) f -> p g b f", b=GB)
        return t[:, :].rearrange("p (g b) -> p g b", b=GB)


class Chain:

    def __init__(self, engine, sem):
        self.engine, self.sem, self.n = engine, sem, 0

    def link(self, instruction):
        self.n += 1
        instruction.then_inc(self.sem, 1)
        self.engine.wait_ge(self.sem, self.n)


def load_and_constants(c):
    nc, nb = c.nc, c.nb
    made, filled, counted = (c.sem(n) for n in ("const_made", "const_zero", "stats_made"))
    parts = min(4, c.groups)
    loaded = [c.sem(f"x_loaded{k}") for k in range(parts)]
    xg, sg = c.grouped(c.x), c.grouped(c.stats)
    with nc.Block() as block:

        @block.sync
        def _(sp):
            n = nb // parts
            for k in range(parts):
                sp.dma_start(c.x[:, k * n:(k + 1) * n, :],
                             c.io["x"][k * n:(k + 1) * n].rearrange("b n d -> n b d")).then_inc(loaded[k], 16)

        @block.gpsimd
        def _(pool):
            pool.memset(c.ident[:], 0.0).then_inc(filled, 1)
            pool.memset(c.ones[:], 1.0).then_inc(made, 1)
            pool.memset(c.mhalf[:], -0.5).then_inc(made, 1)
            pool.memset(c.x[:, nb:, :], 0.0).then_inc(made, 1)
            pool.memset(c.stats[:, nb:, :], 0.0).then_inc(made, 1)
            pool.wait_ge(filled, 1)
            pool.affine_select(out=c.ident[:], in_=c.ident[:], compare_op=ALU.not_equal, fill=1.0, base=0,
                               pattern=[[-1, P]], channel_multiplier=1).then_inc(made, 1)
            pool.wait_ge(made, 5)

        @block.vector
        def _(dve):
            n = c.groups // parts
            for k in range(parts):
                dve.wait_ge(loaded[k], 16)
                with dve.Fori(k * n, (k + 1) * n) as g:
                    for b in range(GB):
                        last = dve.bn_stats(sg[:, g, b, :], xg[:, g, b, :])
                    last.then_inc(counted, 1)
            dve.wait_ge(counted, c.groups)


def ln_dve(c, dve, chain, rooted, double):
    m0, m1 = c.stats[:, :, 1], c.stats[:, :, 4]
    q0, q1 = c.stats[:, :, 2], c.stats[:, :, 5]
    t0, t1, t2 = (t[:] for t in c.tmp)
    link = chain.link
    link(dve.tensor_tensor(t0, m0, m1, ALU.subtract))
    link(dve.tensor_tensor(t1, m0, m1, ALU.add))
    link(dve.tensor_scalar(c.mean[:], t1, 0.5, None, ALU.mult))
    link(dve.tensor_tensor(t1, q0, q1, ALU.add))
    link(dve.tensor_tensor(t2, t0, t0, ALU.mult))
    link(dve.tensor_scalar(t2, t2, 0.25, None, ALU.mult))
    link(dve.scalar_tensor_tensor(t0, t1, 1.0 / P, t2, ALU.mult, ALU.add))

    def inverse_root(out, v, a):
        link(dve.reciprocal(out, a))
        link(dve.tensor_tensor(a, out, out, ALU.mult))
        link(dve.tensor_tensor(a, a, v, ALU.mult))
        link(dve.tensor_scalar(a, a, -0.5, 1.5, ALU.mult, ALU.add))
        link(dve.tensor_tensor(out, out, a, ALU.mult))

    dve.tensor_scalar(t1, t0, EPS, None, ALU.add).then_inc(rooted, 1)
    dve.wait_ge(rooted, 2)
    inverse_root(c.rstd[:], t1, t2)
    if double:
        link(dve.tensor_tensor(t2, c.rstd[:], c.rstd[:], ALU.mult))
        link(dve.tensor_tensor(t2, t2, t0, ALU.mult))
        dve.tensor_scalar(t2, t2, EPS, None, ALU.add).then_inc(rooted, 1)
        dve.wait_ge(rooted, 4)
        inverse_root(c.rstd2[:], t2, t1)
        link(dve.tensor_tensor(c.ratio[:], t2, c.rstd2[:], ALU.mult))
        link(dve.tensor_tensor(c.rstd[:], c.rstd[:], c.rstd2[:], ALU.mult))


def ln_act(c, act, rooted, double):
    act.wait_ge(rooted, 1)
    act.activation(c.tmp[2][:], c.tmp[1][:], ACT.Sqrt).then_inc(rooted, 1)
    if double:
        act.wait_ge(rooted, 3)
        act.activation(c.tmp[1][:], c.tmp[2][:], ACT.Sqrt).then_inc(rooted, 1)


def load_adjacency(c, sp, adj_i, adjg, adj_in, used):
    for u in range(2):
        sp.dma_start(adj_i[u][:], adjg[u]).then_inc(adj_in[u], 16)
    if c.turns > 1:
        with sp.Fori(0, c.turns - 1) as i:
            for u in range(2):
                sp.wait_ge(used.sem, used.done(i * 2 + u))
                sp.dma_start(adj_i[u][:], adjg[i * 2 + u + 2]).then_inc(adj_in[u], 16)
    for u in range(2):
        sp.wait_ge(used.sem, used.done(c.groups - 2 + u))
        sp.dma_start(adj_i[u][:], adjg[u]).then_inc(adj_in[u], 16)


def column_attention(c):
    nc, io = c.nc, c.io
    xg, sg = c.grouped(c.x), c.grouped(c.stats)
    meang, rstdg = c.grouped(c.mean), c.grouped(c.rstd)
    adjg = io["adj"].rearrange("(g b) i j -> g i b j", b=GB)
    with ExitStack() as ctx:
        sb = lambda name, shape, dt=F32: c.sb("ca_" + name, shape, dt, ctx)
        sem = lambda name: c.sem("ca_" + name)
        w, wT, a12, wa, wa1b = sb("w", [P, P]), sb("wT", [P, P]), sb("a12", [P, 2]), sb("wa", [P, 2]), sb("wa1b", [P, P])
        adj_i = [sb(f"adj_i{u}", [P, GB, P], I32) for u in range(2)]
        score = [sb(f"score{u}", [P, GB, P]) for u in range(2)]
        hs = [sb(f"hs{u}", [P, GB, P]) for u in range(2)]
        nmax = [sb(f"nmax{u}", [P, GB]) for u in range(2)]
        den = [sb(f"den{u}", [P, GB]) for u in range(2)]
        adj_f, xn, xT, pen, hp = sb("adj_f", [P, GB, P]), sb("xn", [P, GB, P]), sb("xT", [P, T]), sb("pen", [P, GB, P]), sb("hp", [P, T])
        s2, rden = sb("s2", [P, GB]), sb("rden", [P, GB])
        turned, turned_adj, s1_bank, s2_bank, out = (c.ps("ca_" + n, ctx) for n in ("turned", "turned_adj", "s1", "s2b", "out"))
        h_bank = [c.ps(f"ca_h{u}", ctx) for u in range(2)]
        loaded, chain, rooted, prepared = (sem(n) for n in ("loaded", "chain", "rooted", "prepared"))
        adj_in = [sem(f"adj_in{u}") for u in range(2)]
        adj_ready, xn_ready, xT_ready, adjT_ready, xT_copied, products_ready, pen_done, s2_copied, masked, leaky = (
            Count(sem(n), 1) for n in ("adj_ready", "xn_ready", "xT_ready", "adjT_ready", "xT_copied", "products_ready",
                                       "pen_done", "s2_copied", "masked", "leaky"))
        max_done, exp_done, inv_done, hs_done, out_ready, gelu_done, x_added = (
            Count(sem(n), 1) for n in ("max_done", "exp_done", "inv_done", "hs_done", "out_ready", "gelu_done", "x_added"))
        with nc.Block() as block:

            @block.sync
            def _(sp):
                sp.dma_start(w[:], io["L0_gnn_W"]).then_inc(loaded, 16)
                sp.dma_start(a12[:], io["L0_gnn_a"].rearrange("(t d) o -> d (t o)", t=2),
                             allow_slow_non_contiguous=True).then_inc(loaded, 16)
                load_adjacency(c, sp, adj_i, adjg, adj_in, adj_ready)

            @block.scalar
            def _(act):
                ln_act(c, act, rooted, False)
                def copy_xT(g):
                    act.wait_ge(xT_ready.sem, xT_ready.done(g))
                    act.activation(xT[:], turned[:], ACT.Copy).then_inc(xT_copied.sem, 1)

                def exponentials(g, u):
                    act.wait_ge(max_done.sem, max_done.done(g))
                    for b in range(GB):
                        last = act.activation(score[u][:, b, :], score[u][:, b, :], ACT.Exp,
                                              bias=nmax[u][:, b:b + 1], accum_out=den[u][:, b:b + 1])
                    last.then_inc(exp_done.sem, 1)

                copy_xT(0)
                exponentials(0, 0)
                copy_xT(1)
                with act.Fori(0, c.turns) as i:
                    for u in range(2):
                        g = i * 2 + u
                        copy_xT(g + 2)
                        act.wait_ge(out_ready.sem, out_ready.done(g))
                        act.activation(hp[:], out[:], ACT.Gelu).then_inc(gelu_done.sem, 1)
                        exponentials(g + 1, 1 - u)

            @block.vector
            def _(dve):
                ln_dve(c, dve, Chain(dve, chain), rooted, False)

                def adjacency(g, u, nth):
                    dve.wait_ge(adj_in[u], nth * 16 + 16)
                    dve.tensor_copy(adj_f[:], adj_i[u][:]).then_inc(adj_ready.sem, 1)

                def normalise(g, before=None):
                    if before is not None:
                        dve.wait_ge(xT_ready.sem, xT_ready.done(before))
                    for b in range(GB):
                        last = dve.tensor_scalar(xn[:, b, :], xg[:, g, b, :], meang[:, g, b:b + 1], rstdg[:, g, b:b + 1],
                                                 ALU.subtract, ALU.mult)
                    last.then_inc(xn_ready.sem, 1)

                def penalty(g):
                    dve.wait_ge(adjT_ready.sem, adjT_ready.done(g))
                    dve.tensor_scalar(pen[:].rearrange("p b f -> p (b f)"), turned_adj[:], 0.0, -1e20 / 0.4,
                                      ALU.is_le, ALU.mult).then_inc(pen_done.sem, 1)

                def scores(g, u):
                    dve.wait_ge(products_ready.sem, products_ready.done(g))
                    dve.tensor_copy(s2[:], s2_bank[:, 0:GB]).then_inc(s2_copied.sem, 1)
                    dve.wait_ge(s2_copied.sem, s2_copied.done(g))
                    dve.wait_ge(pen_done.sem, pen_done.done(g))
                    for b in range(GB):
                        last = dve.scalar_tensor_tensor(score[u][:, b, :], s1_bank[:, b * P:(b + 1) * P],
                                                        s2[:, b:b + 1], pen[:, b, :], ALU.add, ALU.add)
                    last.then_inc(masked.sem, 1)
                    dve.wait_ge(masked.sem, masked.done(g))
                    dve.scalar_tensor_tensor(score[u][:], score[u][:], 0.4, score[u][:], ALU.mult, ALU.max).then_inc(leaky.sem, 1)
                    dve.wait_ge(leaky.sem, leaky.done(g))
                    dve.tensor_reduce(nmax[u][:], score[u][:], AX_X, ALU.max, negate=True).then_inc(max_done.sem, 1)

                dve.wait_ge(loaded, 32)
                dve.wait_ge(prepared, 1)
                dve.tensor_copy(wT[:], turned[:, 0:P]).then_inc(prepared, 1)
                dve.wait_ge(prepared, 3)
                dve.tensor_copy(wa[:], turned[:, 0:2]).then_inc(prepared, 1)
                dve.wait_ge(prepared, 4)
                dve.tensor_scalar(wa1b[:], c.ones[:], wa[:, 0:1], None, ALU.mult).then_inc(prepared, 1)
                adjacency(0, 0, 0)
                normalise(0)
                penalty(0)
                scores(0, 0)
                adjacency(1, 1, 0)
                normalise(1)
                with dve.Fori(0, c.turns) as i:
                    for u in range(2):
                        g = i * 2 + u
                        penalty(g + 1)
                        adjacency(g + 2, u, i + 1)
                        normalise(g + 2, g + 1)
                        dve.wait_ge(exp_done.sem, exp_done.done(g))
                        dve.reciprocal(rden[:], den[u][:]).then_inc(inv_done.sem, 1)
                        dve.wait_ge(inv_done.sem, inv_done.done(g))
                        for b in range(GB):
                            last = dve.tensor_scalar(hs[u][:, b, :], h_bank[u][:, b * P:(b + 1) * P], rden[:, b:b + 1], None,
                                                     ALU.mult)
                        last.then_inc(hs_done.sem, 1)
                        scores(g + 1, 1 - u)
                        dve.wait_ge(gelu_done.sem, gelu_done.done(g))
                        dve.tensor_tensor(xg[:, g, :, :], xg[:, g, :, :], hp[:].rearrange("p (b f) -> p b f", b=GB), ALU.add)\
                            .then_inc(x_added.sem, 1)
                        dve.wait_ge(x_added.sem, x_added.done(g))
                        for b in range(GB):
                            dve.bn_stats(sg[:, g, b, :], xg[:, g, b, :])

            @block.tensor
            def _(pe):
                def turn(g, before=None):
                    pe.wait_ge(xn_ready.sem, xn_ready.done(g))
                    if before is not None:
                        pe.wait_ge(xT_copied.sem, xT_copied.done(before))
                        pe.wait_ge(pen_done.sem, pen_done.done(before))
                    for b in range(GB):
                        last = pe.transpose(turned[:, b * P:(b + 1) * P], xn[:, b, :], c.ident[:])
                    last.then_inc(xT_ready.sem, 1)
                    pe.wait_ge(adj_ready.sem, adj_ready.done(g))
                    for b in range(GB):
                        last = pe.transpose(turned_adj[:, b * P:(b + 1) * P], adj_f[:, b, :], c.ident[:])
                    last.then_inc(adjT_ready.sem, 1)

                def products(g, u, before=None):
                    pe.wait_ge(xT_copied.sem, xT_copied.done(g))
                    if before is not None:
                        pe.wait_ge(max_done.sem, max_done.done(before))
                    pe.matmul(s1_bank[:], wa1b[:], xT[:], start=True, stop=True)
                    for b in range(GB):
                        pe.matmul(s2_bank[:, b:b + 1], xT[:, b * P:(b + 1) * P], wa[:, 1:2], start=True, stop=True)
                    for b in range(GB):
                        last = pe.matmul(h_bank[u][:, b * P:(b + 1) * P], xT[:, b * P:(b + 1) * P], w[:], start=True, stop=True)
                    last.then_inc(products_ready.sem, 1)

                pe.wait_ge(loaded, 32)
                pe.transpose(turned[:, 0:P], w[:], c.ident[:]).then_inc(prepared, 1)
                pe.wait_ge(prepared, 2)
                pe.matmul(turned[:, 0:2], wT[:], a12[:], start=True, stop=True).then_inc(prepared, 1)
                pe.wait_ge(prepared, 5)
                turn(0)
                products(0, 0)
                turn(1, 0)
                with pe.Fori(0, c.turns) as i:
                    for u in range(2):
                        g = i * 2 + u
                        products(g + 1, 1 - u, g)
                        turn(g + 2, g + 1)
                        pe.wait_ge(hs_done.sem, hs_done.done(g))
                        for b in range(GB):
                            last = pe.matmul(out[:, b * P:(b + 1) * P], score[u][:, b, :], hs[u][:, b, :], start=True, stop=True)
                        last.then_inc(out_ready.sem, 1)


def experts(c, tag, hidden, w1, b1, w2, b2, wr, br=None, gain=None, shift=None, routed_gain=False, double=False,
            shared=None, out=None):
    nc = c.nc
    ch = hidden // P
    first = 1 if shared else 0
    ne = E + first
    nk = ne * ch
    xg, sg = c.grouped(c.x), c.grouped(c.stats)
    meang, rstdg, ratiog = c.grouped(c.mean), c.grouped(c.rstd), c.grouped(c.ratio)
    SLOTS = 4
    PROD1, GELU, SPLIT, PROD2, YCOPY = 5, 4, 4, 2, 1
    NORM, TURN, COPY, CUT, ROUTE, TOP, TANH, PROBS = 0, 2, 3, 5, 5, 7, 9, 10
    HI_BY_ACT = (1, 2, 3) if ch == 2 else (1, 3)
    LO_BY_POOL = (3,)
    assert nk % SLOTS == 0 and ch > YCOPY and PROBS < nk - PROD1

    with ExitStack() as ctx:
        sb = lambda name, shape, dt=F32: c.sb(f"{tag}_{name}", shape, dt, ctx)
        sem = lambda name: c.sem(f"{tag}_{name}")
        w1h, w1l = sb("w1_hi", [P, nk, P], F32R), sb("w1_lo", [P, nk, P], F32R)
        w2h, w2l = sb("w2_hi", [P, nk, P], F32R), sb("w2_lo", [P, nk, P], F32R)
        RAW, FIRST = 8, 4
        raw = [sb(f"raw{k}", [P, ch, P]) for k in range(RAW)]
        b1_rows, b2_rows, gain_rows, shift_rows = sb("b1_rows", [nk, P]), sb("b2_rows", [ne, P]), sb("gain_rows", [E, P]), sb("shift_rows", [E, P])
        b1T, b2T, gainT, shiftT = sb("b1T", [P, nk]), sb("b2T", [P, ne]), sb("gainT", [P, E]), sb("shiftT", [P, E])
        wr_sb, br_row, br_all = sb("wr", [P, E]), sb("br_row", [1, E]), sb("br_all", [P, E])
        iota, iota_i = sb("iota", [P, GB, E]), sb("iota_i", [P, GB, E], I32)
        shift_wide = sb("shift_wide", [P, P])
        xn, xf = sb("xn", [P, GB, P]), sb("xf", [P, T])
        x_hi = [sb(f"x_hi{u}", [P, T], F32R) for u in range(2)]
        x_lo = [sb(f"x_lo{u}", [P, T], F32R) for u in range(2)]
        g_full = [sb(f"g_full{k}", [P, T]) for k in range(SLOTS)]
        g_hi = [sb(f"g_hi{k}", [P, T], F32R) for k in range(SLOTS)]
        g_lo = [sb(f"g_lo{k}", [P, T], F32R) for k in range(SLOTS)]
        yT = [sb(f"yT{k}", [P, T]) for k in range(2)]
        probs = [sb(f"probs{u}", [P, GB, E]) for u in range(2)]
        logit, top = sb("logit", [P, GB, E]), sb("top", [P, GB, E])
        where, wheref = sb("where", [P, GB, E], U32), sb("wheref", [P, GB, E])
        gap, half, pa, pb = sb("gap", [P, GB]), sb("half", [P, GB]), sb("pa", [P, GB]), sb("pb", [P, GB])
        is_a, is_b = sb("is_a", [P, GB, E]), sb("is_b", [P, GB, E])
        hid = [c.ps(f"{tag}_hid{k}", ctx) for k in range(SLOTS)]
        ysum = [c.ps(f"{tag}_ysum{k}", ctx) for k in range(2)]
        yback, misc = c.ps(f"{tag}_yback", ctx), c.ps(f"{tag}_misc", ctx)

        small_in, chain, rooted, prep, made = sem("small_in"), sem("chain"), sem("rooted"), sem("prep"), sem("made")
        raw_in = [sem(f"raw_in{k}") for k in range(RAW)]
        raw_hi, raw_lo, b1_sum = sem("raw_hi"), sem("raw_lo"), sem("b1_sum")
        stored = sem("stored")
        hid_ready = Count(sem("hid_ready"), nk)
        gelu_done = Count(sem("gelu_done"), nk, SLOTS)
        second = Count(sem("second"), nk, SLOTS)
        hi_done = [Count(sem(f"hi_done{k}"), nk // SLOTS) for k in range(SLOTS)]
        lo_done = [Count(sem(f"lo_done{k}"), nk // SLOTS, 1) for k in range(SLOTS)]
        y_copied, turned_back, added = Count(sem("y_copied"), ne, 2), Count(sem("turned_back"), ne, 2), Count(sem("added"), ne, 1)
        xn_ready, xf_ready, gap_ready, tanh_ready = (
            Count(sem(n), 1) for n in ("xn_ready", "xf_ready", "gap_ready", "tanh_ready"))
        xT_ready, logit_ready, x_split, top_ready = (
            Count(sem(n), k, 1) for n, k in (("xT_ready", 1), ("logit_ready", 1), ("x_split", 2), ("top_ready", 5)))
        route = Count(sem("route"), 8)
        small = [(b1_rows[first * ch:nk, :], b1.rearrange("e (c h) -> (e c) h", h=P)), (b2_rows[first:ne, :], b2), (wr_sb[:], wr)]
        if shared:
            small += [(b1_rows[0:ch, :], shared[1].rearrange("(c h) -> c h", h=P)),
                      (b2_rows[0:1, :], shared[3].rearrange("(o d) -> o d", o=1))]
        if br is not None:
            small += [(br_row[:], br.rearrange("(o e) -> o e", o=1))]
        if gain is not None:
            small += [(gain_rows[:], gain), (shift_rows[:], shift)]

        def source(k):
            e = k % ne
            if k < ne:
                w = shared[0] if e < first else w1[e - first]
                return w.rearrange("d (c h) -> d c h", h=P)
            w = shared[2] if e < first else w2[e - first]
            return w.rearrange("(c h) d -> h c d", h=P)

        with nc.Block() as block:

            @block.sync
            def _(sp):
                for dst, src in small:
                    sp.dma_start(dst, src).then_inc(small_in, 16)
                for k in range(2 * ne):
                    if k >= RAW:
                        sp.wait_ge(raw_lo, k - RAW + 1)
                        if gain is not None and k - RAW < ne:
                            sp.wait_ge(b1_sum, k - RAW + 1)
                    sp.dma_start(raw[k % RAW][:], source(k)).then_inc(raw_in[k % RAW], 16)

                if out is not None:
                    og = out.rearrange("(g b) n d -> g n b d", b=GB)
                    with sp.Fori(0, c.turns) as i:
                        for u in range(2):
                            g = i * 2 + u
                            sp.wait_ge(added.sem, added.done(g, ne - 1))
                            sp.dma_start(og[g], xg[:, g, :, :]).then_inc(stored, 16)
                    sp.wait_ge(stored, 16 * c.groups)

            @block.gpsimd
            def _(pool):
                pool.iota(iota_i[:], pattern=[[0, GB], [1, E]], base=0, channel_multiplier=0).then_inc(made, 1)

                def split(g, n):
                    k = n % SLOTS
                    if k in LO_BY_POOL:
                        pool.wait_ge(hi_done[k].sem, hi_done[k].done(g, n // SLOTS))
                        pool.tensor_tensor(g_lo[k][:], g_full[k][:], g_hi[k][:].bitcast(F32), ALU.subtract)\
                            .then_inc(lo_done[k].sem, 1)

                for n in range(SPLIT):
                    split(0, n)
                with pool.Fori(0, c.turns) as i:
                    for u in range(2):
                        for m in range(nk):
                            split(i * 2 + u, m + SPLIT)

            @block.scalar
            def _(act):
                ln_act(c, act, rooted, double)
                act.sem_inc(gelu_done.sem, gelu_done.credit)
                act.sem_inc(y_copied.sem, y_copied.credit)

                def copy_xT(g):
                    act.wait_ge(xT_ready.sem, xT_ready.done(g))
                    act.wait_ge(x_split.sem, x_split.done(g, -1))
                    act.wait_ge(logit_ready.sem, logit_ready.done(g, -1))
                    act.activation(xf[:], misc[:], ACT.Copy).then_inc(xf_ready.sem, 1)

                def tanh(g):
                    act.wait_ge(gap_ready.sem, gap_ready.done(g))
                    act.activation(half[:], gap[:], ACT.Tanh, scale=0.5).then_inc(tanh_ready.sem, 1)

                def gelu(g, u, n):
                    act.wait_ge(hid_ready.sem, hid_ready.done(g, n))
                    k = n % SLOTS
                    act.wait_ge(lo_done[k].sem, lo_done[k].done(g, n // SLOTS - 1))
                    act.activation(g_full[k][:], hid[k][:], ACT.Gelu, bias=b1T[:, n % nk:n % nk + 1])\
                        .then_inc(gelu_done.sem, 1)
                    if k in HI_BY_ACT:
                        act.wait_ge(gelu_done.sem, gelu_done.done(g, n))
                        act.wait_ge(second.sem, second.done(g, n - SLOTS))
                        act.activation(g_hi[k][:], g_full[k][:], ACT.Copy).then_inc(hi_done[k].sem, 1)

                def copy_y(g, u, e):
                    k = (u * ne + e) % 2
                    act.wait_ge(second.sem, second.done(g, e * ch + ch - 1))
                    act.wait_ge(turned_back.sem, turned_back.done(g, e - 2))
                    act.activation(yT[k][:], ysum[k][:], ACT.Identity, bias=b2T[:, e:e + 1]).then_inc(y_copied.sem, 1)

                for k in range(2 * ne):
                    if k == FIRST:
                        copy_xT(0)
                        tanh(0)
                    act.wait_ge(raw_in[k % RAW], 16 * (k // RAW + 1))
                    if k == 0:
                        act.wait_ge(prep, 2)
                    e = k % ne
                    dst = (w1h if k < ne else w2h)[:, e * ch:(e + 1) * ch, :]
                    scale = gainT[:, e - first:e - first + 1] if gain is not None and k < ne and e >= first else 1.0
                    act.activation(dst, raw[k % RAW][:], ACT.Copy, scale=scale).then_inc(raw_hi, 1)
                act.wait_ge(prep, 5)
                for n in range(GELU):
                    gelu(0, 0, n)
                with act.Fori(0, c.turns) as i:
                    for u in range(2):
                        g = i * 2 + u
                        for m in range(nk):
                            gelu(g, u, m + GELU)
                            if (m + YCOPY) % ch == ch - 1 and m + YCOPY < nk:
                                copy_y(g, u, (m + YCOPY) // ch)
                            if m == COPY:
                                copy_xT(g + 1)
                            if m == TANH:
                                tanh(g + 1)

            @block.vector
            def _(dve):
                ln = Chain(dve, chain)
                link = ln.link
                for k in range(SLOTS):
                    dve.sem_inc(lo_done[k].sem, lo_done[k].credit)
                dve.sem_inc(added.sem, added.credit)
                dve.sem_inc(x_split.sem, x_split.credit)
                dve.sem_inc(top_ready.sem, top_ready.credit)
                ln_dve(c, dve, ln, rooted, double)

                def normalise(g):
                    dve.wait_ge(xT_ready.sem, xT_ready.done(g, -1))
                    for b in range(GB):
                        last = dve.tensor_scalar(xn[:, b, :], xg[:, g, b, :], meang[:, g, b:b + 1], rstdg[:, g, b:b + 1],
                                                 ALU.subtract, ALU.mult)
                    last.then_inc(xn_ready.sem, 1)

                def cut(g, u):
                    dve.wait_ge(xf_ready.sem, xf_ready.done(g))
                    dve.tensor_copy(x_hi[u][:], xf[:]).then_inc(x_split.sem, 1)
                    dve.wait_ge(x_split.sem, x_split.done(g, 0))
                    dve.tensor_tensor(x_lo[u][:], xf[:], x_hi[u][:].bitcast(F32), ALU.subtract).then_inc(x_split.sem, 1)

                def top_two(g):
                    dve.wait_ge(logit_ready.sem, logit_ready.done(g))
                    for b in range(GB):
                        scale = ratiog[:, g, b:b + 1] if double and not routed_gain else 1.0
                        last = dve.scalar_tensor_tensor(logit[:, b, :], misc[:, b * E:(b + 1) * E], scale, br_all[:],
                                                        ALU.mult, ALU.add)
                    last.then_inc(top_ready.sem, 1)
                    dve.wait_ge(top_ready.sem, top_ready.done(g, 0))
                    dve.memset(c.pace[:], 0.0)
                    for b in range(GB):
                        last = dve.max(top[:, b, :], logit[:, b, :])
                    last.then_inc(top_ready.sem, 1)
                    dve.wait_ge(top_ready.sem, top_ready.done(g, 1))
                    dve.tensor_tensor(gap[:], top[:, :, 0], top[:, :, 1], ALU.subtract).then_inc(gap_ready.sem, 1)
                    for b in range(GB):
                        last = dve.max_index(where[:, b, :], top[:, b, :], logit[:, b, :])
                    last.then_inc(top_ready.sem, 1)
                    dve.wait_ge(top_ready.sem, top_ready.done(g, 2))
                    dve.tensor_copy(wheref[:], where[:]).then_inc(top_ready.sem, 1)
                    dve.wait_ge(top_ready.sem, top_ready.done(g, 3))
                    wide = [P, GB, E]
                    dve.tensor_tensor(is_a[:], iota[:], wheref[:, :, 0:1].to_broadcast(wide), ALU.is_equal)
                    dve.tensor_tensor(is_b[:], iota[:], wheref[:, :, 1:2].to_broadcast(wide), ALU.is_equal)\
                        .then_inc(top_ready.sem, 1)

                def two_probs(g, u):
                    dve.wait_ge(tanh_ready.sem, tanh_ready.done(g))
                    wide = [P, GB, E]
                    dve.tensor_scalar(pa[:], half[:], 0.5, 0.5, ALU.mult, ALU.add)
                    dve.tensor_scalar(pb[:], half[:], -0.5, 0.5, ALU.mult, ALU.add).then_inc(route.sem, 1)
                    dve.wait_ge(route.sem, route.done(g, 0))
                    dve.tensor_tensor(is_a[:], is_a[:], pa[:].unsqueeze(2).to_broadcast(wide), ALU.mult)
                    dve.tensor_tensor(is_b[:], is_b[:], pb[:].unsqueeze(2).to_broadcast(wide), ALU.mult)\
                        .then_inc(route.sem, 1)
                    dve.wait_ge(route.sem, route.done(g, 1))
                    dve.tensor_tensor(probs[u][:], is_a[:], is_b[:], ALU.add).then_inc(route.sem, 6)

                def split(g, u, n):
                    k = n % SLOTS
                    if k not in HI_BY_ACT:
                        dve.wait_ge(gelu_done.sem, gelu_done.done(g, n))
                        dve.wait_ge(second.sem, second.done(g, n - SLOTS))
                        dve.tensor_copy(g_hi[k][:], g_full[k][:]).then_inc(hi_done[k].sem, 1)
                    if k not in LO_BY_POOL:
                        dve.wait_ge(hi_done[k].sem, hi_done[k].done(g, n // SLOTS))
                        dve.tensor_tensor(g_lo[k][:], g_full[k][:], g_hi[k][:].bitcast(F32), ALU.subtract)\
                            .then_inc(lo_done[k].sem, 1)

                def add(g, u, e):
                    dve.wait_ge(turned_back.sem, turned_back.done(g, e))
                    dve.wait_ge(added.sem, added.done(g, e - 1))
                    if e == first:
                        dve.wait_ge(route.sem, route.done(g, 7))
                    for b in range(GB):
                        p = 1.0 if e < first else probs[u][:, b, e - first:e - first + 1]
                        last = dve.scalar_tensor_tensor(xg[:, g, b, :], yback[:, b * P:(b + 1) * P], p, xg[:, g, b, :],
                                                        ALU.mult, ALU.add)
                    last.then_inc(added.sem, 1)

                dve.wait_ge(prep, 1)
                dve.wait_ge(made, 1)
                dve.tensor_copy(iota[:], iota_i[:])
                dve.tensor_copy(b2T[:], yback[:, 0:ne])
                if gain is not None:
                    dve.tensor_copy(gainT[:], hid[0][:, 0:E])
                    link(dve.tensor_copy(shiftT[:], hid[1][:, 0:E]))
                if routed_gain:
                    dve.tensor_scalar(shift_wide[:], c.ones[:], shiftT[:, 0:1], None, ALU.mult)
                if br is None:
                    dve.memset(br_all[:], 0.0)
                dve.drain().then_inc(prep, 1)
                dve.wait_ge(prep, 3)
                if br is not None:
                    dve.tensor_copy(br_all[:], hid[2][:, 0:E])
                if routed_gain:
                    dve.tensor_scalar(wr_sb[:], wr_sb[:], gainT[:, 0:1], None, ALU.mult)
                dve.drain().then_inc(prep, 1)
                for k in range(2 * ne):
                    if k == FIRST:
                        normalise(0)
                        cut(0, 0)
                        top_two(0)
                        two_probs(0, 0)
                    e = k % ne
                    dst, hi = ((w[:, e * ch:(e + 1) * ch, :]) for w in ((w1l, w1h) if k < ne else (w2l, w2h)))
                    dve.wait_ge(raw_hi, k + 1)
                    if gain is not None and k < ne and e >= first:
                        ins = dve.scalar_tensor_tensor(dst, raw[k % RAW][:], gainT[:, e - first:e - first + 1],
                                                       hi.bitcast(F32), ALU.mult, ALU.subtract)
                    else:
                        ins = dve.tensor_tensor(dst, raw[k % RAW][:], hi.bitcast(F32), ALU.subtract)
                    ins.then_inc(raw_lo, 1)
                if gain is not None:
                    dve.wait_ge(b1_sum, ne)
                    link(dve.tensor_copy(b1T[:], ysum[1][:, 0:nk]))
                    dve.tensor_tensor(b1T[:], b1T[:], ysum[0][:, 0:nk], ALU.add).then_inc(prep, 1)
                else:
                    dve.tensor_copy(b1T[:], ysum[1][:, 0:nk]).then_inc(prep, 1)
                for n in range(SPLIT):
                    split(0, 0, n)
                with dve.Fori(0, c.turns) as i:
                    for u in range(2):
                        g = i * 2 + u
                        for m in range(nk):
                            split(g, u, m + SPLIT)
                            if m == NORM:
                                normalise(g + 1)
                            if m == CUT:
                                cut(g + 1, 1 - u)
                            if m == TOP:
                                top_two(g + 1)
                            if m == PROBS:
                                two_probs(g + 1, 1 - u)
                            if m % ch == ch - 1:
                                add(g, u, m // ch)
                        if out is None:
                            dve.wait_ge(added.sem, added.done(g, ne - 1))
                            for b in range(GB):
                                dve.bn_stats(sg[:, g, b, :], xg[:, g, b, :])

            @block.tensor
            def _(pe):
                pe.sem_inc(second.sem, second.credit)
                pe.sem_inc(turned_back.sem, turned_back.credit)
                pe.sem_inc(xT_ready.sem, xT_ready.credit)
                pe.sem_inc(logit_ready.sem, logit_ready.credit)

                def turn(g):
                    pe.wait_ge(xn_ready.sem, xn_ready.done(g))
                    pe.wait_ge(top_ready.sem, top_ready.done(g, -1))
                    for b in range(GB):
                        last = pe.transpose(misc[:, b * P:(b + 1) * P], xn[:, b, :], c.ident[:])
                    last.then_inc(xT_ready.sem, 1)

                def router(g):
                    pe.wait_ge(xf_ready.sem, xf_ready.done(g))
                    for b in range(GB):
                        last = pe.matmul(misc[:, b * E:(b + 1) * E], xf[:, b * P:(b + 1) * P], wr_sb[:], start=True, stop=True)
                    last.then_inc(logit_ready.sem, 1)

                def product(out, hi, lo, x, y, start, stop):
                    pe.matmul(out, hi, x, start=start, stop=False)
                    pe.matmul(out, hi, y, start=False, stop=False)
                    return pe.matmul(out, lo, x, start=False, stop=stop)

                def first_product(g, u, n):
                    k = n % SLOTS
                    if n % nk == 0:
                        pe.wait_ge(x_split.sem, x_split.done(g, 2 * (n // nk) + 1))
                    pe.wait_ge(gelu_done.sem, gelu_done.done(g, n - SLOTS))
                    v = (u + n // nk) % 2
                    product(hid[k][:], w1h[:, n % nk, :], w1l[:, n % nk, :], x_hi[v][:], x_lo[v][:], True, True)\
                        .then_inc(hid_ready.sem, 1)

                def second_product(g, u, n):
                    k = n % SLOTS
                    pe.wait_ge(lo_done[k].sem, lo_done[k].done(g, n // SLOTS))
                    e = n // ch
                    if n % ch == 0:
                        pe.wait_ge(y_copied.sem, y_copied.done(g, e - 2))
                    product(ysum[(u * ne + e) % 2][:], w2h[:, n % nk, :], w2l[:, n % nk, :], g_hi[k][:], g_lo[k][:],
                            n % ch == 0, n % ch == ch - 1).then_inc(second.sem, 1)

                def turn_back(g, u, e):
                    k = (u * ne + e) % 2
                    pe.wait_ge(y_copied.sem, y_copied.done(g, e))
                    pe.wait_ge(added.sem, added.done(g, e - 1))
                    for b in range(GB):
                        last = pe.transpose(yback[:, b * P:(b + 1) * P], yT[k][:, b * P:(b + 1) * P], c.ident[:])
                    last.then_inc(turned_back.sem, 1)

                pe.wait_ge(small_in, 16 * len(small))
                pe.transpose(ysum[1][:, 0:nk], b1_rows[:], c.ident[0:nk, 0:nk])
                last = pe.transpose(yback[:, 0:ne], b2_rows[:], c.ident[0:ne, 0:ne])
                if gain is not None:
                    pe.transpose(hid[0][:, 0:E], gain_rows[:], c.ident[0:E, 0:E])
                    last = pe.transpose(hid[1][:, 0:E], shift_rows[:], c.ident[0:E, 0:E])
                last.then_inc(prep, 1)
                pe.wait_ge(prep, 2)
                if br is not None:
                    last = pe.matmul(hid[2][:, 0:E], c.ones[0:1, :], br_row[:], start=True, stop=not routed_gain)
                    if routed_gain:
                        last = pe.matmul(hid[2][:, 0:E], shift_wide[:], wr_sb[:], start=False, stop=True)
                    last.then_inc(prep, 1)
                else:
                    pe.sem_inc(prep, 1)
                pe.wait_ge(prep, 4)
                if gain is not None:
                    for k in range(ne):
                        if k == FIRST:
                            turn(0)
                            router(0)
                        pe.wait_ge(raw_in[k % RAW], 16 * (k // RAW + 1))
                        for j in range(ch):
                            last = pe.matmul(ysum[0][:, k * ch + j:k * ch + j + 1], raw[k % RAW][:, j, :], shiftT[:, k:k + 1],
                                             start=True, stop=True)
                        last.then_inc(b1_sum, 1)
                else:
                    turn(0)
                    router(0)
                pe.wait_ge(prep, 5)
                pe.wait_ge(raw_lo, 2 * ne)
                for n in range(PROD1):
                    first_product(0, 0, n)
                for n in range(PROD2):
                    second_product(0, 0, n)
                with pe.Fori(0, c.turns) as i:
                    for u in range(2):
                        g = i * 2 + u
                        for m in range(nk):
                            first_product(g, u, m + PROD1)
                            second_product(g, u, m + PROD2)
                            if m == TURN:
                                turn(g + 1)
                            if m == ROUTE:
                                router(g + 1)
                            if m % ch == ch - 1:
                                turn_back(g, u, m // ch)
                if PROD2 % ch:
                    pe.matmul(ysum[0][:], w2h[:, 0, :], g_hi[0][:], start=False, stop=True)


def l0_experts(c):
    io = c.io
    row = lambda v: v.rearrange("(o d) -> o d", o=1).to_broadcast([E, P])
    experts(c, "e0", 256, io["L0_ffn_W1"], io["L0_ffn_b1"], io["L0_ffn_W2"], io["L0_ffn_b2"], io["L0_ffn_Wr"],
            br=io["L0_ffn_br"], gain=row(io["L0_ffn_gamma"]), shift=row(io["L0_ffn_beta"]), routed_gain=True, double=True)


def l1_experts(c):
    io = c.io
    experts(c, "e1", 512, io["L1_ffn_W1"], io["L1_ffn_b1"], io["L1_ffn_W2"], io["L1_ffn_b2"], io["L1_ffn_Wr"],
            br=io["L1_ffn_br"], gain=io["L1_ffn_ln_g"], shift=io["L1_ffn_ln_b"], double=True)


def l3_experts(c):
    io = c.io
    experts(c, "e3", 512, io["L3_ffn_W1p"], io["L3_ffn_b1p"], io["L3_ffn_W2p"], io["L3_ffn_b2p"], io["L3_ffn_Wr"],
            shared=(io["L3_ffn_W1s"], io["L3_ffn_b1s"], io["L3_ffn_W2s"], io["L3_ffn_b2s"]), out=io["out"])


HEADS = 8
DK = P // HEADS


def head_attention(c):
    nc, io = c.nc, c.io
    xg, sg = c.grouped(c.x), c.grouped(c.stats)
    meang, rstdg = c.grouped(c.mean), c.grouped(c.rstd)
    adjg = io["adj"].rearrange("(g b) i j -> g i b j", b=GB)
    row = lambda v: v.rearrange("(o d) -> o d", o=1)
    with ExitStack() as ctx:
        sb = lambda name, shape, dt=F32: c.sb("ha_" + name, shape, dt, ctx)
        sem = lambda name: c.sem("ha_" + name)
        w = {k: sb("w" + k, [P, P]) for k in "qkvo"}
        bias_rows, biasT, biasq4 = sb("bias_rows", [4, P]), sb("biasT", [P, 4]), sb("biasq4", [P, 1])
        bo_row, bv_col, ds, nds = sb("bo_row", [1, P]), sb("bv_col", [P, 1]), sb("ds", [1, 1]), sb("nds", [P, 1])
        head = sb("head", [P, HEADS])
        adj_i = [sb(f"adj_i{u}", [P, GB, P], I32) for u in range(2)]
        pen = [sb(f"pen{u}", [P, GB, P]) for u in range(2)]
        qT = [sb(f"qT{u}", [P, T]) for u in range(2)]
        km = [sb(f"km{u}", [P, HEADS, T]) for u in range(2)]
        va = [sb(f"va{u}", [P, GB, HEADS, DK + 1]) for u in range(2)]
        xn, xT, kT, oT = sb("xn", [P, GB, P]), sb("xT", [P, T]), sb("kT", [P, T]), sb("oT", [P, T])
        sc = [sb(f"sc{k}", [P, HEADS, P]) for k in range(2)]
        mx = [sb(f"mx{k}", [P, HEADS]) for k in range(2)]
        pT = [sb(f"pT{k}", [P, HEADS, P]) for k in range(2)]
        rd, on = sb("rd", [P, HEADS, 1]), sb("on", [P, HEADS, DK])
        scores = [c.ps(f"ha_scores{k}", ctx, (P, HEADS, P)) for k in range(2)]
        turned_w = c.ps("ha_turned_w", ctx, (P, HEADS, P))
        out, misc = c.ps("ha_out", ctx), c.ps("ha_misc", ctx)
        heads_o = out[:, 0:HEADS * (DK + 1)].rearrange("p (h d) -> p h d", h=HEADS)
        turned_o = out[:, 2 * P:3 * P]
        loaded, chain, rooted, prep, head_made = (sem(n) for n in ("loaded", "chain", "rooted", "prep", "head_made"))
        adj_in = [sem(f"adj_in{u}") for u in range(2)]
        score_ready, masked, max_done, sub_done, exp_done, wT_ready, wT_copied, o_ready, inv_done, on_done, oT_ready = (
            Count(sem(n), GB) for n in ("score_ready", "masked", "max_done", "sub_done", "exp_done", "wT_ready",
                                        "wT_copied", "o_ready", "inv_done", "on_done", "oT_ready"))
        oT_copied = Count(sem("oT_copied"), GB, 1)
        xn_ready, xT_ready, xT_copied, k_ready, k_copied, q_ready, q_copied, v_ready, v_copied, y_ready = (
            Count(sem(n), 1) for n in ("xn_ready", "xT_ready", "xT_copied", "k_ready", "k_copied", "q_ready", "q_copied",
                                       "v_ready", "v_copied", "y_ready"))
        far, pen_done, km_low, km_high = (Count(sem(n), 1) for n in ("far", "pen_done", "km_low", "km_high"))
        x_added = Count(sem("x_added"), 1, 1)
        half = HEADS // 2
        with nc.Block() as block:

            @block.sync
            def _(sp):
                for k in "qkvo":
                    sp.dma_start(w[k][:], io["L1_gnn_W_" + k]).then_inc(loaded, 16)
                for n, k in enumerate("qkvo"):
                    sp.dma_start(bias_rows[n:n + 1, :], row(io["L1_gnn_b_" + k])).then_inc(loaded, 16)
                sp.dma_start(bo_row[:], row(io["L1_gnn_b_o"])).then_inc(loaded, 16)
                sp.dma_start(ds[:], io["L1_gnn_dist_scale"]).then_inc(loaded, 16)
                for u in range(2):
                    sp.dma_start(adj_i[u][:], adjg[u]).then_inc(adj_in[u], 16)
                if c.turns > 1:
                    with sp.Fori(0, c.turns - 1) as i:
                        for u in range(2):
                            sp.wait_ge(pen_done.sem, pen_done.done(i * 2 + u))
                            sp.dma_start(adj_i[u][:], adjg[i * 2 + u + 2]).then_inc(adj_in[u], 16)
                sp.wait_ge(pen_done.sem, pen_done.done(c.groups - 2))
                sp.dma_start(adj_i[0][:], adjg[0]).then_inc(adj_in[0], 16)

            @block.gpsimd
            def _(pool):
                def subtract(g, b):
                    k = b % 2
                    pool.wait_ge(max_done.sem, max_done.done(g, b))
                    pool.tensor_tensor(sc[k][:], sc[k][:], mx[k][:].unsqueeze(2).to_broadcast([P, HEADS, P]), ALU.subtract)\
                        .then_inc(sub_done.sem, 1)

                pool.memset(head[:], 1.0).then_inc(head_made, 1)
                for u in range(2):
                    pool.memset(va[u][:], 1.0).then_inc(head_made, 1)
                pool.wait_ge(head_made, 1)
                pool.affine_select(out=head[:], in_=head[:], compare_op=ALU.is_ge, fill=0.0, base=0,
                                   pattern=[[-DK, HEADS]], channel_multiplier=1).then_inc(head_made, 1)
                pool.wait_ge(head_made, 4)
                pool.affine_select(out=head[:], in_=head[:], compare_op=ALU.is_ge, fill=0.0, base=DK - 1,
                                   pattern=[[DK, HEADS]], channel_multiplier=-1).then_inc(head_made, 1)
                subtract(0, 0)
                subtract(0, 1)
                with pool.Fori(0, c.turns) as i:
                    for u in range(2):
                        for b in range(GB):
                            subtract(i * 2 + u, b + 2)

            @block.scalar
            def _(act):
                ln_act(c, act, rooted, False)
                act.sem_inc(oT_copied.sem, oT_copied.credit)

                def exponentials(g, b):
                    act.wait_ge(sub_done.sem, sub_done.done(g, b))
                    act.activation(sc[b % 2][:], sc[b % 2][:], ACT.Exp).then_inc(exp_done.sem, 1)

                def copy_turned(g, b):
                    act.wait_ge(wT_ready.sem, wT_ready.done(g, b))
                    act.activation(pT[b % 2][:], turned_w[:], ACT.Copy).then_inc(wT_copied.sem, 1)

                def copy_xT(g):
                    act.wait_ge(xT_ready.sem, xT_ready.done(g))
                    act.activation(xT[:], misc[:], ACT.Copy).then_inc(xT_copied.sem, 1)

                def copy_k(g):
                    act.wait_ge(k_ready.sem, k_ready.done(g))
                    act.activation(kT[:], misc[:], ACT.Identity, bias=biasT[:, 1:2]).then_inc(k_copied.sem, 1)

                def mask_k(g, u):
                    act.wait_ge(k_copied.sem, k_copied.done(g))
                    for h in range(half, HEADS):
                        last = act.activation(km[u][:, h, :], kT[:], ACT.Copy, scale=head[:, h:h + 1])
                    last.then_inc(km_high.sem, 1)

                def copy_q(g, u):
                    act.wait_ge(q_ready.sem, q_ready.done(g))
                    act.activation(qT[u][:], misc[:], ACT.Identity, bias=biasq4[:], scale=DK ** -0.5).then_inc(q_copied.sem, 1)

                def copy_v(g, u):
                    act.wait_ge(v_ready.sem, v_ready.done(g))
                    for b in range(GB):
                        last = act.activation(va[u][:, b, :, 0:DK], misc[:, b * P:(b + 1) * P].rearrange("p (h d) -> p h d", h=HEADS),
                                              ACT.Copy)
                    last.then_inc(v_copied.sem, 1)

                act.wait_ge(prep, 4)
                copy_xT(0)
                copy_k(0)
                mask_k(0, 0)
                copy_q(0, 0)
                copy_v(0, 0)
                copy_xT(1)
                exponentials(0, 0)
                copy_turned(0, 0)
                exponentials(0, 1)
                with act.Fori(0, c.turns) as i:
                    for u in range(2):
                        g = i * 2 + u
                        for b in range(GB):
                            if b == 0:
                                copy_k(g + 1)
                            copy_turned(g, b + 1)
                            act.wait_ge(oT_ready.sem, oT_ready.done(g, b))
                            act.activation(oT[:, b * P:(b + 1) * P], turned_o, ACT.Copy).then_inc(oT_copied.sem, 1)
                            if b == 0:
                                mask_k(g + 1, 1 - u)
                                copy_q(g + 1, 1 - u)
                            if b == 1:
                                copy_v(g + 1, 1 - u)
                            if b == 2:
                                copy_xT(g + 2)
                            exponentials(g, b + 2)

            @block.vector
            def _(dve):
                ln = Chain(dve, chain)
                ln_dve(c, dve, ln, rooted, False)
                dve.sem_inc(x_added.sem, x_added.credit)

                def normalise(g):
                    for b in range(GB):
                        last = dve.tensor_scalar(xn[:, b, :], xg[:, g, b, :], meang[:, g, b:b + 1], rstdg[:, g, b:b + 1],
                                                 ALU.subtract, ALU.mult)
                    last.then_inc(xn_ready.sem, 1)

                def penalty(g, u, nth):
                    dve.wait_ge(adj_in[u], nth * 16 + 16)
                    dve.tensor_scalar(pen[u][:], adj_i[u][:], 0.0, -1e9, ALU.is_le, ALU.mult).then_inc(far.sem, 1)
                    dve.wait_ge(far.sem, far.done(g))
                    dve.scalar_tensor_tensor(pen[u][:], adj_i[u][:], nds[:], pen[u][:], ALU.mult, ALU.add)\
                        .then_inc(pen_done.sem, 1)

                def mask_k(g, u):
                    dve.wait_ge(k_copied.sem, k_copied.done(g))
                    for h in range(half):
                        last = dve.tensor_scalar(km[u][:, h, :], kT[:], head[:, h:h + 1], None, ALU.mult)
                    last.then_inc(km_low.sem, 1)

                def maxima(g, u, b):
                    k = b % 2
                    v = (u + b // GB) % 2
                    dve.wait_ge(score_ready.sem, score_ready.done(g, b))
                    if b % GB == 0:
                        dve.wait_ge(pen_done.sem, pen_done.done(g + b // GB))
                    dve.tensor_tensor(sc[k][:], scores[k][:], pen[v][:, b % GB:b % GB + 1, :].to_broadcast([P, HEADS, P]), ALU.add)\
                        .then_inc(masked.sem, 1)
                    dve.wait_ge(masked.sem, masked.done(g, b))
                    dve.tensor_reduce(mx[k][:], sc[k][:], AX_X, ALU.max).then_inc(max_done.sem, 1)

                dve.wait_ge(prep, 1)
                dve.tensor_copy(nds[:], misc[:, 4:5])
                ln.link(dve.tensor_copy(biasT[:], misc[:, 0:4]))
                ln.link(dve.tensor_scalar(nds[:], nds[:], -1.0, None, ALU.mult))
                dve.tensor_scalar(biasq4[:], biasT[:, 0:1], DK ** -0.5, None, ALU.mult)
                dve.wait_ge(head_made, 5)
                dve.tensor_copy(bv_col[:], biasT[:, 2:3]).then_inc(prep, 1)
                dve.wait_ge(prep, 3)
                dve.tensor_tensor(bo_row[:], bo_row[:], misc[0:1, 8:8 + P], ALU.add).then_inc(prep, 1)
                normalise(0)
                penalty(0, 0, 0)
                dve.wait_ge(xT_ready.sem, xT_ready.done(0))
                normalise(1)
                mask_k(0, 0)
                maxima(0, 0, 0)
                maxima(0, 0, 1)
                with dve.Fori(0, c.turns) as i:
                    for u in range(2):
                        g = i * 2 + u
                        for b in range(GB):
                            dve.wait_ge(o_ready.sem, o_ready.done(g, b))
                            dve.reciprocal(rd[:], heads_o[:, :, DK:DK + 1]).then_inc(inv_done.sem, 1)
                            dve.wait_ge(inv_done.sem, inv_done.done(g, b))
                            dve.tensor_tensor(on[:], heads_o[:, :, 0:DK], rd[:].to_broadcast([P, HEADS, DK]), ALU.mult)\
                                .then_inc(on_done.sem, 1)
                            if b == 1:
                                mask_k(g + 1, 1 - u)
                            dve.wait_ge(wT_ready.sem, wT_ready.done(g, b))
                            maxima(g, u, b + 2)
                            if b == 0:
                                penalty(g + 1, 1 - u, i + u)
                            if b == 1:
                                normalise(g + 2)
                        dve.wait_ge(y_ready.sem, y_ready.done(g))
                        dve.tensor_tensor(xg[:, g, :, :], xg[:, g, :, :], misc[:].rearrange("p (b f) -> p b f", b=GB), ALU.add)\
                            .then_inc(x_added.sem, 1)
                        dve.wait_ge(x_added.sem, x_added.done(g))
                        for b in range(GB):
                            dve.bn_stats(sg[:, g, b, :], xg[:, g, b, :])

            @block.tensor
            def _(pe):
                def turn(g):
                    pe.wait_ge(xn_ready.sem, xn_ready.done(g))
                    for b in range(GB):
                        last = pe.transpose(misc[:, b * P:(b + 1) * P], xn[:, b, :], c.ident[:])
                    last.then_inc(xT_ready.sem, 1)

                def make_k(g):
                    pe.wait_ge(xT_copied.sem, xT_copied.done(g))
                    pe.matmul(misc[:], w["k"][:], xT[:], start=True, stop=True).then_inc(k_ready.sem, 1)

                def make_q(g):
                    pe.wait_ge(k_copied.sem, k_copied.done(g))
                    pe.matmul(misc[:], w["q"][:], xT[:], start=True, stop=True).then_inc(q_ready.sem, 1)

                def make_v(g):
                    pe.wait_ge(q_copied.sem, q_copied.done(g))
                    for b in range(GB):
                        last = pe.matmul(misc[:, b * P:(b + 1) * P], xT[:, b * P:(b + 1) * P], w["v"][:], start=True, stop=True)
                    last.then_inc(v_ready.sem, 1)

                def take_scores(g, u, b):
                    v = (u + b // GB) % 2
                    at = slice(b % GB * P, b % GB * P + P)
                    if b % GB == 0:
                        for ready in (q_copied, km_low, km_high):
                            pe.wait_ge(ready.sem, ready.done(g + b // GB))
                    for k in range(2):
                        last = pe.matmul(scores[b % 2][:, k * half:(k + 1) * half, :], qT[v][:, at],
                                         km[v][:, k * half:(k + 1) * half, at], start=True, stop=True)
                    last.then_inc(score_ready.sem, 1)

                def turn_weights(g, b):
                    pe.wait_ge(exp_done.sem, exp_done.done(g, b))
                    for h in range(HEADS):
                        last = pe.transpose(turned_w[:, h, :], sc[b % 2][:, h, :], c.ident[:])
                    last.then_inc(wT_ready.sem, 1)

                pe.wait_ge(loaded, 160)
                pe.transpose(misc[:, 0:4], bias_rows[:], c.ident[0:4, 0:4])
                pe.matmul(misc[:, 4:5], c.ones[0:1, :], ds[:], start=True, stop=True).then_inc(prep, 1)
                pe.wait_ge(prep, 2)
                pe.matmul(misc[0:1, 8:8 + P], bv_col[:], w["o"][:], start=True, stop=True).then_inc(prep, 1)
                pe.wait_ge(prep, 4)
                turn(0)
                make_k(0)
                make_q(0)
                make_v(0)
                pe.wait_ge(v_copied.sem, v_copied.done(0))
                turn(1)
                take_scores(0, 0, 0)
                take_scores(0, 0, 1)
                turn_weights(0, 0)
                take_scores(0, 0, 2)
                with pe.Fori(0, c.turns) as i:
                    for u in range(2):
                        g = i * 2 + u
                        for b in range(GB):
                            pe.wait_ge(wT_copied.sem, wT_copied.done(g, b))
                            pe.wait_ge(oT_copied.sem, oT_copied.done(g, b - 1))
                            for h in range(HEADS):
                                last = pe.matmul(heads_o[:, h, :], pT[b % 2][:, h, :], va[u][:, b, h, :], start=True, stop=True)
                            last.then_inc(o_ready.sem, 1)
                            if b == 0:
                                pe.wait_ge(x_added.sem, x_added.done(g, -1))
                                make_k(g + 1)
                            turn_weights(g, b + 1)
                            pe.wait_ge(on_done.sem, on_done.done(g, b))
                            pe.transpose(turned_o, on[:].rearrange("p h d -> p (h d)"), c.ident[:]).then_inc(oT_ready.sem, 1)
                            if b == 0:
                                make_q(g + 1)
                            if b == 1:
                                make_v(g + 1)
                            if b == 2:
                                pe.wait_ge(v_copied.sem, v_copied.done(g + 1))
                                turn(g + 2)
                            take_scores(g, u, b + 3)
                        pe.wait_ge(oT_copied.sem, oT_copied.done(g, GB - 1))
                        pe.wait_ge(xT_copied.sem, xT_copied.done(g + 2))
                        for b in range(GB):
                            at = slice(b * P, (b + 1) * P)
                            pe.matmul(misc[:, at], c.ones[0:1, :], bo_row[:], start=True, stop=False)
                            last = pe.matmul(misc[:, at], oT[:, at], w["o"][:], start=False, stop=True)
                        last.then_inc(y_ready.sem, 1)


def mean_messages(c):
    nc, io = c.nc, c.io
    xg, sg = c.grouped(c.x), c.grouped(c.stats)
    meang, rstdg = c.grouped(c.mean), c.grouped(c.rstd)
    adjg = io["adj"].rearrange("(g b) i j -> g i b j", b=GB)
    with ExitStack() as ctx:
        sb = lambda name, shape, dt=F32: c.sb("mm_" + name, shape, dt, ctx)
        sem = lambda name: c.sem("mm_" + name)
        wm, wu, bias = sb("wm", [P, P]), sb("wu", [P, P]), sb("bias", [1, P])
        adj_i = [sb(f"adj_i{u}", [P, GB, P], I32) for u in range(2)]
        adj_f = [sb(f"adj_f{u}", [P, GB, P]) for u in range(2)]
        ha = [sb(f"ha{u}", [P, GB, P + 1]) for u in range(2)]
        up = [sb(f"up{u}", [P, GB, P]) for u in range(2)]
        xn, xT = sb("xn", [P, GB, P]), sb("xT", [P, T])
        deg, rdeg = sb("deg", [P, GB]), sb("rdeg", [P, GB])
        turned, h_bank, up_bank = (c.ps("mm_" + n, ctx) for n in ("turned", "h_bank", "up_bank"))
        msg_bank = [[c.ps(f"mm_msg{u}{k}", ctx) for k in range(2)] for u in range(2)]
        loaded, chain, rooted, ones = (sem(n) for n in ("loaded", "chain", "rooted", "ones"))
        adj_in = [sem(f"adj_in{u}") for u in range(2)]
        adj_ready, xn_ready, xT_ready, xT_copied, h_ready, msg_ready = (
            Count(sem(n), 1) for n in ("adj_ready", "xn_ready", "xT_ready", "xT_copied", "h_ready", "msg_ready"))
        h_copied = Count(sem("h_copied"), 1)
        x_added = Count(sem("x_added"), 1, 2)
        scale = Count(sem("scale"), 4)
        summed = Count(sem("summed"), 1)
        wide = "p (b f) -> p b f"
        with nc.Block() as block:

            @block.sync
            def _(sp):
                sp.dma_start(wm[:], io["L2_gnn_W_msg"]).then_inc(loaded, 16)
                sp.dma_start(wu[:], io["L2_gnn_W_upd"]).then_inc(loaded, 16)
                sp.dma_start(bias[:], io["L2_gnn_bias"].rearrange("(o d) -> o d", o=1)).then_inc(loaded, 16)
                load_adjacency(c, sp, adj_i, adjg, adj_in, adj_ready)

            @block.gpsimd
            def _(pool):
                for u in range(2):
                    pool.memset(ha[u][:], 1.0).then_inc(ones, 1)

            @block.scalar
            def _(act):
                ln_act(c, act, rooted, False)
                def copy_xT(g):
                    act.wait_ge(xT_ready.sem, xT_ready.done(g))
                    act.activation(xT[:], turned[:], ACT.Copy).then_inc(xT_copied.sem, 1)

                def copy_h(g, u):
                    act.wait_ge(h_ready.sem, h_ready.done(g))
                    act.activation(ha[u][:, :, 0:P], h_bank[:].rearrange(wide, b=GB), ACT.Copy)
                    act.wait_ge(x_added.sem, x_added.done(g, -2))
                    act.activation(up[u][:], up_bank[:].rearrange(wide, b=GB), ACT.Copy).then_inc(h_copied.sem, 1)

                act.wait_ge(ones, 2)
                copy_xT(0)
                copy_h(0, 0)
                copy_xT(1)
                with act.Fori(0, c.turns) as i:
                    for u in range(2):
                        copy_h(i * 2 + u + 1, 1 - u)
                        copy_xT(i * 2 + u + 2)

            @block.vector
            def _(dve):
                ln_dve(c, dve, Chain(dve, chain), rooted, False)
                dve.sem_inc(x_added.sem, x_added.credit)

                def adjacency(g, u, nth):
                    dve.wait_ge(adj_in[u], nth * 16 + 16)
                    dve.tensor_copy(adj_f[u][:], adj_i[u][:]).then_inc(adj_ready.sem, 1)

                def normalise(g, before=None):
                    if before is not None:
                        dve.wait_ge(xT_ready.sem, xT_ready.done(before))
                    for b in range(GB):
                        last = dve.tensor_scalar(xn[:, b, :], xg[:, g, b, :], meang[:, g, b:b + 1], rstdg[:, g, b:b + 1],
                                                 ALU.subtract, ALU.mult)
                    last.then_inc(xn_ready.sem, 1)

                normalise(0)
                adjacency(0, 0, 0)
                normalise(1, 0)
                adjacency(1, 1, 0)
                with dve.Fori(0, c.turns) as i:
                    for u in range(2):
                        g = i * 2 + u
                        normalise(g + 2, g + 1)
                        msg = lambda b: msg_bank[u][b // 2][:, b % 2 * (P + 1):(b % 2 + 1) * (P + 1)]
                        dve.wait_ge(msg_ready.sem, msg_ready.done(g))
                        for b in range(GB):
                            last = dve.tensor_copy(deg[:, b:b + 1], msg(b)[:, P:P + 1])
                        last.then_inc(scale.sem, 1)
                        dve.wait_ge(scale.sem, scale.done(g, 0))
                        dve.tensor_scalar(rdeg[:], deg[:], 1.0, None, ALU.max).then_inc(scale.sem, 1)
                        dve.wait_ge(scale.sem, scale.done(g, 1))
                        dve.reciprocal(rdeg[:], rdeg[:])
                        dve.tensor_scalar(deg[:], deg[:], 0.0, None, ALU.is_gt).then_inc(scale.sem, 1)
                        dve.wait_ge(scale.sem, scale.done(g, 2))
                        dve.tensor_tensor(rdeg[:], rdeg[:], deg[:], ALU.mult).then_inc(scale.sem, 1)
                        dve.wait_ge(h_copied.sem, h_copied.done(g))
                        dve.wait_ge(scale.sem, scale.done(g, 3))
                        for b in range(GB):
                            last = dve.scalar_tensor_tensor(up[u][:, b, :], msg(b)[:, 0:P], rdeg[:, b:b + 1], up[u][:, b, :],
                                                            ALU.mult, ALU.add)
                        last.then_inc(summed.sem, 1)
                        dve.wait_ge(summed.sem, summed.done(g))
                        dve.scalar_tensor_tensor(xg[:, g, :, :], up[u][:], 0.0, xg[:, g, :, :], ALU.max, ALU.add)\
                            .then_inc(x_added.sem, 1)
                        adjacency(g + 2, u, i + 1)
                        dve.wait_ge(x_added.sem, x_added.done(g))
                        for b in range(GB):
                            dve.bn_stats(sg[:, g, b, :], xg[:, g, b, :])

            @block.tensor
            def _(pe):
                def turn(g, before=None):
                    pe.wait_ge(xn_ready.sem, xn_ready.done(g))
                    if before is not None:
                        pe.wait_ge(xT_copied.sem, xT_copied.done(before))
                    for b in range(GB):
                        last = pe.transpose(turned[:, b * P:(b + 1) * P], xn[:, b, :], c.ident[:])
                    last.then_inc(xT_ready.sem, 1)

                def products(g, before=None):
                    pe.wait_ge(xT_copied.sem, xT_copied.done(g))
                    if before is not None:
                        pe.wait_ge(h_copied.sem, h_copied.done(before))
                    for b in range(GB):
                        at = slice(b * P, (b + 1) * P)
                        pe.matmul(h_bank[:, at], xT[:, at], wm[:], start=True, stop=True)
                        pe.matmul(up_bank[:, at], c.ones[0:1, :], bias[:], start=True, stop=False)
                        last = pe.matmul(up_bank[:, at], xT[:, at], wu[:], start=False, stop=True)
                    last.then_inc(h_ready.sem, 1)

                pe.wait_ge(loaded, 48)
                turn(0)
                products(0)
                turn(1, 0)
                with pe.Fori(0, c.turns) as i:
                    for u in range(2):
                        g = i * 2 + u
                        pe.wait_ge(h_copied.sem, h_copied.done(g))
                        pe.wait_ge(adj_ready.sem, adj_ready.done(g))
                        pe.wait_ge(x_added.sem, x_added.done(g, -2))
                        for b in range(GB):
                            last = pe.matmul(msg_bank[u][b // 2][:, b % 2 * (P + 1):(b % 2 + 1) * (P + 1)], adj_f[u][:, b, :],
                                             ha[u][:, b, :], start=True, stop=True)
                        last.then_inc(msg_ready.sem, 1)
                        products(g + 1, g)
                        turn(g + 2, g + 1)


def edge_gates(c):
    nc, io = c.nc, c.io
    xg, sg = c.grouped(c.x), c.grouped(c.stats)
    meang, rstdg = c.grouped(c.mean), c.grouped(c.rstd)
    adjg = io["adj"].rearrange("(g b) i j -> g i b j", b=GB)
    K = 4
    with ExitStack() as ctx:
        sb = lambda name, shape, dt=F32: c.sb("eg_" + name, shape, dt, ctx)
        sem = lambda name: c.sem("eg_" + name)
        a, bias = sb("a", [P, K]), sb("bias", [1, P])
        adj_i = [sb(f"adj_i{u}", [P, GB, P], I32) for u in range(2)]
        xn = [sb(f"xn{u}", [P, GB, P]) for u in range(2)]
        xT = [sb(f"xT{u}", [P, T]) for u in range(2)]
        adjT = [sb(f"adjT{u}", [P, GB, P]) for u in range(2)]
        ax = [sb(f"ax{u}", [P, K, T]) for u in range(2)]
        known = [sb(f"known{u}", [P, GB, P]) for u in range(2)]
        adj_f, kind, e = sb("adj_f", [P, GB, P]), sb("kind", [P, K, GB, P], I32), sb("e", [P, GB, P])
        scores = c.ps("eg_scores", ctx, (P, GB, T))
        turned, turned_adj, out = (c.ps("eg_" + n, ctx) for n in ("turned", "turned_adj", "out"))
        loaded, chain, rooted = (sem(n) for n in ("loaded", "chain", "rooted"))
        adj_in = [sem(f"adj_in{u}") for u in range(2)]
        adj_ready, xn_ready, xT_ready, adjT_ready, xT_copied, adjT_copied, ax_ready, mask_made, known_made = (
            Count(sem(n), 1) for n in ("adj_ready", "xn_ready", "xT_ready", "adjT_ready", "xT_copied", "adjT_copied",
                                       "ax_ready", "mask_made", "known_made"))
        kinds_made, leaky_done, sigmoid_done, alpha_done, out_ready, x_added = (
            Count(sem(n), 1) for n in ("kinds_made", "leaky_done", "sigmoid_done", "alpha_done", "out_ready", "x_added"))
        score_ready, picked = Count(sem("score_ready"), 2), Count(sem("picked"), 2 * K)
        wide = "p (b f) -> p b f"
        halves = [slice(0, GB // 2), slice(GB // 2, GB)]
        with nc.Block() as block:

            @block.sync
            def _(sp):
                for k in range(K):
                    sp.dma_start(a[:, k:k + 1], io[f"L3_gnn_a{k}"], allow_slow_non_contiguous=True).then_inc(loaded, 16)
                sp.dma_start(bias[:], io["L3_gnn_bias"].rearrange("(o d) -> o d", o=1)).then_inc(loaded, 16)
                load_adjacency(c, sp, adj_i, adjg, adj_in, adj_ready)

            @block.scalar
            def _(act):
                ln_act(c, act, rooted, False)
                def scaled(g, u):
                    act.wait_ge(xT_copied.sem, xT_copied.done(g))
                    for k in range(K):
                        last = act.activation(ax[u][:, k, :], xT[u][:], ACT.Copy, scale=a[:, k:k + 1])
                    last.then_inc(ax_ready.sem, 1)

                def copies(g, u):
                    act.wait_ge(xT_ready.sem, xT_ready.done(g))
                    act.activation(xT[u][:], turned[:], ACT.Copy).then_inc(xT_copied.sem, 1)
                    act.wait_ge(adjT_ready.sem, adjT_ready.done(g))
                    act.activation(adjT[u][:], turned_adj[:].rearrange(wide, b=GB), ACT.Copy).then_inc(adjT_copied.sem, 1)

                act.wait_ge(loaded, 80)
                for g in range(2):
                    copies(g, g)
                    scaled(g, g)
                with act.Fori(0, c.turns) as i:
                    for u in range(2):
                        g = i * 2 + u
                        act.wait_ge(leaky_done.sem, leaky_done.done(g))
                        act.activation(e[:], e[:], ACT.Sigmoid).then_inc(sigmoid_done.sem, 1)
                        copies(g + 2, u)
                        scaled(g + 2, u)

            @block.vector
            def _(dve):
                ln_dve(c, dve, Chain(dve, chain), rooted, False)

                def adjacency(g, u, nth):
                    dve.wait_ge(adj_in[u], nth * 16 + 16)
                    dve.tensor_copy(adj_f[:], adj_i[u][:]).then_inc(adj_ready.sem, 1)

                def normalise(g, u):
                    for b in range(GB):
                        last = dve.tensor_scalar(xn[u][:, b, :], xg[:, g, b, :], meang[:, g, b:b + 1], rstdg[:, g, b:b + 1],
                                                 ALU.subtract, ALU.mult)
                    last.then_inc(xn_ready.sem, 1)

                def mask(g, u):
                    dve.wait_ge(adjT_copied.sem, adjT_copied.done(g))
                    dve.tensor_scalar(known[u][:], adjT[u][:], 1.0, None, ALU.is_ge).then_inc(mask_made.sem, 1)
                    dve.wait_ge(mask_made.sem, mask_made.done(g))
                    dve.scalar_tensor_tensor(known[u][:], adjT[u][:], float(K), known[u][:], ALU.is_le, ALU.mult)\
                        .then_inc(known_made.sem, 1)

                def kinds(g, u):
                    for k in range(1, K):
                        last = dve.tensor_scalar(kind[:, k, :, :], adjT[u][:], float(k + 1), None, ALU.is_equal)
                    last.then_inc(kinds_made.sem, 1)

                normalise(0, 0)
                adjacency(0, 0, 0)
                mask(0, 0)
                kinds(0, 0)
                normalise(1, 1)
                adjacency(1, 1, 0)
                with dve.Fori(0, c.turns) as i:
                    for u in range(2):
                        g = i * 2 + u
                        for h, half in enumerate(halves):
                            ek = lambda k: scores[:, half, k * P:(k + 1) * P]
                            dve.wait_ge(score_ready.sem, score_ready.done(g, h))
                            dve.tensor_copy(e[:, half, :], ek(0)).then_inc(picked.sem, 1)
                            dve.wait_ge(kinds_made.sem, kinds_made.done(g))
                            for k in range(1, K):
                                dve.wait_ge(picked.sem, picked.done(g, h * K + k - 1))
                                dve.memset(c.pace[:], 0.0)
                                dve.copy_predicated(e[:, half, :], kind[:, k, half, :], ek(k)).then_inc(picked.sem, 1)
                        dve.wait_ge(picked.sem, picked.done(g, 2 * K - 1))
                        dve.scalar_tensor_tensor(e[:], e[:], 0.2, e[:], ALU.mult, ALU.max).then_inc(leaky_done.sem, 1)
                        mask(g + 1, 1 - u)
                        dve.wait_ge(sigmoid_done.sem, sigmoid_done.done(g))
                        dve.wait_ge(known_made.sem, known_made.done(g))
                        dve.tensor_tensor(e[:], e[:], known[u][:], ALU.mult).then_inc(alpha_done.sem, 1)
                        kinds(g + 1, 1 - u)
                        dve.wait_ge(adjT_ready.sem, adjT_ready.done(g + 1))
                        adjacency(g + 2, u, i + 1)
                        dve.wait_ge(out_ready.sem, out_ready.done(g))
                        dve.tensor_tensor(xg[:, g, :, :], xg[:, g, :, :], out[:].rearrange(wide, b=GB), ALU.add)\
                            .then_inc(x_added.sem, 1)
                        normalise(g + 2, u)
                        dve.wait_ge(x_added.sem, x_added.done(g))
                        for b in range(GB):
                            dve.bn_stats(sg[:, g, b, :], xg[:, g, b, :])

            @block.tensor
            def _(pe):
                def turn(g, u, before=None):
                    pe.wait_ge(xn_ready.sem, xn_ready.done(g))
                    if before is not None:
                        pe.wait_ge(adjT_copied.sem, adjT_copied.done(before))
                    for b in range(GB):
                        last = pe.transpose(turned[:, b * P:(b + 1) * P], xn[u][:, b, :], c.ident[:])
                    last.then_inc(xT_ready.sem, 1)
                    pe.wait_ge(adj_ready.sem, adj_ready.done(g))
                    for b in range(GB):
                        last = pe.transpose(turned_adj[:, b * P:(b + 1) * P], adj_f[:, b, :], c.ident[:])
                    last.then_inc(adjT_ready.sem, 1)

                def take_scores(g, u, h, before=None):
                    pe.wait_ge(ax_ready.sem, ax_ready.done(g))
                    if before is not None:
                        pe.wait_ge(picked.sem, picked.done(before, h * K + K - 1))
                    for b in range(GB)[halves[h]]:
                        at = slice(b * P, (b + 1) * P)
                        last = pe.matmul(scores[:, b, :], xT[u][:, at], ax[u][:, :, at], start=True, stop=True)
                    last.then_inc(score_ready.sem, 1)

                pe.wait_ge(loaded, 80)
                turn(0, 0)
                take_scores(0, 0, 0)
                take_scores(0, 0, 1)
                turn(1, 1, 0)
                with pe.Fori(0, c.turns) as i:
                    for u in range(2):
                        g = i * 2 + u
                        take_scores(g + 1, 1 - u, 0, g)
                        pe.wait_ge(alpha_done.sem, alpha_done.done(g))
                        for b in range(GB):
                            at = slice(b * P, (b + 1) * P)
                            pe.matmul(out[:, at], c.ones[0:1, :], bias[:], start=True, stop=False)
                            last = pe.matmul(out[:, at], e[:, b, :], xn[u][:, b, :], start=False, stop=True)
                        last.then_inc(out_ready.sem, 1)
                        take_scores(g + 1, 1 - u, 1, g)
                        turn(g + 2, u, g + 1)

SH = 8
SP = P // 2
CK = 4
CONV = 3
Z0, X0, B0, C0, B1, DT0, IN_COLS = 0, 512, 1024, 1088, 1152, 1216, 1232


def slices(c):
    nc, io = c.nc, c.io
    xg, sg = c.grouped(c.x), c.grouped(c.stats)
    meang, rstdg = c.grouped(c.mean), c.grouped(c.rstd)
    PAIRS = GB // 2
    W = 2 * P
    row = lambda v: v.rearrange("(o d) -> o d", o=1)
    with ExitStack() as ctx:
        sb = lambda name, shape, dt=F32: c.sb("sl_" + name, shape, dt, ctx)
        sem = lambda name: c.sem("sl_" + name)
        in_t, ho_t, ow_t, fc_t = sb("in_t", [P, CK, IN_COLS]), sb("ho_t", [P, CK, CK * P]), sb("ow_t", [P, CK, P]), sb("fc_t", [P, CK, SH])
        fx_t, wc, bc, bfx = sb("fx_t", [P, CK, P]), sb("wc", [P, SH, SP]), sb("bc", [P, SH, SP]), sb("bfx", [P, CK * P])
        cw, cb = sb("cw", [P, 6, CONV]), sb("cb", [P, 6])
        ob = sb("ob", [1, P])
        heads_all = sb("heads_all", [P, 5, SH])
        a2 = sb("a2", [P, 2, SH])
        up, low = sb("up", [P, SP]), sb("low", [P, SP])
        seg_f, seg_b = sb("seg_f", [P, P]), sb("seg_b", [P, P])
        xn, xT = sb("xn", [P, GB, P]), sb("xT", [P, T])
        sw = [sb(f"sw{b}", [P, SH, SP]) for b in range(GB)]
        fx = [sb(f"fx{b}", [P, CK * P]) for b in range(2)]
        rs = sb("rs", [P, CK])
        inv = sb("inv", [P, CK, SP])
        eye2, same = sb("eye2", [P, SP]), sb("same", [P, P])
        mx, sm = sb("mx", [P, GB, SH]), sb("sm", [P, GB, SH])
        st = [sb(f"st{u}", [P, CK, GB, SP]) for u in range(2)]
        swT = [sb(f"swT{u}", [P, GB, CK, P]) for u in range(2)]
        zs = [sb(f"zs{q}", [P, CK * P]) for q in range(PAIRS)]
        xa, xe = sb("xa", [P, 6, GB, SP]), sb("xe", [P, 6, GB, SP])
        dt, dn, de, dl, du, dc = (sb(n, [P, PAIRS, 2, SH]) for n in ("dt", "dn", "de", "dl", "du", "dc"))
        seg_rhs = [sb(f"seg_rhs{k}", [P, SH, SP]) for k in range(2)]
        dec = [sb(f"dec{q}", [P, SH, SP]) for q in range(PAIRS)]
        bcp = [sb(f"bcp{q}", [P, SP + 2]) for q in range(PAIRS)]
        gu, gd = sb("gu", [P, SP]), sb("gd", [P, SP])
        m1, m2 = sb("m1", [P, SH, SP]), sb("m2", [P, SH, SP])
        mb = [sb(f"mb{q}", [P, SH, P]) for q in range(PAIRS)]
        fcd = sb("fcd", [P, PAIRS, SH])
        xs = [sb(f"xs{q}", [P, SH, SP]) for q in range(PAIRS)]
        y = [sb(f"y{q}", [P, CK * P]) for q in range(PAIRS)]
        ms, rms = sb("ms", [P, PAIRS]), sb("rms", [P, PAIRS])
        yT = sb("yT", [P, CK, PAIRS, P])
        otb = sb("otb", [P, CK, GB, P])
        zz = [sb(f"zz{k}", [P, CK, P]) for k in range(2)]
        bank = [c.ps(f"sl_bank{k}", ctx) for k in range(8)]
        heads8 = lambda ap: ap.rearrange("p (h f) -> p h f", h=SH)

        rows_up, rows_read = sem("rows_up"), sem("rows_read")
        small_in, pre, masks, chain, rooted = sem("small_in"), sem("pre"), sem("masks"), sem("chain"), sem("rooted")
        with ExitStack() as ctx2:
            sb2 = lambda name, shape, dt=F32: c.sb("sw_" + name, shape, dt, ctx2)
            RAW = 4
            rows = [sb2(f"rows{k}", [P, CK * P]) for k in range(RAW)]
            rows_in = [sem(f"rows_in{k}") for k in range(RAW)]
            vec_rows, vecs = sb2("vec_rows", [2 * CK, P]), sb2("vecs", [P, 2 * CK])
            ws2, wsT = sb2("ws2", [SP, 2, SP]), sb2("wsT", [P, SP])
            wx = sb2("wx", [P, CK, P])
            heads_row = sb2("heads_row", [1, 5, SH])
            bfx_row, bs_row, bs_all = sb2("bfx_row", [1, CK * P]), sb2("bs_row", [1, SP]), sb2("bs_all", [P, SP])
            bx_wide = sb2("bx_wide", [P, CK, P])
            cols = [(io["L2_ffn_hy_in_w"][128 * k:128 * k + 128, :], P, in_t[:, :, 128 * k:128 * k + 128]) for k in range(9)]
            cols += [(io["L2_ffn_hy_in_w"][1152:1168, :], 16, in_t[:, :, DT0:DT0 + 16]),
                     (io["L2_ffn_hy_in_w"][B0:C0, :], SP, in_t[:, :, B1:B1 + SP])]
            cols += [(io["L2_ffn_hy_out_w"][128 * k:128 * k + 128, :], P, ho_t[:, :, 128 * k:128 * k + 128]) for k in range(4)]
            cols += [(io["L2_ffn_out_w"], P, ow_t[:]), (io["L2_ffn_hy_fcD_w"], SH, fc_t[:]),
                     (io["L2_ffn_W_fx"].rearrange("(j p) d -> p j d", p=P), P, fx_t[:])]
            conv_w, conv_b = io["L2_ffn_hy_conv_w"], io["L2_ffn_hy_conv_b"].rearrange("(c o) -> c o", o=1)
            smalls = [(vec_rows[0:CK, :], io["L2_ffn_hy_norm_w"].rearrange("(k p) -> k p", p=P)),
                      (vec_rows[CK:2 * CK, :], io["L2_ffn_b_x"].rearrange("(k p) -> k p", p=P)),
                      (ws2[:, 0, :], io["L2_ffn_W_slice"]), (ws2[:, 1, :], io["L2_ffn_W_slice"]),
                      (wx[:], io["L2_ffn_W_x"].rearrange("(j p) d -> p j d", p=P)),
                      (heads_row[:, 0, :], io["L2_ffn_temperature"].rearrange("a h b c -> a (h b c)")),
                      (heads_row[:, 1, :], row(io["L2_ffn_hy_D"])), (heads_row[:, 2, :], row(io["L2_ffn_hy_dt_bias"])),
                      (heads_row[:, 3, :], row(io["L2_ffn_hy_dt_bias"])), (heads_row[:, 4, :], row(io["L2_ffn_hy_A_log"])),
                      (bfx_row[:], row(io["L2_ffn_b_fx"])), (bs_row[:], row(io["L2_ffn_b_slice"])),
                      (ob[:], row(io["L2_ffn_out_b"]))]
            smalls += [(cw[:, 0:CK, :], conv_w[0:CK * P, :].rearrange("(j p) k -> p j k", p=P)),
                       (cb[:, 0:CK], conv_b[0:CK * P, :].rearrange("(j p) o -> p (j o)", p=P))]
            for p0, j, ch0 in ((0, 4, 512), (SP, 4, 576), (0, 5, 576), (SP, 5, 512)):
                smalls += [(cw[p0:p0 + SP, j, :], conv_w[ch0:ch0 + SP, :]), (cb[p0:p0 + SP, j:j + 1], conv_b[ch0:ch0 + SP, :])]
            with nc.Block() as block:

                @block.sync
                def _(sp):
                    for k, (src, n, _) in enumerate(cols):
                        if k == RAW:
                            for small_dst, small_src in smalls:
                                sp.dma_start(small_dst, small_src, allow_slow_non_contiguous=True).then_inc(small_in, 16)
                        if k >= RAW:
                            sp.wait_ge(rows_up, k - RAW + 1)
                        dst = rows[k % RAW][0:n, :]
                        if len(src.shape) == 3:
                            dst = dst.rearrange("p (j d) -> p j d", d=P)
                        sp.dma_start(dst, src).then_inc(rows_in[k % RAW], 16)

                @block.gpsimd
                def _(pool):
                    link = Chain(pool, masks).link
                    pool.memset(up[:], 1.0)
                    pool.memset(low[:], 1.0)
                    pool.memset(seg_f[:], 0.0)
                    pool.memset(seg_b[:], 0.0)
                    for q in range(PAIRS):
                        pool.memset(mb[q][:], 0.0)
                        pool.memset(bcp[q][:], 0.0)
                    pool.memset(same[:], 0.0)
                    link(pool.memset(otb[:], 0.0))
                    for r in range(2):
                        half = slice(SP * r, SP * r + SP)
                        link(pool.affine_select(out=up[half, :], in_=up[half, :], compare_op=ALU.is_gt, fill=0.0, base=0,
                                                pattern=[[1, SP]], channel_multiplier=-1))
                        link(pool.affine_select(out=low[half, :], in_=low[half, :], compare_op=ALU.is_gt, fill=0.0, base=0,
                                                pattern=[[-1, SP]], channel_multiplier=1))
                    for r in range(2):
                        half = slice(SP * r, SP * r + SP)
                        link(pool.tensor_copy(seg_f[half, half], low[half, :]))
                        link(pool.tensor_copy(seg_b[half, half], up[half, :]))
                        link(pool.tensor_copy(same[half, half], c.ones[half, half]))
                        link(pool.tensor_copy(eye2[half, :], c.ident[half, half]))

                @block.scalar
                def _(act):
                    ln_act(c, act, rooted, False)
                    for k, (_, n, dst) in enumerate(cols):
                        act.wait_ge(rows_up, k + 1)
                        act.activation(dst, bank[k % 2][:].rearrange("p (j n) -> p j n", j=CK)[:, :, 0:n], ACT.Copy).then_inc(rows_read, 1)
                    act.wait_ge(pre, 4)
                    for k in range(2):
                        act.activation(a2[:, k, :], heads_all[:, 4, :], ACT.Exp)

                @block.vector
                def _(dve):
                    link = Chain(dve, chain)
                    ln_dve(c, dve, link, rooted, False)
                    link = link.link
                    dve.wait_ge(small_in, 16 * len(smalls))
                    link(dve.tensor_scalar(heads_row[:, 0, :], heads_row[:, 0, :], 1e-6, None, ALU.max))
                    dve.reciprocal(heads_row[:, 0, :], heads_row[:, 0, :]).then_inc(pre, 1)
                    dve.wait_ge(pre, 2)
                    dve.tensor_copy(vecs[:], bank[2][:, 0:2 * CK])
                    dve.tensor_copy(wsT[:], bank[3][:, 0:SP])
                    dve.tensor_copy(heads_all[:].rearrange("p k h -> p (k h)"), bank[4][:, 0:5 * SH])
                    dve.tensor_copy(bfx[:], bank[5][:])
                    link(dve.tensor_copy(bs_all[:], bank[6][:, 0:SP]))
                    for k in range(CK):
                        dve.tensor_scalar(bx_wide[:, k, :], c.ones[:], vecs[:, CK + k:CK + k + 1], None, ALU.mult)
                    dve.drain().then_inc(pre, 2)
                    dve.wait_ge(pre, 5)
                    for r in range(2):
                        for n, dst in ((2, wc), (4, bc)):
                            half = dst[:].rearrange("p (k r) g -> p r k g", r=2)[:, r, :, :]
                            temp = heads_all[:, 0, :].rearrange("p (k r) -> p r k", r=2)[:, r, :].unsqueeze(2).to_broadcast([P, CK, SP])
                            src = bank[n + r][:, 0:CK * SP].rearrange("p (k g) -> p k g", k=CK)
                            if dst is bc:
                                link(dve.tensor_tensor(half, src, bs_all[:].unsqueeze(1).to_broadcast([P, CK, SP]), ALU.add))
                                src = half
                            link(dve.tensor_tensor(half, src, temp, ALU.mult))
                    dve.wait_ge(rows_read, len(cols))
                    for k in range(CK):
                        dve.tensor_scalar(ho_t[:, k, :], ho_t[:, k, :], vecs[:, k:k + 1], None, ALU.mult)

                @block.tensor
                def _(pe):
                    for k, (_, n, _) in enumerate(cols):
                        pe.wait_ge(rows_in[k % RAW], 16 * (k // RAW + 1))
                        if k >= 2:
                            pe.wait_ge(rows_read, k - 1)
                        for j in range(CK):
                            last = pe.transpose(bank[k % 2][:, j * P:j * P + n], rows[k % RAW][0:n, j * P:(j + 1) * P], c.ident[0:n, 0:n])
                        last.then_inc(rows_up, 1)
                    pe.wait_ge(small_in, 16 * len(smalls))
                    pe.wait_ge(pre, 1)
                    pe.transpose(bank[2][:, 0:2 * CK], vec_rows[:], c.ident[0:2 * CK, 0:2 * CK])
                    pe.transpose(bank[3][:, 0:SP], ws2[:].rearrange("g r c -> g (r c)"), c.ident[0:SP, 0:SP])
                    pe.matmul(bank[4][:, 0:5 * SH], c.ones[0:1, :], heads_row[:].rearrange("p k h -> p (k h)"), start=True, stop=True)
                    pe.matmul(bank[5][:], c.ones[0:1, :], bfx_row[:], start=True, stop=True)
                    pe.matmul(bank[6][:, 0:SP], c.ones[0:1, :], bs_row[:], start=True, stop=True).then_inc(pre, 1)
                    pe.wait_ge(pre, 4)
                    for r in range(2):
                        half = slice(SP * r, SP * r + SP)
                        for k in range(CK):
                            at = slice(SP * k, SP * k + SP)
                            pe.matmul(bank[2 + r][:, at], wx[half, k, :], wsT[half, :], start=True, stop=True)
                            last = pe.matmul(bank[4 + r][:, at], bx_wide[half, k, :], wsT[half, :], start=True, stop=True)
                    last.then_inc(pre, 1)

        per = lambda names, n: " ".join(f"{k}{b}" for b in range(n) for k in names.split())
        two = lambda names: " ".join(f"{k}{b}" for k in names.split() for b in range(GB))
        xn_ready = Count(sem("xn_ready"), 1)
        av = Steps(sem("a_dve"), two("logit max") + " " + two("sum") + " rsum " + per("fx norm rnorm inv st", GB))
        aa = Steps(sem("a_act"), "xT " + two("exp") + " " + two("swT"))
        ap = Steps(sem("a_pe"), "xT " + two("logit") + " " + per("swT fx total st inv", GB))
        ag = Steps(sem("a_pool"), two("sub") + " " + two("sw"))
        bv = Steps(sem("b_dve"), "zs0 zs1 tap1 tap2 tap45 dt dneg dabs x du dd dc dru dcr dsum dt2 da seg0b seg1b "
                   + "bcp0 bcp1 fcd g0 m0 mm0 g1 m1 mm1 y0 y1 yg0 yg1 mean ygn0 ygn1 ot x_out")
        ba = Steps(sem("b_act"), "z0 z1 xa xa45 xe de dl dec0 dec1 xs0 xs1 ms0 ms1 yT0 yT1 " + two("z_"))
        bp = Steps(sem("b_pe"), "z0 z1 xbc dtbc seg0 seg1 bc0 bc1 fcd xs0 xs1 y0 y1 yT0 yT1 ot z_0 z_1 out0 z_2 out1 z_3 out2 out3")
        bg = Steps(sem("b_pool"), "seg0f seg1f m20 m21 xf0 xf1 rms")

        wide = [P, SH, SP]
        over_t = lambda v: v.unsqueeze(2).to_broadcast(wide)
        over_h = lambda v: v.unsqueeze(1).to_broadcast(wide)

        with nc.Block() as block:

            @block.scalar
            def _(act):
                aa.start(act)
                ba.start(act)
                def turn(g):
                    act.wait_ge(ap.sem, ap.done(g, "xT"))
                    aa.mark(act.activation(xT[:], bank[4][:], ACT.Copy), "xT")

                def soften(g):
                    for b in range(GB):
                        act.wait_ge(ag.sem, ag.done(g, f"sub{b}"))
                        aa.mark(act.activation(sw[b][:], sw[b][:], ACT.Exp), f"exp{b}")

                def copy_weights(g, u, b, before=None):
                    act.wait_ge(ap.sem, ap.done(g, f"swT{b}"))
                    if b == 0 and before is not None:
                        act.wait_ge(bv.sem, bv.all_done(before))
                    aa.mark(act.activation(swT[u][:, b, :, :], bank[4][:].rearrange("p (k n) -> p k n", k=CK), ACT.Copy),
                            f"swT{b}")

                def convolve(g):
                    for q in range(PAIRS):
                        act.wait_ge(bp.sem, bp.done(g, f"z{q}"))
                        ba.mark(act.activation(zs[q][:], bank[q][:], ACT.Sigmoid), f"z{q}")
                    act.wait_ge(bp.sem, bp.done(g, "xbc"))
                    for j in range(4):
                        last = act.activation(xa[:, j, :, :], bank[2 + j // 2][:, j % 2 * W:(j % 2 + 1) * W].rearrange("p (b t) -> p b t", b=GB),
                                              ACT.Identity, bias=cb[:, j:j + 1], scale=cw[:, j, 2:3])
                    ba.mark(last, "xa")
                    act.wait_ge(bp.sem, bp.done(g, "dtbc"))
                    for j in range(4, 6):
                        last = act.activation(xa[:, j, :, :], bank[0][:, j % 2 * W:(j % 2 + 1) * W].rearrange("p (b t) -> p b t", b=GB),
                                              ACT.Identity, bias=cb[:, j:j + 1], scale=cw[:, j, 2:3])
                    ba.mark(last, "xa45")

                def silu(g):
                    act.wait_ge(bv.sem, bv.done(g, "tap45"))
                    ba.mark(act.activation(xe[:], xa[:], ACT.Sigmoid), "xe")

                def steps(g):
                    act.wait_ge(bv.sem, bv.done(g, "dabs"))
                    ba.mark(act.activation(de[:], dn[:], ACT.Exp, scale=-1.0), "de")
                    act.wait_ge(bv.sem, bv.done(g, "du"))
                    ba.mark(act.activation(dl[:], du[:], ACT.Ln), "dl")

                def model(g):
                    for q in range(PAIRS):
                        act.wait_ge(bp.sem, bp.done(g, f"seg{q}"))
                        ba.mark(act.activation(dec[q][:], heads8(bank[2 + q][:]), ACT.Exp, scale=-1.0), f"dec{q}")
                    for q in range(PAIRS):
                        act.wait_ge(bp.sem, bp.done(g, f"xs{q}"))
                        ba.mark(act.activation(xs[q][:], heads8(bank[2 + q][:]), ACT.Copy), f"xs{q}")

                def squares(g):
                    for q in range(PAIRS):
                        act.wait_ge(bv.sem, bv.done(g, f"yg{q}"))
                        ba.mark(act.activation(zs[q][:], y[q][:], ACT.Square, accum_out=ms[:, q:q + 1]), f"ms{q}")

                def turn_y(g):
                    for q in range(PAIRS):
                        act.wait_ge(bp.sem, bp.done(g, f"yT{q}"))
                        ba.mark(act.activation(yT[:, :, q, :], bank[2 + q][:].rearrange("p (k n) -> p k n", k=CK), ACT.Copy), f"yT{q}")

                def spread(g):
                    for b in range(GB):
                        act.wait_ge(bp.sem, bp.done(g, f"z_{b}"))
                        if b >= 2:
                            act.wait_ge(bp.sem, bp.done(g, f"out{b - 2}"))
                        ba.mark(act.activation(zz[b % 2][:], bank[2 + b % 2][:].rearrange("p (k n) -> p k n", k=CK), ACT.Copy),
                                f"z_{b}")

                turn(0)
                soften(0)
                for b in range(GB):
                    copy_weights(0, 0, b)
                turn(1)
                soften(1)
                with act.Fori(0, c.turns) as i:
                    for u in range(2):
                        g = i * 2 + u
                        convolve(g)
                        copy_weights(g + 1, 1 - u, 0, g)
                        silu(g)
                        steps(g)
                        copy_weights(g + 1, 1 - u, 1)
                        model(g)
                        copy_weights(g + 1, 1 - u, 2)
                        copy_weights(g + 1, 1 - u, 3)
                        turn(g + 2)
                        squares(g)
                        turn_y(g)
                        spread(g)
                        soften(g + 2)

            @block.gpsimd
            def _(pool):
                ag.start(pool)
                bg.start(pool)
                def soften(g):
                    for b in range(GB):
                        pool.wait_ge(av.sem, av.done(g, f"max{b}"))
                        ag.mark(pool.tensor_tensor(sw[b][:], sw[b][:], over_t(mx[:, b, :]), ALU.subtract), f"sub{b}")

                def weights(g):
                    for b in range(GB):
                        pool.wait_ge(av.sem, av.done(g, "rsum"))
                        ag.mark(pool.tensor_tensor(sw[b][:], sw[b][:], over_t(sm[:, b, :]), ALU.mult), f"sw{b}")

                def model(g):
                    for q in range(PAIRS):
                        pool.wait_ge(bv.sem, bv.done(g, "da"))
                        if q:
                            pool.wait_ge(bp.sem, bp.done(g, f"seg{q - 1}"))
                        bg.mark(pool.tensor_tensor(seg_rhs[0][:], over_t(dn[:, q, 0, :]), over_h(up[:]), ALU.mult), f"seg{q}f")
                    for q in range(PAIRS):
                        pool.wait_ge(bv.sem, bv.done(g, f"g{q}"))
                        bg.mark(pool.tensor_tensor(m2[:], over_t(dt[:, q, 1, :]), over_h(gd[:]), ALU.mult), f"m2{q}")
                    for q in range(PAIRS):
                        pool.wait_ge(bv.sem, bv.done(g, "fcd"))
                        pool.wait_ge(ba.sem, ba.done(g, f"xs{q}"))
                        bg.mark(pool.tensor_tensor(heads8(y[q][:]), xs[q][:], over_t(fcd[:, q, :]), ALU.mult), f"xf{q}")
                    pool.wait_ge(bv.sem, bv.done(g, "mean"))
                    bg.mark(pool.tensor_tensor(rms[:], ms[:], c.mhalf[:, 0:PAIRS], ALU.pow), "rms")

                soften(0)
                weights(0)
                soften(1)
                with pool.Fori(0, c.turns) as i:
                    for u in range(2):
                        g = i * 2 + u
                        weights(g + 1)
                        model(g)
                        soften(g + 2)

            @block.vector
            def _(dve):
                av.start(dve)
                bv.start(dve)
                def own(steps, g, name):
                    dve.wait_ge(steps.sem, steps.done(g, name))

                def normalise(g, before=None):
                    if before is not None:
                        dve.wait_ge(ap.sem, ap.done(before, "xT"))
                    for b in range(GB):
                        last = dve.tensor_scalar(xn[:, b, :], xg[:, g, b, :], meang[:, g, b:b + 1], rstdg[:, g, b:b + 1],
                                                 ALU.subtract, ALU.mult)
                    last.then_inc(xn_ready.sem, 1)

                def logits(g, batches):
                    for b in batches:
                        dve.wait_ge(ap.sem, ap.done(g, f"logit{b}"))
                        av.mark(dve.tensor_tensor(sw[b][:], heads8(bank[4 + b][:]), bc[:], ALU.add), f"logit{b}")

                def maxima(g):
                    for b in range(GB):
                        own(av, g, f"logit{b}")
                        av.mark(dve.tensor_reduce(mx[:, b, :], sw[b][:], AX_X, ALU.max), f"max{b}")

                def soften(g):
                    for b in range(GB):
                        dve.wait_ge(aa.sem, aa.done(g, f"exp{b}"))
                        av.mark(dve.tensor_reduce(sm[:, b, :], sw[b][:], AX_X, ALU.add), f"sum{b}")
                    own(av, g, f"sum{GB - 1}")
                    av.mark(dve.reciprocal(sm[:], sm[:]), "rsum")

                def lift(g, b):
                    dve.wait_ge(ap.sem, ap.done(g, f"fx{b}"))
                    av.mark(dve.tensor_tensor(fx[b % 2][:], bank[5][:], bfx[:], ALU.add), f"fx{b}")

                def totals(g, b):
                    dve.wait_ge(ap.sem, ap.done(g, f"total{b}"))
                    av.mark(dve.tensor_scalar(rs[:], bank[6][:, 0:CK], 1e-5, None, ALU.add), f"norm{b}")
                    own(av, g, f"norm{b}")
                    av.mark(dve.reciprocal(rs[:], rs[:]), f"rnorm{b}")
                    own(av, g, f"rnorm{b}")
                    av.mark(dve.tensor_tensor(inv[:], eye2[:].unsqueeze(1).to_broadcast([P, CK, SP]),
                                              rs[:].unsqueeze(2).to_broadcast([P, CK, SP]), ALU.mult), f"inv{b}")

                def slices_of(g, u, b):
                    dve.wait_ge(ap.sem, ap.done(g, f"inv{b}"))
                    for r in range(2):
                        half = slice(SP * r, SP * r + SP)
                        dve.tensor_copy(st[u][half, :, b, :], bank[7][half, :].rearrange("p (k r g) -> p k r g", k=CK, r=2)[:, :, r, :])
                    dve.drain()
                    av.mark(dve.tensor_tensor(st[u][:, :, b, :], st[u][:, :, b, :],
                                              bank[6][:, CK * SP:2 * CK * SP].rearrange("p (k g) -> p k g", k=CK), ALU.mult), f"st{b}")

                def gates(g):
                    for q in range(PAIRS):
                        dve.wait_ge(ba.sem, ba.done(g, f"z{q}"))
                        bv.mark(dve.tensor_tensor(zs[q][:], zs[q][:], bank[q][:], ALU.mult), f"zs{q}")

                def convolve(g):
                    dve.wait_ge(ba.sem, ba.done(g, "xa"))

                    def tap(j, k):
                        src = (bank[2 + j // 2] if j < 4 else bank[0])[:, j % 2 * W:(j % 2 + 1) * W].rearrange("p (b t) -> p b t", b=GB)
                        return dve.scalar_tensor_tensor(xa[:, j, :, k:SP], src[:, :, 0:SP - k], cw[:, j, 2 - k:3 - k],
                                                        xa[:, j, :, k:SP], ALU.mult, ALU.add)

                    for j in range(4):
                        last = tap(j, 1)
                    bv.mark(last, "tap1")
                    own(bv, g, "tap1")
                    for j in range(4):
                        last = tap(j, 2)
                    bv.mark(last, "tap2")
                    dve.wait_ge(ba.sem, ba.done(g, "xa45"))
                    for j in range(4, 6):
                        tap(j, 1)
                    dve.drain()
                    for j in range(4, 6):
                        last = tap(j, 2)
                    bv.mark(last, "tap45")
                    flat = lambda v: v[:].rearrange("p q k h -> p q (k h)")
                    bias = heads_all[:, 2:4, :].rearrange("p k h -> p (k h)").unsqueeze(1).to_broadcast([P, PAIRS, 2 * SH])
                    bv.mark(dve.tensor_tensor(flat(dt), bank[1][:, 0:2 * PAIRS * SH].rearrange("p (q k) -> p q k", q=PAIRS),
                                              bias, ALU.add), "dt")
                    own(bv, g, "dt")
                    bv.mark(dve.tensor_scalar(dn[:], dt[:], -1.0, None, ALU.mult), "dneg")
                    own(bv, g, "dneg")
                    bv.mark(dve.tensor_tensor(dn[:], dt[:], dn[:], ALU.max), "dabs")

                def silu(g):
                    dve.wait_ge(ba.sem, ba.done(g, "xe"))
                    bv.mark(dve.tensor_tensor(xa[:], xa[:], xe[:], ALU.mult), "x")

                def steps(g):
                    dve.wait_ge(ba.sem, ba.done(g, "de"))
                    bv.mark(dve.tensor_scalar(du[:], de[:], 1.0, None, ALU.add), "du")
                    own(bv, g, "du")
                    bv.mark(dve.tensor_scalar(dc[:], du[:], -1.0, None, ALU.add), "dd")
                    own(bv, g, "dd")
                    bv.mark(dve.tensor_tensor(dc[:], de[:], dc[:], ALU.subtract), "dc")
                    dve.wait_ge(ba.sem, ba.done(g, "dl"))
                    bv.mark(dve.reciprocal(du[:], du[:]), "dru")
                    own(bv, g, "dru")
                    bv.mark(dve.tensor_tensor(dc[:], dc[:], du[:], ALU.mult), "dcr")
                    own(bv, g, "dcr")
                    bv.mark(dve.tensor_tensor(dc[:], dc[:], dl[:], ALU.add), "dsum")
                    own(bv, g, "dsum")
                    bv.mark(dve.scalar_tensor_tensor(dt[:], dt[:], 0.0, dc[:], ALU.max, ALU.add), "dt2")
                    own(bv, g, "dt2")
                    bv.mark(dve.tensor_tensor(dn[:], dt[:], a2[:].unsqueeze(1).to_broadcast([P, PAIRS, 2, SH]), ALU.mult), "da")
                    own(bv, g, "da")
                    backward(g, 0)

                def backward(g, q):
                    if q:
                        dve.wait_ge(bp.sem, bp.done(g, f"seg{q - 1}"))
                    bv.mark(dve.tensor_tensor(seg_rhs[1][:], over_t(dn[:, q, 1, :]), over_h(low[:]), ALU.mult), f"seg{q}b")

                def products_of_states(g):
                    dve.wait_ge(bp.sem, bp.done(g, f"bc{PAIRS - 1}"))
                    for q in range(PAIRS):
                        for r in range(2):
                            half = slice(SP * r, SP * r + SP)
                            last = dve.tensor_copy(bcp[q][half, 1:SP + 1], bank[0][half, q * P + SP * r:q * P + SP * r + SP])
                        bv.mark(last, f"bcp{q}")
                    dve.wait_ge(bp.sem, bp.done(g, "fcd"))
                    bv.mark(dve.tensor_tensor(fcd[:], bank[1][:, 64:64 + PAIRS * SH].rearrange("p (q h) -> p q h", q=PAIRS),
                                              heads_all[:, 1:2, :].to_broadcast([P, PAIRS, SH]), ALU.add), "fcd")

                def model(g, q):
                    own(bv, g, f"bcp{q}")
                    if q:
                        dve.wait_ge(bg.sem, bg.done(g, f"m2{q - 1}"))
                    dve.tensor_tensor(gu[:], bcp[q][:, 0:SP], up[:], ALU.mult)
                    bv.mark(dve.tensor_tensor(gd[:], bcp[q][:, 2:SP + 2], low[:], ALU.mult), f"g{q}")
                    own(bv, g, f"g{q}")
                    dve.tensor_tensor(m1[:], over_t(dt[:, q, 0, :]), over_h(gu[:]), ALU.mult)
                    dve.drain()
                    dve.wait_ge(bg.sem, bg.done(g, f"m2{q}"))
                    bv.mark(dve.tensor_tensor(m1[:], m1[:], m2[:], ALU.add), f"m{q}")
                    own(bv, g, f"m{q}")
                    dve.wait_ge(ba.sem, ba.done(g, f"dec{q}"))
                    for r in range(2):
                        half = slice(SP * r, SP * r + SP)
                        last = dve.tensor_tensor(mb[q][half, :, half], m1[half, :, :], dec[q][half, :, :], ALU.mult)
                    bv.mark(last, f"mm{q}")

                def gate(g):
                    for q in range(PAIRS):
                        dve.wait_ge(bp.sem, bp.done(g, f"y{q}"))
                        dve.wait_ge(bg.sem, bg.done(g, f"xf{q}"))
                        bv.mark(dve.tensor_tensor(y[q][:], y[q][:], bank[q][:], ALU.add), f"y{q}")
                    for q in range(PAIRS):
                        own(bv, g, f"y{q}")
                        bv.mark(dve.tensor_tensor(y[q][:], y[q][:], zs[q][:], ALU.mult), f"yg{q}")

                def scale(g):
                    dve.wait_ge(ba.sem, ba.done(g, f"ms{PAIRS - 1}"))
                    bv.mark(dve.tensor_scalar(ms[:], ms[:], 1.0 / (CK * P), EPS, ALU.mult, ALU.add), "mean")
                    dve.wait_ge(bg.sem, bg.done(g, "rms"))
                    for q in range(PAIRS):
                        bv.mark(dve.tensor_scalar(y[q][:], y[q][:], rms[:, q:q + 1], None, ALU.mult), f"ygn{q}")

                def turned(g):
                    dve.wait_ge(bp.sem, bp.done(g, "ot"))
                    for j in range(0, CK, 2):
                        for r in range(2):
                            half = slice(SP * r, SP * r + SP)
                            last = dve.tensor_copy(otb[half, j:j + 2, :, half],
                                                   bank[j // 2][half, :].rearrange("p (j b t) -> p j b t", j=2, b=GB))
                    bv.mark(last, "ot")

                def finish(g):
                    dve.wait_ge(bp.sem, bp.done(g, f"out{GB - 1}"))
                    bv.mark(dve.tensor_tensor(xg[:, g, :, :], xg[:, g, :, :], bank[0][:].rearrange("p (b f) -> p b f", b=GB), ALU.add),
                            "x_out")
                    own(bv, g, "x_out")
                    for b in range(GB):
                        dve.bn_stats(sg[:, g, b, :], xg[:, g, b, :])

                normalise(0)
                logits(0, range(GB))
                maxima(0)
                soften(0)
                for b in range(GB):
                    lift(0, b)
                    totals(0, b)
                    slices_of(0, 0, b)
                normalise(1, 0)
                logits(1, range(GB))
                maxima(1)
                with dve.Fori(0, c.turns) as i:
                    for u in range(2):
                        g = i * 2 + u
                        n = g + 1
                        normalise(g + 2, n)
                        gates(g)
                        soften(n)
                        convolve(g)
                        lift(n, 0)
                        totals(n, 0)
                        silu(g)
                        steps(g)
                        slices_of(n, 1 - u, 0)
                        lift(n, 1)
                        totals(n, 1)
                        backward(g, 1)
                        slices_of(n, 1 - u, 1)
                        lift(n, 2)
                        totals(n, 2)
                        slices_of(n, 1 - u, 2)
                        products_of_states(g)
                        model(g, 0)
                        lift(n, 3)
                        totals(n, 3)
                        model(g, 1)
                        slices_of(n, 1 - u, 3)
                        gate(g)
                        scale(g)
                        logits(g + 2, range(2))
                        turned(g)
                        logits(g + 2, range(2, 3))
                        finish(g)
                        logits(g + 2, range(3, GB))
                        maxima(g + 2)

            @block.tensor
            def _(pe):
                ap.start(pe)
                bp.start(pe)
                def turn(g):
                    pe.wait_ge(xn_ready.sem, xn_ready.done(g))
                    pe.wait_ge(aa.sem, aa.all_done(g))
                    for b in range(GB):
                        last = pe.transpose(bank[4][:, b * P:(b + 1) * P], xn[:, b, :], c.ident[:])
                    ap.mark(last, "xT")

                def logits(g, batches):
                    pe.wait_ge(aa.sem, aa.done(g, "xT"))
                    for b in batches:
                        ap.mark(pe.matmul(bank[4 + b][:], xT[:, b * P:(b + 1) * P], wc[:].rearrange("p h g -> p (h g)"),
                                          start=True, stop=True), f"logit{b}")

                def pool_tokens(g, b):
                    flat = sw[b][:].rearrange("p h g -> p (h g)")
                    pe.wait_ge(ag.sem, ag.done(g, f"sw{b}"))
                    if b:
                        pe.wait_ge(aa.sem, aa.done(g, f"swT{b - 1}"))
                    else:
                        pe.wait_ge(av.sem, av.done(g, f"logit{GB - 1}"))
                    for k in range(CK):
                        last = pe.transpose(bank[4][:, k * P:(k + 1) * P], flat[:, k * P:(k + 1) * P], c.ident[:])
                    ap.mark(last, f"swT{b}")
                    if b:
                        pe.wait_ge(av.sem, av.done(g, f"fx{b - 1}"))
                    ap.mark(pe.matmul(bank[5][:], xT[:, b * P:(b + 1) * P], fx_t[:].rearrange("p k c -> p (k c)"),
                                      start=True, stop=True), f"fx{b}")
                    if b:
                        pe.wait_ge(av.sem, av.done(g, f"st{b - 1}"))
                    for k in range(CK):
                        last = pe.matmul(bank[6][:, k:k + 1], flat[:, k * P:(k + 1) * P], c.ones[:, 0:1], start=True, stop=True)
                    ap.mark(last, f"total{b}")
                    pe.wait_ge(av.sem, av.done(g, f"fx{b}"))
                    for k in range(CK):
                        at = slice(k * P, (k + 1) * P)
                        last = pe.matmul(bank[7][:, at], fx[b % 2][:, at], flat[:, at], start=True, stop=True)
                    ap.mark(last, f"st{b}")
                    pe.wait_ge(av.sem, av.done(g, f"inv{b}"))
                    ap.mark(pe.matmul(bank[6][:, CK * SP:2 * CK * SP], same[:], inv[:].rearrange("p k g -> p (k g)"),
                                      start=True, stop=True), f"inv{b}")

                def project(g, u):
                    pe.wait_ge(av.sem, av.all_done(g + 1))
                    stf = st[u][:].rearrange("p k b t -> p k (b t)")
                    pe.wait_ge(bv.sem, bv.all_done(g))
                    for q in range(PAIRS):
                        for k in range(CK):
                            last = pe.matmul(bank[q][:], stf[:, k, q * P:(q + 1) * P], in_t[:, k, Z0:Z0 + 512],
                                             start=(k == 0), stop=(k == CK - 1))
                        bp.mark(last, f"z{q}")

                    def xbc(out, j):
                        for k in range(CK):
                            last = pe.matmul(out, in_t[:, k, X0 + P * j:X0 + P * (j + 1)] if j < 5 else in_t[:, k, C0:C0 + P],
                                             stf[:, k, :], start=(k == 0), stop=(k == CK - 1))
                        return last

                    for j in range(4):
                        last = xbc(bank[2 + j // 2][:, j % 2 * W:(j % 2 + 1) * W], j)
                    bp.mark(last, "xbc")
                    pe.wait_ge(bv.sem, bv.done(g, "zs1"))
                    for q in range(PAIRS):
                        for k in range(CK):
                            pe.matmul(bank[1][:, q * 2 * SH:(q + 1) * 2 * SH], stf[:, k, q * P:(q + 1) * P],
                                      in_t[:, k, DT0:DT0 + 2 * SH], start=(k == 0), stop=(k == CK - 1))
                    for j in range(4, 6):
                        last = xbc(bank[0][:, j % 2 * W:(j % 2 + 1) * W], j)
                    bp.mark(last, "dtbc")

                def decays(g):
                    for q in range(PAIRS):
                        pe.wait_ge(bg.sem, bg.done(g, f"seg{q}f"))
                        pe.wait_ge(bv.sem, bv.done(g, f"seg{q}b"))
                        pe.matmul(bank[2 + q][:], seg_f[:], seg_rhs[0][:].rearrange("p h t -> p (h t)"), start=True, stop=False)
                        bp.mark(pe.matmul(bank[2 + q][:], seg_b[:], seg_rhs[1][:].rearrange("p h t -> p (h t)"), start=False, stop=True),
                                f"seg{q}")

                def model(g):
                    xaf = xa[:].rearrange("p j b t -> p j (b t)")
                    for q in range(PAIRS):
                        at = slice(q * P, (q + 1) * P)
                        bp.mark(pe.matmul(bank[0][:, at], xaf[0:SP, 4, at], xaf[0:SP, 5, at], start=True, stop=True), f"bc{q}")
                    for q in range(PAIRS):
                        for k in range(CK):
                            last = pe.matmul(bank[1][:, 64 + q * SH:64 + (q + 1) * SH], xaf[:, k, q * P:(q + 1) * P], fc_t[:, k, :],
                                             start=(k == 0), stop=(k == CK - 1))
                    bp.mark(last, "fcd")
                    for q in range(PAIRS):
                        pe.wait_ge(ba.sem, ba.done(g, f"dec{q}"))
                        for k in range(CK):
                            last = pe.transpose(bank[2 + q][:, k * P:(k + 1) * P], xaf[:, k, q * P:(q + 1) * P], c.ident[:])
                        bp.mark(last, f"xs{q}")

                def weigh(g):
                    for q in range(PAIRS):
                        pe.wait_ge(bv.sem, bv.done(g, f"mm{q}"))
                        pe.wait_ge(ba.sem, ba.done(g, f"xs{q}"))
                        for h in range(SH):
                            last = pe.matmul(bank[q][:, h * SP:(h + 1) * SP], mb[q][:, h, :], xs[q][:, h, :], start=True, stop=True)
                        bp.mark(last, f"y{q}")

                def project_back(g):
                    for q in range(PAIRS):
                        pe.wait_ge(bv.sem, bv.done(g, f"ygn{q}"))
                        for k in range(CK):
                            last = pe.transpose(bank[2 + q][:, k * P:(k + 1) * P], y[q][:, k * P:(k + 1) * P], c.ident[:])
                        bp.mark(last, f"yT{q}")
                    pe.wait_ge(ba.sem, ba.done(g, f"yT{PAIRS - 1}"))
                    for j in range(CK):
                        for k in range(CK):
                            last = pe.matmul(bank[j // 2][:, j % 2 * W:(j % 2 + 1) * W], ho_t[:, k, j * P:(j + 1) * P],
                                             yT[:, k, :, :].rearrange("p q n -> p (q n)"), start=(k == 0), stop=(k == CK - 1))
                    bp.mark(last, "ot")

                def spread_slices(g, u):
                    pe.wait_ge(aa.sem, aa.all_done(g + 1))
                    pe.wait_ge(bv.sem, bv.done(g, "ot"))

                    def spread(b):
                        pe.wait_ge(ba.sem, ba.done(g, f"z_{b}"))
                        out = bank[0][:, b * P:(b + 1) * P]
                        pe.matmul(out, c.ones[0:1, :], ob[:], start=True, stop=False)
                        for k in range(CK):
                            last = pe.matmul(out, swT[u][:, b, k, :], zz[b % 2][:, k, :], start=False, stop=(k == CK - 1))
                        bp.mark(last, f"out{b}")

                    for b in range(GB):
                        if b >= 2:
                            pe.wait_ge(ba.sem, ba.done(g, f"z_{b - 2}"))
                        for k in range(CK):
                            last = pe.matmul(bank[2 + b % 2][:, k * P:(k + 1) * P], otb[:, k, b, :], ow_t[:, k, :], start=True, stop=True)
                        bp.mark(last, f"z_{b}")
                        if b >= 1:
                            spread(b - 1)
                    spread(GB - 1)

                turn(0)
                logits(0, range(GB))
                for b in range(GB):
                    pool_tokens(0, b)
                turn(1)
                logits(1, range(GB))
                with pe.Fori(0, c.turns) as i:
                    for u in range(2):
                        g = i * 2 + u
                        project(g, u)
                        pool_tokens(g + 1, 0)
                        pool_tokens(g + 1, 1)
                        decays(g)
                        pool_tokens(g + 1, 2)
                        model(g)
                        pool_tokens(g + 1, 3)
                        turn(g + 2)
                        weigh(g)
                        logits(g + 2, range(2))
                        project_back(g)
                        logits(g + 2, range(2, 3))
                        spread_slices(g, u)
                        logits(g + 2, range(3, GB))


def network(nc, io, n_batch):
    with ExitStack() as ctx:
        c = Chip(nc, ctx, io, n_batch)
        load_and_constants(c)
        for phase in PHASES:
            c.sems = []
            phase(c)
            nc.clear_and_free_semaphores(c.sems)
            nc.all_engine_barrier()


PHASES = [column_attention, l0_experts, head_attention, l1_experts, mean_messages, slices, edge_gates, l3_experts]


def kernel(**inputs):
    import numpy as _np
    import concourse.bacc as _bacc
    from concourse import mybir as _mybir
    from concourse.bass_utils import run_bass_kernel_spmd as _run

    nc = _bacc.Bacc("TRN2", target_bir_lowering=False, num_devices=1)
    arrays, io = {}, {}
    for name, value in inputs.items():
        a = _np.ascontiguousarray(value)
        if a.ndim == 0:
            a = a.reshape(1, 1)
        arrays[f"in_{name}"] = a
        io[name] = nc.dram_tensor(f"in_{name}", a.shape, _mybir.dt.from_np(a.dtype), kind="ExternalInput").ap()
    x = io["x"]
    io["out"] = nc.dram_tensor("out_x", x.shape, F32, kind="ExternalOutput").ap()
    network(nc, io, x.shape[0])
    r = _run(nc, [arrays], core_ids=[0])
    return r.results[0]["out_x"]
```
